# Optimizing a Trainium2 kernel written in Bass

```python
import numpy as np
import jax
import jax.numpy as jnp

def _softmax(x, axis=-1):
    return jax.nn.softmax(x, axis=axis)

def _gelu(x):
    return jax.nn.gelu(x, approximate=True)

def _silu(x):
    return jax.nn.silu(x)

def _sigmoid(x):
    return jax.nn.sigmoid(x)

def _layernorm(x, axis=-1, eps=1e-05):
    m = jnp.mean(x, axis=axis, keepdims=True)
    v = jnp.var(x, axis=axis, keepdims=True)
    return (x - m) / jnp.sqrt(v + eps)

def _scatter_add(tgt, idx, src, axis=0):
    return tgt.at[idx].add(src)

def _segment_sum(src, seg, n):
    return jax.ops.segment_sum(src, seg, n)
kernel_name = 'mk_seq_postln_d2_jaxref_r8_23d393'

def setup_inputs(seed: int=0):
    np.random.seed(seed)
    _w = jnp.asarray

    def _L0_attn_setup():
        import jax, jax.numpy as jnp
        import numpy as np
        import math
        N_HEAD = 16
        N_EMBD = 128
        HEAD_DIM = N_EMBD // N_HEAD
        ROPE_BASE = 10000.0

        def _rope_cos_sin(T, dh, dtype):
            inv_freq = 1.0 / ROPE_BASE ** (jnp.arange(0, dh, 2, dtype=jnp.float32) / dh)
            freqs = jnp.arange(T, dtype=jnp.float32)[:, None] * inv_freq[None, :]
            cos = jnp.repeat(jnp.cos(freqs), 2, axis=-1).astype(dtype)
            sin = jnp.repeat(jnp.sin(freqs), 2, axis=-1).astype(dtype)
            return (cos, sin)

        def _apply_rope(x, cos, sin):
            x_even = x[..., ::2]
            x_odd = x[..., 1::2]
            x_rot = jnp.stack((-x_odd, x_even), axis=-1).reshape(x.shape)
            return x * cos + x_rot * sin
        key = jax.random.key(seed)
        k1, k2, k3 = jax.random.split(key, 3)
        B, T, C = (2, 256, N_EMBD)
        x = jax.random.normal(k1, (B, T, C), dtype=jnp.float32)
        Wqkv = jax.random.normal(k2, (C, 3 * C), dtype=jnp.float32) * (1.0 / math.sqrt(C))
        Wproj = jax.random.normal(k3, (C, C), dtype=jnp.float32) * (1.0 / math.sqrt(C))
        return {'x': x, 'Wqkv': Wqkv, 'Wproj': Wproj}
    _L0_attn_in = _L0_attn_setup()

    def _L0_ffn_setup():
        import jax, jax.numpy as jnp
        import numpy as np
        import math
        D_MODEL = 128
        D_FF = 512
        NUM_EXPERTS = 8
        NUM_SHARED = 1
        E_ROUTED = NUM_EXPERTS - NUM_SHARED
        TOP_K = 2
        CAP_FACTOR = 1.25
        B, S = (4, 256)
        T = B * S
        CAPACITY = math.ceil(CAP_FACTOR * T * TOP_K / E_ROUTED)
        SHARED_SCALE = 1.0

        def _layernorm(x, g, b, eps=1e-05):
            mu = jnp.mean(x, axis=-1, keepdims=True)
            var = jnp.mean((x - mu) ** 2, axis=-1, keepdims=True)
            return (x - mu) * jax.lax.rsqrt(var + eps) * g + b
        key = jax.random.key(seed)
        ks = jax.random.split(key, 10)
        s = 0.02
        return {'x': jax.random.normal(ks[0], (B, S, D_MODEL), dtype=jnp.float32), 'ln_g': jnp.ones((D_MODEL,), jnp.float32), 'ln_b': jnp.zeros((D_MODEL,), jnp.float32), 'Wr': jax.random.normal(ks[1], (D_MODEL, E_ROUTED), jnp.float32) * s, 'W1': jax.random.normal(ks[2], (E_ROUTED, D_MODEL, D_FF), jnp.float32) * s, 'W3': jax.random.normal(ks[3], (E_ROUTED, D_MODEL, D_FF), jnp.float32) * s, 'W2': jax.random.normal(ks[4], (E_ROUTED, D_FF, D_MODEL), jnp.float32) * s, 'W1s': jax.random.normal(ks[5], (D_MODEL, D_FF), jnp.float32) * s, 'W3s': jax.random.normal(ks[6], (D_MODEL, D_FF), jnp.float32) * s, 'W2s': jax.random.normal(ks[7], (D_FF, D_MODEL), jnp.float32) * s}
    _L0_ffn_in = _L0_ffn_setup()

    def _L1_attn_setup():
        import jax, jax.numpy as jnp
        import numpy as np
        NUM_HEADS = 16

        def _rope_tables(seq_len, head_dim, dtype):
            pos = jnp.arange(seq_len, dtype=jnp.float32)
            inv = jnp.power(10000.0, -2.0 * jnp.arange(head_dim // 2, dtype=jnp.float32) / head_dim)
            ang = pos[:, None] * inv[None, :]
            cos = jnp.repeat(jnp.cos(ang), 2, axis=-1).astype(dtype)
            sin = jnp.repeat(jnp.sin(ang), 2, axis=-1).astype(dtype)
            return (cos[None, None], sin[None, None])

        def _rotate_half_interleaved(x):
            x2 = jnp.stack([-x[..., 1::2], x[..., ::2]], axis=-1)
            return x2.reshape(x.shape)
        key = jax.random.key(seed)
        k0, k1, k2, k3 = jax.random.split(key, 4)
        B, N, C = (2, 256, 128)
        s = 1.0 / np.sqrt(C)
        return {'x': jax.random.normal(k0, (B, N, C), dtype=jnp.float32), 'Wq': jax.random.normal(k1, (C, C), dtype=jnp.float32) * s, 'Wk': jax.random.normal(k2, (C, C), dtype=jnp.float32) * s, 'Wv': jax.random.normal(k3, (C, C), dtype=jnp.float32) * s}
    _L1_attn_in = _L1_attn_setup()

    def _L1_ffn_setup():
        import jax, jax.numpy as jnp
        import numpy as np
        D_IN, D_HID = (128, 512)

        def _ternary(key, shape):
            return jax.random.randint(key, shape, -1, 2).astype(jnp.float32)

        def _tlin(x, w, s):
            return jnp.einsum('bsi,oi->bso', x, w) * s
        key = jax.random.key(seed)
        ks = jax.random.split(key, 12)
        inv = lambda fan: 1.0 / np.sqrt(fan).astype(np.float32)
        return {'x': jax.random.normal(ks[0], (4, 256, D_IN), dtype=jnp.float32), 'w1_w': _ternary(ks[1], (D_HID, D_IN)), 'w1_s': jax.random.uniform(ks[2], (D_HID,), dtype=jnp.float32) * inv(D_IN), 'w2_w': _ternary(ks[3], (D_HID, D_IN)), 'w2_s': jax.random.uniform(ks[4], (D_HID,), dtype=jnp.float32) * inv(D_IN), 'h1_w': _ternary(ks[5], (D_HID, D_HID)), 'h1_s': jax.random.uniform(ks[6], (D_HID,), dtype=jnp.float32) * inv(D_HID), 'h2_w': _ternary(ks[7], (D_HID, D_HID)), 'h2_s': jax.random.uniform(ks[8], (D_HID,), dtype=jnp.float32) * inv(D_HID), 'w3_w': _ternary(ks[9], (D_IN, D_HID)), 'w3_s': jax.random.uniform(ks[10], (D_IN,), dtype=jnp.float32) * inv(D_HID)}
    _L1_ffn_in = _L1_ffn_setup()
    _d = {'L0_attn_x': _L0_attn_in['x'], 'L0_attn_Wqkv': _L0_attn_in['Wqkv'], 'L0_attn_Wproj': _L0_attn_in['Wproj'], 'L0_ffn_ln_g': _L0_ffn_in['ln_g'], 'L0_ffn_ln_b': _L0_ffn_in['ln_b'], 'L0_ffn_Wr': _L0_ffn_in['Wr'], 'L0_ffn_W1': _L0_ffn_in['W1'], 'L0_ffn_W3': _L0_ffn_in['W3'], 'L0_ffn_W2': _L0_ffn_in['W2'], 'L0_ffn_W1s': _L0_ffn_in['W1s'], 'L0_ffn_W3s': _L0_ffn_in['W3s'], 'L0_ffn_W2s': _L0_ffn_in['W2s'], 'L1_attn_Wq': _L1_attn_in['Wq'], 'L1_attn_Wk': _L1_attn_in['Wk'], 'L1_attn_Wv': _L1_attn_in['Wv'], 'L1_ffn_w1_w': _L1_ffn_in['w1_w'], 'L1_ffn_w1_s': _L1_ffn_in['w1_s'], 'L1_ffn_w2_w': _L1_ffn_in['w2_w'], 'L1_ffn_w2_s': _L1_ffn_in['w2_s'], 'L1_ffn_h1_w': _L1_ffn_in['h1_w'], 'L1_ffn_h1_s': _L1_ffn_in['h1_s'], 'L1_ffn_h2_w': _L1_ffn_in['h2_w'], 'L1_ffn_h2_s': _L1_ffn_in['h2_s'], 'L1_ffn_w3_w': _L1_ffn_in['w3_w'], 'L1_ffn_w3_s': _L1_ffn_in['w3_s']}
    _x0 = _d['L0_attn_x']
    _d['L0_attn_x'] = jax.random.normal(jax.random.fold_in(jax.random.key(seed), 1), (8, 512, 128), dtype=_x0.dtype)
    del _x0
    return _d

def reference(L0_attn_x, L0_attn_Wqkv, L0_attn_Wproj, L0_ffn_ln_g, L0_ffn_ln_b, L0_ffn_Wr, L0_ffn_W1, L0_ffn_W3, L0_ffn_W2, L0_ffn_W1s, L0_ffn_W3s, L0_ffn_W2s, L1_attn_Wq, L1_attn_Wk, L1_attn_Wv, L1_ffn_w1_w, L1_ffn_w1_s, L1_ffn_w2_w, L1_ffn_w2_s, L1_ffn_h1_w, L1_ffn_h1_s, L1_ffn_h2_w, L1_ffn_h2_s, L1_ffn_w3_w, L1_ffn_w3_s):

    def _L0_attn_ref(x, Wqkv, Wproj):
        import jax, jax.numpy as jnp
        import numpy as np
        import math
        N_HEAD = 16
        N_EMBD = 128
        HEAD_DIM = N_EMBD // N_HEAD
        ROPE_BASE = 10000.0

        def _rope_cos_sin(T, dh, dtype):
            inv_freq = 1.0 / ROPE_BASE ** (jnp.arange(0, dh, 2, dtype=jnp.float32) / dh)
            freqs = jnp.arange(T, dtype=jnp.float32)[:, None] * inv_freq[None, :]
            cos = jnp.repeat(jnp.cos(freqs), 2, axis=-1).astype(dtype)
            sin = jnp.repeat(jnp.sin(freqs), 2, axis=-1).astype(dtype)
            return (cos, sin)

        def _apply_rope(x, cos, sin):
            x_even = x[..., ::2]
            x_odd = x[..., 1::2]
            x_rot = jnp.stack((-x_odd, x_even), axis=-1).reshape(x.shape)
            return x * cos + x_rot * sin
        B, T, C = x.shape
        H, Dh = (N_HEAD, HEAD_DIM)
        qkv = x @ Wqkv
        q, k, v = jnp.split(qkv, 3, axis=-1)
        Q = q.reshape(B, T, H, Dh).transpose(0, 2, 1, 3)
        K = k.reshape(B, T, H, Dh).transpose(0, 2, 1, 3)
        V = v.reshape(B, T, H, Dh).transpose(0, 2, 1, 3)
        cos, sin = _rope_cos_sin(T, Dh, x.dtype)
        Q = _apply_rope(Q, cos, sin)
        K = _apply_rope(K, cos, sin)
        scores = jnp.einsum('bhqd,bhkd->bhqk', Q, K) / math.sqrt(Dh)
        causal = jnp.tril(jnp.ones((T, T), dtype=bool))
        scores = jnp.where(causal, scores, jnp.finfo(scores.dtype).min)
        attn = jax.nn.softmax(scores, axis=-1)
        y = jnp.einsum('bhqk,bhkd->bhqd', attn, V)
        y = y.transpose(0, 2, 1, 3).reshape(B, T, C)
        return y @ Wproj

    def _L0_ffn_ref(x, ln_g, ln_b, Wr, W1, W3, W2, W1s, W3s, W2s):
        import jax, jax.numpy as jnp
        import numpy as np
        import math
        D_MODEL = 128
        D_FF = 512
        NUM_EXPERTS = 8
        NUM_SHARED = 1
        E_ROUTED = NUM_EXPERTS - NUM_SHARED
        TOP_K = 2
        CAP_FACTOR = 1.25
        B, S = (4, 256)
        T = B * S
        CAPACITY = math.ceil(CAP_FACTOR * T * TOP_K / E_ROUTED)
        SHARED_SCALE = 1.0

        def _layernorm(x, g, b, eps=1e-05):
            mu = jnp.mean(x, axis=-1, keepdims=True)
            var = jnp.mean((x - mu) ** 2, axis=-1, keepdims=True)
            return (x - mu) * jax.lax.rsqrt(var + eps) * g + b
        Bx, Sx, D = x.shape
        Tn = Bx * Sx
        h = _layernorm(x, ln_g, ln_b).reshape(Tn, D)
        logits = h @ Wr
        top_vals, top_idx = jax.lax.top_k(logits, TOP_K)
        gates = jax.nn.softmax(top_vals, axis=-1)
        idx = top_idx.T.reshape(-1)
        gat = gates.T.reshape(-1)
        tok = jnp.tile(jnp.arange(Tn), TOP_K)
        onehot = jax.nn.one_hot(idx, E_ROUTED, dtype=jnp.int32)
        pos = jnp.sum(jnp.cumsum(onehot, axis=0) * onehot, axis=-1) - 1
        keep = pos < CAPACITY
        pos_c = jnp.where(keep, pos, CAPACITY)
        xe = jnp.zeros((E_ROUTED, CAPACITY, D), h.dtype).at[idx, pos_c].set(h[tok], mode='drop')
        a = jnp.einsum('ecd,edf->ecf', xe, W1)
        b = jnp.einsum('ecd,edf->ecf', xe, W3)
        ye = jnp.einsum('ecf,efd->ecd', jax.nn.silu(a) * b, W2)
        out_slots = ye[jnp.clip(idx, 0, E_ROUTED - 1), jnp.clip(pos_c, 0, CAPACITY - 1)]
        out_slots = out_slots * (gat * keep.astype(gat.dtype))[:, None]
        routed = jnp.zeros((Tn, D), h.dtype).at[tok].add(out_slots)
        shared = jax.nn.silu(h @ W1s) * (h @ W3s) @ W2s
        out = routed + SHARED_SCALE * shared
        return out.reshape(Bx, Sx, D)

    def _L1_attn_ref(x, Wq, Wk, Wv):
        import jax, jax.numpy as jnp
        import numpy as np
        NUM_HEADS = 16

        def _rope_tables(seq_len, head_dim, dtype):
            pos = jnp.arange(seq_len, dtype=jnp.float32)
            inv = jnp.power(10000.0, -2.0 * jnp.arange(head_dim // 2, dtype=jnp.float32) / head_dim)
            ang = pos[:, None] * inv[None, :]
            cos = jnp.repeat(jnp.cos(ang), 2, axis=-1).astype(dtype)
            sin = jnp.repeat(jnp.sin(ang), 2, axis=-1).astype(dtype)
            return (cos[None, None], sin[None, None])

        def _rotate_half_interleaved(x):
            x2 = jnp.stack([-x[..., 1::2], x[..., ::2]], axis=-1)
            return x2.reshape(x.shape)
        B, N, C = x.shape
        H = NUM_HEADS
        D = C // H
        scale = D ** (-0.5)

        def heads(y):
            return y.reshape(B, N, H, D).transpose(0, 2, 1, 3)
        q = heads(x @ Wq.T)
        k = heads(x @ Wk.T)
        v = heads(x @ Wv.T)
        cos, sin = _rope_tables(N, D, x.dtype)
        q = q * cos + _rotate_half_interleaved(q) * sin
        k = k * cos + _rotate_half_interleaved(k) * sin
        attn = jnp.einsum('bhnd,bhmd->bhnm', q, k) * scale
        attn = jax.nn.softmax(attn, axis=-1)
        out = jnp.einsum('bhnm,bhmd->bhnd', attn, v)
        return out.transpose(0, 2, 1, 3).reshape(B, N, C)

    def _L1_ffn_ref(x, w1_w, w1_s, w2_w, w2_s, h1_w, h1_s, h2_w, h2_s, w3_w, w3_s):
        import jax, jax.numpy as jnp
        import numpy as np
        D_IN, D_HID = (128, 512)

        def _ternary(key, shape):
            return jax.random.randint(key, shape, -1, 2).astype(jnp.float32)

        def _tlin(x, w, s):
            return jnp.einsum('bsi,oi->bso', x, w) * s
        h = jax.nn.silu(_tlin(x, w1_w, w1_s)) * _tlin(x, w2_w, w2_s)
        h = jax.nn.gelu(_tlin(h, h1_w, h1_s), approximate=False)
        h = jax.nn.gelu(_tlin(h, h2_w, h2_s), approximate=False)
        return _tlin(h, w3_w, w3_s)
    x = L0_attn_x
    x = _layernorm(x + _L0_attn_ref(x, L0_attn_Wqkv, L0_attn_Wproj), axis=-1)
    x = _layernorm(x + _L0_ffn_ref(x, L0_ffn_ln_g, L0_ffn_ln_b, L0_ffn_Wr, L0_ffn_W1, L0_ffn_W3, L0_ffn_W2, L0_ffn_W1s, L0_ffn_W3s, L0_ffn_W2s), axis=-1)
    x = _layernorm(x + _L1_attn_ref(x, L1_attn_Wq, L1_attn_Wk, L1_attn_Wv), axis=-1)
    x = _layernorm(x + _L1_ffn_ref(x, L1_ffn_w1_w, L1_ffn_w1_s, L1_ffn_w2_w, L1_ffn_w2_s, L1_ffn_h1_w, L1_ffn_h1_s, L1_ffn_h2_w, L1_ffn_h2_s, L1_ffn_w3_w, L1_ffn_w3_s), axis=-1)
    return x

_drawn_inputs = setup_inputs


def setup_inputs(seed=0):
    import zlib

    import numpy as np

    out = dict(_drawn_inputs(seed))
    spreads = {'L0_ffn_ln_g': (1.0, 0.6), 'L0_ffn_ln_b': (0.0, 0.8)}
    factors = {'L0_ffn_Wr': 8.0,
     'L0_ffn_W1': 8.0,
     'L0_ffn_W3': 8.0,
     'L0_ffn_W2': 8.0,
     'L0_ffn_W1s': 4.341,
     'L0_ffn_W3s': 4.288,
     'L0_ffn_W2s': 4.293,
     'L1_ffn_w1_w': 8.0,
     'L1_ffn_w1_s': 8.0,
     'L1_ffn_w2_w': 8.0,
     'L1_ffn_w2_s': 8.0,
     'L1_ffn_h1_w': 8.0,
     'L1_ffn_h1_s': 8.0,
     'L1_ffn_h2_w': 8.0,
     'L1_ffn_h2_s': 8.0,
     'L1_ffn_w3_w': 8.0,
     'L1_ffn_w3_s': 8.0}
    for name, (base, spread) in spreads.items():
        noise = np.random.default_rng([zlib.crc32(name.encode()), seed]).standard_normal(out[name].shape)
        drawn = base * np.exp(spread * noise) if base else spread * noise
        out[name] = jnp.asarray(drawn.astype(out[name].dtype))
    for name, factor in factors.items():
        out[name] = (out[name] * factor).astype(out[name].dtype)
    return out
```

```python
import concourse.bass as bass
from concourse import mybir
from contextlib import ExitStack

F32 = mybir.dt.float32
BF16 = mybir.dt.bfloat16
ALU = mybir.AluOpType
ACT = mybir.ActivationFunctionType
AX = mybir.AxisListType

P = 128
C = 128
B, T = 8, 512
QT = T // P
NT = B * QT
H, D = 16, 8
HG = 4
NG = H // HG
PARTS = 3
PROD = PARTS * PARTS
ROWS = PROD * D
FULL = 96
VW = 32
EPS = 1e-5
NEWTON = 3


def causal_widths(causal):
    seen_by = [T - P * j if causal else T for j in range(QT)]
    sees = [P * (i + 1) if causal else T for i in range(QT)]
    return seen_by, sees


def by_itself(eng, sem):
    eng.sem_inc(sem, 1)


def layernorm(dve, out, src, stats, mv, rs, tmp, sem, n, past):
    steps = [0]

    def done(ins):
        steps[0] += 1
        ins.then_inc(sem, 1)

    def wait():
        dve.wait_ge(sem, n * LN_STEPS + steps[0])

    by_itself(dve, past)
    for i in range(QT):
        done(dve.bn_stats(stats[:, i, :], src[:, i, :]))
    wait()
    by_itself(dve, past)
    for i in range(QT):
        done(dve.bn_aggr(mv[:, i, :], stats[:, i, :]))
    wait()
    var, y, half = tmp[:, 0, :], tmp[:, 1, :], tmp[:, 2, :]
    t = tmp[:, 3, :]
    I32 = mybir.dt.int32
    done(dve.tensor_scalar(var, mv[:, :, 1], EPS, None, ALU.add))
    wait()
    done(dve.tensor_scalar(half, var, -0.5, None, ALU.mult))
    done(dve.tensor_scalar(t.bitcast(I32), var.bitcast(I32), 1, None, ALU.arith_shift_right))
    wait()
    done(dve.tensor_scalar(y.bitcast(I32), t.bitcast(I32), -1.0, float(0x5F3759DF), ALU.mult, ALU.add))
    wait()
    for k in range(NEWTON):
        done(dve.tensor_tensor(t, y, y, ALU.mult))
        wait()
        done(dve.tensor_tensor(t, t, half, ALU.mult))
        wait()
        done(dve.scalar_tensor_tensor(rs[:, :] if k == NEWTON - 1 else y, t, 1.5, y, ALU.add, ALU.mult))
        wait()
    for i in range(QT):
        done(dve.tensor_scalar(out[:, i, :], src[:, i, :], mv[:, i, 0:1], rs[:, i:i + 1],
                               ALU.subtract, ALU.mult))
    assert steps[0] == LN_STEPS


LN_STEPS = QT + QT + 4 + 3 * NEWTON + QT


def attention(nc, x, x_dram, ident, identb, mask, weights, wproj, cos, sin, causal, tag):
    seen_by, sees = causal_widths(causal)
    unit_heads = [2 * T // (seen_by[j] if seen_by[j] in (T, T // 2, T // 4) else T) for j in range(QT)]
    unit_heads = [min(HG, u) for u in unit_heads]
    max_heads = [T // sees[i] if sees[i] in (P, 2 * P) else 1 for i in range(QT)]
    SU = sum(HG // u for u in unit_heads)
    MU = sum(HG // u for u in max_heads)
    RING = 4
    LAG = 2
    G = B * NG

    def jobs(b, g, j, first, last):
        out = []
        if j == 0 and not (last and g == NG - 1):
            out.append("maxT")
        if not last:
            out += {(0, 0): ["xT"], (0, 1): ["k"], (0, 2): ["kr"], (0, 3): ["q"], (1, 0): ["qr"], (1, 1): ["v"]}.get((g, j), [])
        if j == 2 and not (first and g == 0):
            out.append("norm")
        if not first:
            out += {(0, 3): ["yT"], (1, 1): ["proj"]}.get((g, j), []) if wproj is not None else []
        return out

    START = ["xT", "k", "kr", "q", "qr", "v", "maxT"]
    END = ["norm"] + (["yT", "proj"] if wproj is not None else [])

    def batch_jobs(first, last):
        return [(g, j, name) for g in range(NG) for j in range(QT) for name in jobs(0, g, j, first, last)]

    N0, N1 = len(batch_jobs(True, False)), len(batch_jobs(False, False))

    def jobs_before(b, first):
        return len(START) if first else len(START) + N0 + (b - 1) * N1

    def number(b, first, last, g, name):
        at = [n for n, (gg, _, x) in enumerate(batch_jobs(first, last)) if (gg, x) == (g, name)]
        assert len(at) == 1
        return jobs_before(b, first) + at[0]

    FREED = 2
    SPLIT = 2 * PARTS

    with ExitStack() as ctx:
        def psum(name, shape, dt=F32):
            return ctx.enter_context(nc.psum_tensor(tag + name, shape, dt))

        def sbuf(name, shape, dt=F32):
            return ctx.enter_context(nc.sbuf_tensor(tag + name, shape, dt))

        def sem(name):
            return ctx.enter_context(nc.semaphore(tag + name))

        qst = [sbuf(f"qst{i}", [FULL, H, T], BF16) for i in range(2)]
        kst = [sbuf(f"kst{i}", [FULL, H, T], BF16) for i in range(2)]
        vst = [sbuf(f"vst{i}", [P, QT, H, VW]) for i in range(2)]
        prob = [sbuf(f"prob{i}", [P, HG, T]) for i in range(RING)]
        xin = sbuf("xin", [P, QT, C])
        xT = sbuf("xT", [C, T])
        rope = {n: sbuf("rope_" + n, [C, T]) for n in ("k", "kr", "q", "qr")}
        part = {n: sbuf("part_" + n, [C, PARTS, T], BF16) for n in ("k", "q")}
        mx = sbuf("mx", [P, 2, QT, HG])
        rest = sbuf("rest", [P, 2, QT, HG])
        mpart = sbuf("mpart", [P, QT, PARTS, HG], BF16)
        mrow = sbuf("mrow", [PARTS * HG, T], BF16)
        oT = sbuf("oT", [P, T])
        rden = sbuf("rden", [P, QT, HG])
        y = sbuf("y", [P, QT, C])
        yT = sbuf("yT", [C, T]) if wproj is not None else None
        ones = sbuf("ones", [PARTS, T], BF16)
        stats = sbuf("stats", [P, QT, 6])
        mv = sbuf("mv", [P, QT, 2])
        lntmp = sbuf("lntmp", [P, 4, QT])
        rs = sbuf("rs", [P, QT])
        ps_s = [psum(f"ps_s{i}", [P, 2, T]) for i in range(2)]
        ps_m = [psum(f"ps_m{i}", [P, T]) for i in range(2)]
        ps_o = psum("ps_o", [P, T])
        ps_x = psum("ps_x", [P, T])

        s_score = sem("score")
        s_score_free = sem("score_free")
        s_max = sem("max")
        s_max_free = sem("max_free")
        s_masked = sem("masked")
        s_pv = sem("pv")
        s_oT = sem("oT")
        s_job = sem("job")
        s_job_free = sem("job_free")
        s_xin = sem("xin")
        s_split = sem("split")
        s_st = {"k": sem("stack_k"), "q": sem("stack_q")}
        s_mp = sem("mp")
        s_mst = sem("mst")
        s_norm = sem("norm")
        s_ln = sem("ln")
        s_res = sem("res")
        s_init = sem("init")
        s_ones = sem("ones_dma")
        s_passed = sem("passed")
        s_vinit = sem("vinit")

        with nc.Block() as block:
            @block.sync
            def _(sp):
                def load(b, turned):
                    if turned is not None:
                        sp.wait_ge(s_job, turned + 1)
                        by_itself(sp, s_passed)
                    src = x_dram[b] if x_dram is not None else \
                        x[:, bass.ds(QT * b, QT), :] if not isinstance(b, int) else x[:, QT * b:QT * b + QT, :]
                    sp.dma_start(xin[:, :, :], src).then_inc(s_xin, 16)

                load(0, None)
                sp.wait_ge(s_init, 5)
                for i in range(2):
                    sp.dma_start(kst[i][ROWS:ROWS + PARTS, :, :],
                                 ones[:, :].unsqueeze(1).to_broadcast([PARTS, H, T])).then_inc(s_ones, 16)
                sp.wait_ge(s_ones, 32)

                def stacks(b, r, wait_scores):
                    for n, (name, dst) in enumerate((("k", kst[r]), ("q", qst[r]))):
                        sp.wait_ge(s_split, (2 * b + n + 1) * SPLIT)
                        by_itself(sp, s_passed)
                        if n == 0 and wait_scores is not None:
                            sp.wait_ge(s_score, wait_scores)
                        by_itself(sp, s_passed)
                        for a in range(PARTS):
                            for c in range(PARTS):
                                row = (a * PARTS + c) * D
                                src = part[name][:, a if name == "k" else c, :]
                                sp.dma_start(dst[row:row + D, :, :], src).then_inc(s_st[name], 16)

                def max_rows(turned, r, g):
                    sp.wait_ge(s_job_free, turned + FREED)
                    sp.dma_start(qst[r][ROWS:ROWS + PARTS, HG * g:HG * g + HG, :],
                                 mrow[:, :]).then_inc(s_mst, 16)

                def batch(b, r, first=False, last=False, before_last=False):
                    for g in range(NG):
                        if g == NG - 1 and not last and not before_last:
                            load(b + 2, number(b, first, last, 0, "xT"))
                        if g < NG - 1:
                            max_rows(number(b, first, last, g, "maxT"), r, g + 1)
                        elif not last:
                            max_rows(number(b, first, last, g, "maxT"), 1 - r, 0)
                        if g == 0 and not last:
                            stacks(b + 1, 1 - r, None if first else b * (NG * SU))

                stacks(0, 0, None)
                load(1, 0)
                max_rows(len(START) - 1, 0, 0)
                batch(0, 0, first=True)
                with sp.Fori(0, B // 2 - 2) as it:
                    batch(2 * it + 1, 1)
                    batch(2 * it + 2, 0)
                batch(B - 3, 1)
                batch(B - 2, 0, before_last=True)
                batch(B - 1, 1, last=True)

            @block.gpsimd
            def _(pool):
                for st in (*qst, *kst):
                    pool.memset(st[64:FULL, :, :], 0.0).then_inc(s_init, 1)
                pool.wait_ge(s_init, 4)
                pool.memset(ones[:, :], 1.0).then_inc(s_init, 1)
                pool.wait_ge(s_init, 5)

                def parts(b, n, name, turned):
                    base = (2 * b + n) * SPLIT
                    s, t = rope[name], rope[name + "r"]
                    pool.wait_ge(s_job_free, turned + FREED)
                    pool.tensor_tensor(s[:, :], s[:, :], t[:, :], ALU.add).then_inc(s_split, 1)
                    if not (isinstance(b, int) and b == 0):
                        pool.wait_ge(s_st[name], b * (PROD * 16))
                    for i in range(PARTS):
                        pool.wait_ge(s_split, base + 1 + 2 * i)
                        by_itself(pool, s_passed)
                        pool.tensor_copy(part[name][:, i, :], s[:, :]).then_inc(s_split, 1)
                        if i < PARTS - 1:
                            pool.wait_ge(s_split, base + 2 + 2 * i)
                            pool.tensor_tensor(s[:, :], s[:, :], part[name][:, i, :], ALU.subtract)\
                                .then_inc(s_split, 1)

                def batch(b, r, first=False, last=False):
                    for g in range(NG):
                        for j in range(QT):
                            if causal:
                                u0 = sum(HG // u for u in unit_heads[:j])
                                for u in range(HG // unit_heads[j]):
                                    h = u * unit_heads[j]
                                    pool.wait_ge(s_score_free, b * (NG * SU) + g * SU + u0 + u + 3)
                                    by_itself(pool, s_passed)
                                    diag = prob[j % RING][:, h:h + unit_heads[j], 0:P]
                                    pool.affine_select(out=diag, in_=diag, compare_op=ALU.is_ge, fill=0.0,
                                                       base=0, pattern=[[0, unit_heads[j]], [1, P]],
                                                       channel_multiplier=-1).then_inc(s_masked, 1)
                            if not last and (g, j) == (0, 2):
                                parts(b + 1, 0, "k", number(b, first, last, 0, "kr"))
                            if not last and (g, j) == (1, 0):
                                parts(b + 1, 1, "q", number(b, first, last, 1, "qr"))

                parts(0, 0, "k", START.index("kr"))
                parts(0, 1, "q", START.index("qr"))
                batch(0, 0, first=True)
                with pool.Fori(0, B // 2 - 1) as it:
                    batch(2 * it + 1, 1)
                    batch(2 * it + 2, 0)
                batch(B - 1, 1, last=True)

            @block.scalar
            def _(act):
                act.sem_inc(s_score_free, 2)

                def job(name, b, r, n, count):
                    act.wait_ge(s_job, n + 1)
                    if name == "maxT" and count is not None:
                        act.wait_ge(s_mst, count * 16)
                    if name == "xT":
                        ins = act.activation(xT[:, :], ps_x[:, :], ACT.Copy)
                    elif name == "v":
                        ins = act.activation(vst[r][:, :, :, 0:D],
                                             ps_x[:, :].rearrange("p (t h d) -> p t h d", t=QT, h=H), ACT.Copy)
                    elif name == "maxT":
                        ins = act.activation(mrow[:, :], ps_x[0:PARTS * HG, 0:T // 2].bitcast(BF16), ACT.Copy)
                    elif name == "yT":
                        ins = act.activation(yT[:, :], ps_x[:, :], ACT.Copy)
                    ins.then_inc(s_job_free, 1)

                def batch(b, r, first=False, last=False):
                    k = 0
                    for g in range(NG):
                        for j in range(QT):
                            u0 = sum(HG // u for u in unit_heads[:j])
                            w = seen_by[j]
                            for u in range(HG // unit_heads[j]):
                                nu, h = unit_heads[j], u * unit_heads[j]
                                n = b * (NG * SU) + g * SU + u0 + u
                                act.wait_ge(s_score, n + 1)
                                if u == 0 and not (first and g == 0):
                                    act.wait_ge(s_pv, b * (NG * QT) + g * QT + j - RING + 1)
                                pbank = ps_s[(g * SU + u0 + u) % 2]
                                if nu * w == 2 * T or w == T:
                                    src = pbank[:, :, :].rearrange("p a t -> p (a t)")[:, 0:nu * w]\
                                        .rearrange("p (h t) -> p h t", h=nu)
                                elif nu == 2:
                                    src = pbank[:, :, 0:w]
                                else:
                                    src = pbank[:, :, :].rearrange("p a t -> p (a t)")[:, 0:nu * w]\
                                        .rearrange("p (h t) -> p h t", h=nu)
                                act.activation(prob[j % RING][:, h:h + nu, 0:w], src, ACT.Exp,
                                               scale=float(D) ** -0.5).then_inc(s_score_free, 1)
                            if j == 1 and not (first and g == 0):
                                out_evac(b * NG + g - 1, number(b, first, last, g - 1, "norm") if g > 0 and not (first and g == 1)
                                         else None if first else jobs_before(b, first) - 1)
                            for name in jobs(0, g, j, first, last):
                                n = jobs_before(b, first) + k
                                k += 1
                                if name in ("xT", "v"):
                                    job(name, b + 1, 1 - r, n, None)
                                elif name == "maxT":
                                    job(name, None, None, n, b * NG + g + 1)
                                elif name == "yT":
                                    job(name, b - 1, None, n, None)

                def out_evac(n, turned):
                    act.wait_ge(s_pv, n * QT + QT)
                    if turned is not None:
                        act.wait_ge(s_job, turned + 1)
                    act.activation(oT[:, :], ps_o[:, :], ACT.Copy).then_inc(s_oT, 1)

                for n, name in enumerate(START):
                    if name in ("xT", "v"):
                        job(name, 0, 0, n, None)
                    elif name == "maxT":
                        job(name, None, None, n, None)
                batch(0, 0, first=True)
                with act.Fori(0, B // 2 - 1) as it:
                    batch(2 * it + 1, 1)
                    batch(2 * it + 2, 0)
                batch(B - 1, 1, last=True)
                out_evac(G - 1, number(B - 1, False, True, NG - 1, "norm"))
                if wproj is not None:
                    job("yT", B - 1, None, jobs_before(B - 1, False) + len(batch_jobs(False, True)) + 1, None)

            @block.tensor
            def _(pe):
                def job(name, b, r, n, count):
                    pe.wait_ge(s_job_free, n + 1)
                    if name == "xT":
                        pe.wait_ge(s_xin, (b + 1) * 16)
                        for i in range(QT):
                            last = pe.transpose(ps_x[:, P * i:P * i + P], xin[:, i, :], ident[:, :])
                    elif name in ("k", "kr", "q", "qr"):
                        last = pe.matmul(ps_x[:, :], weights[name][:, :], xT[:, :], start=True, stop=True)
                    elif name == "v":
                        for i in range(QT):
                            last = pe.matmul(ps_x[:, P * i:P * i + P], xT[:, P * i:P * i + P], weights["v"][:, :],
                                             start=True, stop=True)
                    elif name == "maxT":
                        pe.wait_ge(s_mp, (count + 1) * MP_STEPS)
                        for i in range(QT):
                            last = pe.transpose(ps_x[0:PARTS * HG, 0:T // 2].bitcast(BF16)[:, P * i:P * i + P],
                                                mpart[:, i, :, :].rearrange("p a h -> p (a h)"), identb[:, :])
                    elif name == "norm":
                        pe.wait_ge(s_oT, count + 1)
                        for i in range(QT):
                            last = pe.transpose(ps_x[:, P * i:P * i + P], oT[:, P * i:P * i + P], ident[:, :])
                    elif name == "yT":
                        for i in range(QT):
                            last = pe.transpose(ps_x[:, P * i:P * i + P], y[:, i, :], ident[:, :])
                    elif name == "proj":
                        for i in range(QT):
                            last = pe.matmul(ps_x[:, P * i:P * i + P], yT[:, P * i:P * i + P], wproj[:, :],
                                             start=True, stop=True)
                    last.then_inc(s_job, 1)

                def maxima(n, r, g, lo, hi):
                    unit = 0
                    for i in range(QT):
                        w = sees[i]
                        for u in range(HG // max_heads[i]):
                            if lo <= unit < hi:
                                pe.wait_ge(s_max_free, n * MU + unit + 1)
                                bank = ps_m[(unit + g * MU) % 2]
                                mh = max_heads[i]
                                for v in range(mh):
                                    h = HG * g + u * mh + v
                                    last = pe.matmul(bank[:, v * w:v * w + w], qst[r][0:ROWS, h, P * i:P * i + P],
                                                     kst[r][0:ROWS, h, 0:w], start=True, stop=not causal)
                                    if causal:
                                        last = pe.matmul(bank[:, v * w + w - P:v * w + w], identb[:, :], mask[:, :],
                                                         start=False, stop=True)
                                last.then_inc(s_max, 1)
                            unit += 1

                def scores(b, r, g, j):
                    u0 = sum(HG // u for u in unit_heads[:j])
                    w = seen_by[j]
                    for u in range(HG // unit_heads[j]):
                        nu = unit_heads[j]
                        n = b * (NG * SU) + g * SU + u0 + u
                        pe.wait_ge(s_score_free, n + 1)
                        pbank = ps_s[(g * SU + u0 + u) % 2]
                        for v in range(nu):
                            h = HG * g + u * nu + v
                            if w * nu <= 2 * T and T % w == 0:
                                dst = pbank[:, (v * w) // T, (v * w) % T:(v * w) % T + w]
                            else:
                                dst = pbank[:, v, 0:w]
                            last = pe.matmul(dst, kst[r][:, h, P * j:P * j + P], qst[r][:, h, T - w:T],
                                             start=True, stop=True)
                        last.then_inc(s_score, 1)

                def values(b, r, g, j):
                    n = b * NG + g
                    if causal:
                        u0 = sum(HG // u for u in unit_heads[:j + 1])
                        pe.wait_ge(s_masked, n * SU + u0)
                    else:
                        u0 = sum(HG // u for u in unit_heads[:j + 1])
                        pe.wait_ge(s_score_free, n * SU + u0 + 2)
                    if j == 0:
                        pe.wait_ge(s_oT, n) if not (isinstance(n, int) and n == 0) else None
                    w = seen_by[j]
                    for h in range(HG):
                        last = pe.matmul(ps_o[VW * h:VW * h + VW, T - w:T], vst[r][:, j, HG * g + h, :],
                                         prob[j % RING][:, h, 0:w], start=(j == 0), stop=(j == QT - 1))
                    last.then_inc(s_pv, 1)

                def batch(b, r, first=False, last=False):
                    k = 0
                    for g in range(NG):
                        for j in range(QT):
                            if j == 0:
                                pe.wait_ge(s_mst, (b * NG + g + 1) * 16)
                            scores(b, r, g, j)
                            if g < NG - 2 or not last:
                                if (g, j) == (NG - 2, 0):
                                    for stack in s_st.values():
                                        pe.wait_ge(stack, (b + 2) * (PROD * 16))
                                a, c = MU * j // QT, MU * (j + 1) // QT
                                if g < NG - 2:
                                    maxima(b * NG + g + 2, r, g + 2, a, c)
                                else:
                                    maxima(b * NG + g + 2, 1 - r, g + 2 - NG, a, c)
                            g2, j2 = (g, j - LAG) if j >= LAG else (g - 1, j - LAG + QT)
                            if g2 >= 0:
                                values(b, r, g2, j2)
                            elif not first:
                                values(b - 1, 1 - r, NG - 1, j2)
                            for name in jobs(0, g, j, first, last):
                                n = jobs_before(b, first) + k
                                k += 1
                                if name in ("xT", "k", "kr", "q", "qr", "v"):
                                    job(name, b + 1, 1 - r, n, None)
                                elif name == "maxT":
                                    job(name, None, None, n, b * NG + g + 1)
                                elif name == "norm":
                                    job(name, None, None, n, b * NG + g - 1)
                                else:
                                    job(name, b - 1, 1 - r, n, None)

                pe.wait_ge(s_vinit, 4)
                for n, name in enumerate(START[:-1]):
                    job(name, 0, 0, n, None)
                for stack in s_st.values():
                    pe.wait_ge(stack, PROD * 16)
                pe.wait_ge(s_ones, 32)
                maxima(0, 0, 0, 0, MU)
                maxima(1, 0, 1, 0, MU)
                job("maxT", None, None, len(START) - 1, 0)
                batch(0, 0, first=True)
                with pe.Fori(0, B // 2 - 1) as it:
                    batch(2 * it + 1, 1)
                    batch(2 * it + 2, 0)
                batch(B - 1, 1, last=True)
                for j in range(QT - LAG, QT):
                    values(B - 1, 1, NG - 1, j)
                n = jobs_before(B - 1, False) + len(batch_jobs(False, True))
                job("norm", None, None, n, G - 1)
                if wproj is not None:
                    job("yT", B - 1, 1, n + 1, None)
                    job("proj", B - 1, 1, n + 2, None)

            @block.vector
            def _(dve):
                dve.sem_inc(s_max_free, 2)
                dve.sem_inc(s_job_free, 1)
                for i in range(2):
                    dve.memset(vst[i][:, :, :, D + 1:VW], 0.0).then_inc(s_vinit, 1)
                    dve.memset(vst[i][:, :, :, D:D + 1], 1.0).then_inc(s_vinit, 1)

                def job(name, b, r, n, count):
                    dve.wait_ge(s_job, n + 1)
                    if name in ("k", "kr", "q", "qr"):
                        if not (isinstance(b, int) and b == 0):
                            dve.wait_ge(s_split, (2 * (b - 1) + (1 if name[0] == "k" else 2)) * SPLIT)
                        dve.tensor_tensor(rope[name][:, :], ps_x[:, :], (sin if name[-1] == "r" else cos)[:, :],
                                          ALU.mult).then_inc(s_job_free, 1)
                    elif name == "proj":
                        residual(b, ps_x[:, :].rearrange("p (i c) -> p i c", i=QT), n)

                def xb(b):
                    return x[:, QT * b:QT * b + QT, :] if isinstance(b, int) else x[:, bass.ds(QT * b, QT), :]

                def residual(b, add, shared):
                    done, count = (s_res, b + 1) if shared is None else (s_job_free, shared + FREED)
                    dve.tensor_tensor(xb(b), xb(b), add, ALU.add).then_inc(done, 1)
                    dve.wait_ge(done, count)
                    layernorm(dve, xb(b), xb(b), stats, mv, rs, lntmp, s_ln, b, s_passed)

                def reduce_units(n, g, lo, hi, turned):
                    unit = 0
                    for i in range(QT):
                        w = sees[i]
                        for u in range(HG // max_heads[i]):
                            if lo <= unit < hi:
                                mh = max_heads[i]
                                dve.wait_ge(s_max, n * MU + unit + 1)
                                dve.reduce_max(mx[:, g % 2, i, u * mh:u * mh + mh],
                                               ps_m[(unit + g * MU) % 2][:, 0:mh * w]
                                               .rearrange("p (h t) -> p h t", h=mh), AX.X)\
                                    .then_inc(s_max_free, 1)
                            unit += 1
                    if hi == MU:
                        split_max(n, g, turned)

                def split_max(n, g, turned):
                    left = [mx[:, g % 2, :, :], rest[:, 0, :, :], rest[:, 1, :, :]]
                    dve.wait_ge(s_max_free, (n + 1) * MU + 2)
                    if turned is not None:
                        dve.wait_ge(s_job, turned + 1)
                    k = n * MP_STEPS
                    dve.tensor_scalar(mpart[:, :, 0, :], left[0], -1.0, None, ALU.mult).then_inc(s_mp, 1)
                    dve.wait_ge(s_mp, k + 1)
                    dve.tensor_tensor(left[1], left[0], mpart[:, :, 0, :], ALU.add).then_inc(s_mp, 1)
                    dve.wait_ge(s_mp, k + 2)
                    dve.tensor_scalar(mpart[:, :, 1, :], left[1], -1.0, None, ALU.mult).then_inc(s_mp, 1)
                    dve.wait_ge(s_mp, k + 3)
                    dve.tensor_tensor(left[2], left[1], mpart[:, :, 1, :], ALU.add).then_inc(s_mp, 1)
                    dve.wait_ge(s_mp, k + 4)
                    dve.tensor_scalar(mpart[:, :, 2, :], left[2], -1.0, None, ALU.mult).then_inc(s_mp, 1)

                def batch(b, r, first=False, last=False):
                    k = 0
                    for g in range(NG):
                        for j in range(QT):
                            if g < NG - 2 or not last:
                                a, c = MU * j // QT, MU * (j + 1) // QT
                                reduce_units(b * NG + g + 2, (g + 2) % NG, a, c, number(b, first, last, g, "maxT"))
                            for name in jobs(0, g, j, first, last):
                                n = jobs_before(b, first) + k
                                k += 1
                                if name in ("k", "kr", "q", "qr"):
                                    job(name, b + 1, None, n, None)
                                elif name == "norm":
                                    norm_job(n, b, g - 1, first)
                                elif name == "proj":
                                    job(name, b - 1, None, n, None)

                def norm_job(n, b, g, first):
                    count = b * NG + g
                    bb, gg = (b, g) if g >= 0 else (b - 1, NG - 1)
                    heads = ps_x[:, :].rearrange("p (i h v) -> p i h v", i=QT, h=HG)
                    dve.wait_ge(s_job, n + 1)
                    dve.reciprocal(rden[:, :, :], heads[:, :, :, D]).then_inc(s_norm, 1)
                    dve.wait_ge(s_norm, count + 1)
                    dve.tensor_tensor(y[:, :, gg * HG * D:(gg + 1) * HG * D].rearrange("p i (h d) -> p i h d", h=HG),
                                      heads[:, :, :, 0:D],
                                      rden[:, :, :].unsqueeze(3).to_broadcast([P, QT, HG, D]),
                                      ALU.mult).then_inc(s_job_free, 1)
                    if gg == NG - 1 and wproj is None:
                        dve.wait_ge(s_job_free, n + FREED)
                        residual(bb, y[:, :, :], None)

                for n, name in enumerate(START[:-1]):
                    if name in ("k", "kr", "q", "qr"):
                        job(name, 0, None, n, None)
                reduce_units(0, 0, 0, MU, None)
                reduce_units(1, 1, 0, MU, len(START) - 1)
                batch(0, 0, first=True)
                with dve.Fori(0, B // 2 - 1) as it:
                    batch(2 * it + 1, 1)
                    batch(2 * it + 2, 0)
                batch(B - 1, 1, last=True)
                n = jobs_before(B - 1, False) + len(batch_jobs(False, True))
                norm_job(n, B - 1, NG - 1, False)
                if wproj is not None:
                    job("proj", B - 1, None, n + 2, None)


MP_STEPS = 5


I32 = mybir.dt.int32
FF = 512
FB = FF // P
E = 7
CAPACITY = 366
ET = 3
SLOTS = ET * P
ST = E * ET
TOP = 2
TC = TOP * NT
TOKENS = NT * P
PAY = 3 + PARTS
BEFORE = 6


def moe_ffn(nc, x, ident, identb, dram, tag="f0"):
    with ExitStack() as ctx:
        def psum(name, shape, dt=F32):
            return ctx.enter_context(nc.psum_tensor(tag + name, shape, dt))

        def sbuf(name, shape, dt=F32):
            return ctx.enter_context(nc.sbuf_tensor(tag + name, shape, dt))

        def sem(name):
            return ctx.enter_context(nc.semaphore(tag + name))

        nrm = [sbuf(f"nrm{i}", [P, QT, C]) for i in range(2)]
        hT = sbuf("hT", [C, TOKENS])
        ln_g = sbuf("ln_g", [C, 1])
        ln_b = sbuf("ln_b", [C, 1])
        wr = sbuf("wr", [C, E])
        w1 = [sbuf(f"w1_{i}", [C, FF]) for i in range(2)]
        w3 = [sbuf(f"w3_{i}", [C, FF]) for i in range(2)]
        w2 = [sbuf(f"w2_{i}", [P, FB, C]) for i in range(2)]
        w1s, w3s, w2s = sbuf("w1s", [C, FF]), sbuf("w3s", [C, FF]), sbuf("w2s", [P, FB, C])
        lgT = sbuf("lgT", [E, T])
        logit = sbuf("logit", [P, NT, E])
        stats, mv = sbuf("stats", [P, QT, 6]), sbuf("mv", [P, QT, 2])
        lntmp, rs = sbuf("lntmp", [P, 4, QT]), sbuf("rs", [P, QT])
        gatea = [sbuf(f"gatea{i}", [P, T]) for i in range(2)]
        copyb = [sbuf(f"copyb{i}", [P, T]) for i in range(2)]
        hid = sbuf("hid", [P, FB, T])
        sharedT = sbuf("sharedT", [C, TOKENS])
        routed = [sbuf(f"routed{i}", [P, QT, C]) for i in range(2)]
        iota_e = sbuf("iota_e", [P, E])
        iota_lo = sbuf("iota_lo", [P, P])
        iota_hi = sbuf("iota_hi", [P, ST])
        iota_t = sbuf("iota_t", [P, NT])
        iota_p = sbuf("iota_p", [P, 1])
        tri = sbuf("tri", [P, P], BF16)
        onesb = sbuf("onesb", [P, P], BF16)
        top = sbuf("top", [P, TOP, NT])
        hot = sbuf("hot", [P, TOP, NT, E])
        hotb = sbuf("hotb", [P, TOP, NT, E], BF16)
        wk = [sbuf(f"wk{i}", [P, TOP, NT, E]) for i in range(3)]
        expert = sbuf("expert", [P, TOP, NT])
        gate = sbuf("gate", [P, TOP, NT])
        grest = [sbuf(f"grest{i}", [P, TOP, NT]) for i in range(2)]
        gpart = sbuf("gpart", [P, PARTS, TOP, NT], BF16)
        small = [sbuf(f"small{i}", [P, TC]) for i in range(4)]
        smalli = [sbuf(f"smalli{i}", [P, TC], I32) for i in range(3)]
        lohot = sbuf("lohot", [P, TC, P], BF16)
        pay = sbuf("pay", [P, TC, PAY, ST], BF16)
        slot = sbuf("slot", [P, PAY, ST])
        sgate = sbuf("sgate", [P, ST])
        stmp = [sbuf(f"stmp{i}", [P, ST]) for i in range(3)]
        token = sbuf("token", [P, ST], I32)
        xg = [sbuf(f"xg{i}", [P, ET, C]) for i in range(2)]
        xeT = [sbuf(f"xeT{i}", [C, SLOTS]) for i in range(2)]
        yeT = sbuf("yeT", [C, SLOTS])
        ye = [sbuf(f"ye{i}", [P, ET, C]) for i in range(2)]
        zero = sbuf("zero", [P, C])
        ps_a = [psum(f"ps_a{i}", [P, T]) for i in range(2)]
        ps_b = [psum(f"ps_b{i}", [P, T]) for i in range(2)]
        ps_y = psum("ps_y", [P, T])
        ps_t = psum("ps_t", [P, T])
        ps_r = psum("ps_r", [P, T])
        ps_r2 = psum("ps_r2", [P, T])

        s_w = sem("w")
        s_we = [sem(f"we{i}") for i in range(2)]
        s_ln = sem("ln")
        s_nout = [sem(f"nout{i}") for i in range(2)]
        s_nT = sem("nT")
        s_hT = sem("hT")
        s_lgT = sem("lgT")
        s_lgc = sem("lgc")
        s_lg = sem("lg")
        s_lge = sem("lge")
        s_const = sem("const")
        s_zero = sem("zero")
        s_rt = sem("rt")
        s_exp = sem("exp")
        s_cnt = sem("cnt")
        s_map = sem("map")
        s_up = sem("up")
        s_gate = sem("gate")
        s_hid = sem("hid")
        s_down = sem("down")
        s_y = sem("y")
        s_gath = [sem(f"gath{i}") for i in range(2)]
        s_xgT = sem("xgT")
        s_xe = sem("xe")
        s_yeT = sem("yeT")
        s_ye = sem("ye")
        s_scat = sem("scat")
        s_sT = sem("sT")
        s_acc = [sem(f"acc{i}") for i in range(2)]
        s_sum = sem("sum")
        s_passed = sem("passed")

        CONSTS = 9
        U_EXP = BEFORE * FB
        U_END = U_EXP + E * FB
        UNITS = U_END + (B - BEFORE) * FB

        with nc.Block() as block:
            @block.sync
            def _(sp):
                for dst, src in ((ln_g[:, :], dram["ln_g"].rearrange("(c a) -> c a", a=1)),
                                 (ln_b[:, :], dram["ln_b"].rearrange("(c a) -> c a", a=1)),
                                 (wr[:, :], dram["Wr"]), (w1s[:, :], dram["W1s"]), (w3s[:, :], dram["W3s"]),
                                 (w2s[:, :, :], dram["W2s"].rearrange("(k p) d -> p k d", p=P))):
                    sp.dma_start(dst, src).then_inc(s_w, 16)

                def expert_weights(e, r):
                    sp.dma_start(w1[r][:, :], dram["W1"][e]).then_inc(s_we[r], 16)
                    sp.dma_start(w3[r][:, :], dram["W3"][e]).then_inc(s_we[r], 16)
                    sp.dma_start(w2[r][:, :, :], dram["W2"][e].rearrange("(k p) d -> p k d", p=P)).then_inc(s_we[r], 16)

                for e in range(2):
                    expert_weights(e, e)
                sp.wait_ge(s_const, 1)
                n_acc = TOKENS // P + 1
                sp.dma_start(dram["acc"].rearrange("(n p) c -> p n c", p=P),
                             zero[:, :].unsqueeze(1).to_broadcast([P, n_acc, C])).then_inc(s_zero, 16)
                sp.dma_start(dram["normed"][TOKENS:TOKENS + P, :], zero[:, :]).then_inc(s_zero, 16)

                def rows_out(c, r):
                    sp.wait_ge(s_ln, (c + 1) * LN_STEPS)
                    by_itself(sp, s_passed)
                    sp.dma_start(dram["normed_rows"](c), nrm[r][:, :, :]).then_inc(s_nout[r], 16)

                with sp.Fori(0, B // 2) as it:
                    rows_out(2 * it, 0)
                    rows_out(2 * it + 1, 1)
                for e in range(2, E):
                    sp.wait_ge(s_down, U_EXP + (e - 1) * FB)
                    expert_weights(e, e % 2)
                sp.wait_ge(s_scat, ST * 16)
                for c in range(B):
                    if c >= 2:
                        sp.wait_ge(s_sum, 2 * (c - 1))
                    sp.dma_start(routed[c % 2][:, :, :],
                                 dram["acc"][c * T:(c + 1) * T, :].rearrange("(i p) c -> p i c", p=P)).then_inc(s_acc[c % 2], 16)

            @block.gpsimd
            def _(pool):
                steps = [0]

                def const(ins):
                    steps[0] += 1
                    ins.then_inc(s_const, 1)

                const(pool.memset(zero[:, :], 0.0))
                const(pool.memset(tri[:, :], 1.0))
                const(pool.memset(onesb[:, :], 1.0))
                pool.wait_ge(s_const, steps[0])
                const(pool.affine_select(out=tri[:, :], in_=tri[:, :], compare_op=ALU.is_ge, fill=0.0, base=0,
                                         pattern=[[1, P]], channel_multiplier=-1))
                for dst, n in ((iota_e, E), (iota_lo, P), (iota_hi, ST), (iota_t, NT)):
                    const(pool.iota(dst[:, :], pattern=[[1, n]], base=0, channel_multiplier=0,
                                    allow_small_or_imprecise_dtypes=True))
                const(pool.iota(iota_p[:, :], pattern=[[1, 1]], base=0, channel_multiplier=1,
                                allow_small_or_imprecise_dtypes=True))
                assert steps[0] == CONSTS

                def product(u, f):
                    pool.wait_ge(s_gate, u + 1)
                    by_itself(pool, s_passed)
                    if not (isinstance(u, int) and u < FB):
                        pool.wait_ge(s_down, u - FB + 1)
                    pool.tensor_tensor(hid[:, f, :], gatea[f % 2][:, :], copyb[f % 2][:, :], ALU.mult)\
                        .then_inc(s_hid, 1)

                for f in range(FB):
                    product(f, f)
                with pool.Fori(1, BEFORE) as c:
                    for f in range(FB):
                        product(c * FB + f, f)
                pool.wait_ge(s_rt, RT_STEPS)
                for stored in s_nout:
                    pool.wait_ge(stored, B // 2 * 16)
                pool.wait_ge(s_zero, 32)

                def gather(e):
                    if e >= 2:
                        pool.wait_ge(s_xgT, e - 1)
                    for i in range(ET):
                        k = e * ET + i
                        pool.indirect_dma_start(xg[e % 2][:, i, :], None, dram["normed"],
                                                bass.IndirectOffsetOnAxis(ap=token[:, k:k + 1], axis=0))\
                            .then_inc(s_gath[e % 2], 16)

                def scatter(e):
                    pool.wait_ge(s_ye, e + 1)
                    for i in range(ET):
                        k = e * ET + i
                        if k:
                            pool.wait_ge(s_scat, k * 16)
                        pool.indirect_dma_start(dram["acc"],
                                                bass.IndirectOffsetOnAxis(ap=token[:, k:k + 1], axis=0),
                                                ye[e % 2][:, i, :], None, compute_op=ALU.add).then_inc(s_scat, 16)

                gather(0)
                gather(1)
                for e in range(E):
                    if e + 2 < E:
                        gather(e + 2)
                    scatter(e)

            @block.scalar
            def _(act):
                act.wait_ge(s_w, 6 * 16)

                def prepare(c):
                    act.wait_ge(s_nT, c + 1)
                    act.activation(hT[:, bass.ds(c * T, T)], ps_t[:, :], ACT.Identity, scale=ln_g[:, 0:1],
                                   bias=ln_b[:, 0:1]).then_inc(s_hT, 1)
                    act.wait_ge(s_lgT, c + 1)
                    act.activation(lgT[:, :], ps_r[0:E, :], ACT.Copy).then_inc(s_lgc, 1)
                    act.wait_ge(s_lg, c + 1)
                    act.activation(logit[:, bass.ds(c * QT, QT), :],
                                   ps_r2[:, 0:QT * E].rearrange("p (i e) -> p i e", i=QT), ACT.Copy)\
                        .then_inc(s_lge, 1)

                def unit(u, f, w, both):
                    act.wait_ge(s_up, u + 1)
                    if not (isinstance(u, int) and u < 2):
                        act.wait_ge(s_hid, u - 1)
                    if both:
                        act.activation(copyb[f % 2][:, 0:w], ps_b[f % 2][:, 0:w], ACT.Copy).then_inc(s_passed, 1)
                    act.activation(gatea[f % 2][:, 0:w], ps_a[f % 2][:, 0:w], ACT.Silu).then_inc(s_gate, 1)

                def shared_out(c, n):
                    act.wait_ge(s_down, n)
                    act.activation(sharedT[:, bass.ds(c * T, T)], ps_y[:, :], ACT.Copy).then_inc(s_y, 1)

                prepare(0)
                prepare(1)
                for f in range(FB):
                    unit(f, f, T, True)
                shared_out(0, FB)
                with act.Fori(1, B // 2) as c:
                    prepare(2 * c)
                    prepare(2 * c + 1)
                    for f in range(FB):
                        unit(c * FB + f, f, T, True)
                    shared_out(c, (c + 1) * FB)
                act.wait_ge(s_rt, RT_DIFF)
                act.activation(gate[:, 1, :], small[0][:, 0:NT], ACT.Exp).then_inc(s_exp, 1)
                with act.Fori(B // 2, BEFORE) as c:
                    for f in range(FB):
                        unit(c * FB + f, f, T, True)
                    shared_out(c, (c + 1) * FB)

                def rows(e, r):
                    act.wait_ge(s_xgT, e + 1)
                    act.activation(xeT[r][:, :], ps_t[:, 0:SLOTS], ACT.Identity, scale=ln_g[:, 0:1],
                                   bias=ln_b[:, 0:1]).then_inc(s_xe, 1)

                def expert_out(e):
                    act.wait_ge(s_down, U_EXP + (e + 1) * FB)
                    if not (isinstance(e, int) and e == 0):
                        act.wait_ge(s_yeT, e)
                    act.activation(yeT[:, :], ps_y[:, 0:SLOTS], ACT.Copy).then_inc(s_y, 1)

                def expert(e, r, last=False):
                    for f in range(FB):
                        unit(U_EXP + e * FB + f, f, SLOTS, False)
                        if f == 1 and not last:
                            rows(e + 1, 1 - r)
                    expert_out(e)

                rows(0, 0)
                expert(0, 0)
                with act.Fori(0, (E - 1) // 2 - 1) as it:
                    expert(2 * it + 1, 1)
                    expert(2 * it + 2, 0)
                expert(E - 2, 1)
                expert(E - 1, 0, last=True)
                with act.Fori(BEFORE, B) as c:
                    for f in range(FB):
                        unit(E * FB + c * FB + f, f, T, False)
                    shared_out(c, (c + 1) * FB + E * FB)

            @block.tensor
            def _(pe):
                pe.wait_ge(s_w, 6 * 16)

                def prepare(c, r):
                    pe.wait_ge(s_ln, (c + 1) * LN_STEPS)
                    if not (isinstance(c, int) and c == 0):
                        pe.wait_ge(s_hT, c)
                    for i in range(QT):
                        last = pe.transpose(ps_t[:, P * i:P * i + P], nrm[r][:, i, :], ident[:, :])
                    last.then_inc(s_nT, 1)
                    pe.wait_ge(s_hT, c + 1)
                    if not (isinstance(c, int) and c == 0):
                        pe.wait_ge(s_lgc, c)
                    pe.matmul(ps_r[0:E, :], wr[:, :], hT[:, bass.ds(c * T, T)], start=True, stop=True)\
                        .then_inc(s_lgT, 1)
                    pe.wait_ge(s_lgc, c + 1)
                    if not (isinstance(c, int) and c == 0):
                        pe.wait_ge(s_lge, c)
                    by_itself(pe, s_passed)
                    for i in range(QT):
                        last = pe.transpose(ps_r2[:, E * i:E * i + E], lgT[:, P * i:P * i + P], ident[0:E, 0:E])
                    last.then_inc(s_lg, 1)

                def up(u, f, wa, wb, rhs, w):
                    if not (isinstance(u, int) and u < 2):
                        pe.wait_ge(s_hid, u - 1)
                    pe.matmul(ps_a[f % 2][:, 0:w], wa[:, P * f:P * f + P], rhs, start=True, stop=True)
                    pe.matmul(ps_b[f % 2][:, 0:w], wb[:, P * f:P * f + P], rhs, start=True, stop=True)\
                        .then_inc(s_up, 1)

                def down(u, f, wd, w, outs):
                    pe.wait_ge(s_hid, u + 1)
                    if f == 0 and not (isinstance(outs, int) and outs == 0):
                        pe.wait_ge(s_y, outs)
                    pe.matmul(ps_y[:, 0:w], wd[:, f, :], hid[:, f, 0:w], start=(f == 0), stop=(f == FB - 1))\
                        .then_inc(s_down, 1)

                def shared(c, u, outs):
                    rhs = hT[:, bass.ds(c * T, T)]
                    for f in range(FB):
                        up(u + f, f, w1s, w3s, rhs, T)
                        if f:
                            down(u + f - 1, f - 1, w2s, T, outs)
                    down(u + FB - 1, FB - 1, w2s, T, outs)

                prepare(0, 0)
                prepare(1, 1)
                shared(0, 0, 0)
                with pe.Fori(1, B // 2) as c:
                    prepare(2 * c, 0)
                    prepare(2 * c + 1, 1)
                    shared(c, c * FB, c)
                pe.wait_ge(s_const, CONSTS)
                pe.wait_ge(s_rt, RT_HOT)
                pe.matmul(ps_r[:, 0:TC * E], tri[:, :], hotb[:, :, :, :].rearrange("p s t e -> p (s t e)"),
                          start=True, stop=True)
                pe.matmul(ps_r2[:, 0:TC * E], onesb[:, :], hotb[:, :, :, :].rearrange("p s t e -> p (s t e)"),
                          start=True, stop=True).then_inc(s_cnt, 1)
                with pe.Fori(B // 2, BEFORE) as c:
                    shared(c, c * FB, c)
                pe.wait_ge(s_rt, RT_PAY)
                for k in range(TC):
                    last = pe.matmul(ps_t[:, 0:PAY * ST], lohot[:, k, :], pay[:, k, :, :].rearrange("p a h -> p (a h)"),
                                     start=(k == 0), stop=(k == TC - 1))
                last.then_inc(s_map, 1)

                def rows(e, r, n):
                    pe.wait_ge(s_gath[r], n * ET * 16)
                    if isinstance(e, int) and e == 0:
                        pe.wait_ge(s_rt, RT_SLOT)
                    for i in range(ET):
                        last = pe.transpose(ps_t[:, P * i:P * i + P], xg[r][:, i, :], ident[:, :])
                    last.then_inc(s_xgT, 1)

                def back(e):
                    pe.wait_ge(s_y, BEFORE + e + 1)
                    if not (isinstance(e, int) and e == 0):
                        pe.wait_ge(s_ye, e)
                    for i in range(ET):
                        last = pe.transpose(ps_r[:, P * i:P * i + P], yeT[:, P * i:P * i + P], ident[:, :])
                    last.then_inc(s_yeT, 1)

                def expert(e, r, n, last=False, first=False):
                    u = U_EXP + e * FB
                    pe.wait_ge(s_we[r], n * 48)
                    for f in range(FB):
                        if f == 0:
                            pe.wait_ge(s_xe, e + 1)
                        up(u + f, f, w1[r], w3[r], xeT[r][:, :], SLOTS)
                        if f:
                            down(u + f - 1, f - 1, w2[r], SLOTS, BEFORE + e)
                        if f == 1:
                            if not last:
                                rows(e + 1, 1 - r, n + (1 if r else 0))
                            if not first:
                                back(e - 1)
                    down(u + FB - 1, FB - 1, w2[r], SLOTS, BEFORE + e)

                rows(0, 0, 1)
                expert(0, 0, 1, first=True)
                with pe.Fori(0, (E - 1) // 2 - 1) as it:
                    expert(2 * it + 1, 1, it + 1)
                    expert(2 * it + 2, 0, it + 2)
                expert(E - 2, 1, (E - 1) // 2)
                expert(E - 1, 0, (E + 1) // 2, last=True)
                back(E - 1)
                with pe.Fori(BEFORE, B) as c:
                    shared(c, c * FB + E * FB, c + E)

                def turn(c):
                    if not (isinstance(c, int) and c == 0):
                        pe.wait_ge(s_sum, 2 * c - 1)
                    for i in range(QT):
                        last = pe.transpose(ps_t[:, P * i:P * i + P], sharedT[:, (c * QT + i) * P:(c * QT + i + 1) * P],
                                            ident[:, :])
                    last.then_inc(s_sT, 1)

                pe.wait_ge(s_y, B + E)
                for c in range(B):
                    turn(c)

            def route(dve):
                steps = [0]

                def step(ins, at=None):
                    steps[0] += 1
                    ins.then_inc(s_rt, 1)
                    dve.wait_ge(s_rt, steps[0])
                    assert at is None or at == steps[0], (at, steps[0])

                def over_e(ap):
                    return ap.unsqueeze(2).to_broadcast([P, NT, E])

                def e_row():
                    return iota_e[:, :].unsqueeze(1).to_broadcast([P, NT, E])

                dve.wait_ge(s_const, CONSTS)
                dve.wait_ge(s_lge, B)
                left = logit[:, :, :]
                for s in range(TOP):
                    step(dve.reduce_max(top[:, s, :], left, AX.X))
                    a, b = wk[0][:, 0, :, :], wk[1][:, 0, :, :]
                    step(dve.tensor_tensor(a, left, over_e(top[:, s, :]), ALU.is_lt))
                    step(dve.scalar_tensor_tensor(b, a, 8.0, e_row(), ALU.mult, ALU.add))
                    step(dve.tensor_reduce(expert[:, s, :], b, AX.X, ALU.min))
                    step(dve.tensor_tensor(hot[:, s, :, :], e_row(), over_e(expert[:, s, :]), ALU.is_equal))
                    if s == 0:
                        left = wk[2][:, 0, :, :]
                        step(dve.scalar_tensor_tensor(left, hot[:, 0, :, :], -3.0e38, logit[:, :, :], ALU.mult, ALU.add))
                step(dve.tensor_copy(hotb[:, :, :, :], hot[:, :, :, :]), RT_HOT)
                step(dve.tensor_tensor(small[0][:, 0:NT], top[:, 1, :], top[:, 0, :], ALU.subtract), RT_DIFF)
                dve.wait_ge(s_cnt, 1)
                flat = [w[:, :, :, :].rearrange("p s t e -> p (s t) e") for w in wk]
                step(dve.tensor_copy(flat[0], ps_r2[:, 0:TC * E].rearrange("p (k e) -> p k e", e=E)))
                cur, nxt, d = 0, 1, 1
                while d < TC:
                    step(dve.tensor_copy(flat[nxt][:, 0:d, :], flat[cur][:, 0:d, :]))
                    step(dve.tensor_tensor(flat[nxt][:, d:TC, :], flat[cur][:, d:TC, :], flat[cur][:, 0:TC - d, :], ALU.add))
                    cur, nxt, d = nxt, cur, 2 * d
                step(dve.tensor_tensor(flat[cur], flat[cur], ps_r2[:, 0:TC * E].rearrange("p (k e) -> p k e", e=E), ALU.subtract))
                step(dve.tensor_tensor(flat[cur], flat[cur], ps_r[:, 0:TC * E].rearrange("p (k e) -> p k e", e=E), ALU.add))
                hotf = hot[:, :, :, :].rearrange("p s t e -> p (s t) e")
                step(dve.tensor_tensor(flat[2], flat[cur], hotf, ALU.mult))
                rank = small[1]
                step(dve.tensor_reduce(rank[:, :], flat[2], AX.X, ALU.add))
                pos, lo, hi = smalli
                step(dve.tensor_scalar(pos[:, :], rank[:, :], -1.0, None, ALU.add))
                step(dve.tensor_scalar(lo[:, :], pos[:, :], P - 1, None, ALU.bitwise_and))
                step(dve.tensor_scalar(hi[:, :], pos[:, :], P.bit_length() - 1, None, ALU.arith_shift_right))
                lof, hif = small[2], small[3]
                step(dve.tensor_copy(lof[:, :], lo[:, :]))
                step(dve.tensor_copy(hif[:, :], hi[:, :]))
                step(dve.scalar_tensor_tensor(hif[:, :], expert[:, :, :].rearrange("p s t -> p (s t)"), float(ET),
                                              hif[:, :], ALU.mult, ALU.add))
                step(dve.tensor_scalar(rank[:, :], rank[:, :], float(CAPACITY), 1000.0, ALU.is_gt, ALU.mult))
                step(dve.tensor_tensor(hif[:, :], hif[:, :], rank[:, :], ALU.add))
                dve.wait_ge(s_exp, 1)
                step(dve.tensor_scalar(gate[:, 0, :], gate[:, 1, :], 1.0, None, ALU.add))
                step(dve.reciprocal(gate[:, 0, :], gate[:, 0, :]))
                step(dve.tensor_tensor(gate[:, 1, :], gate[:, 1, :], gate[:, 0, :], ALU.mult))
                rests = [gate, grest[0], grest[1]]
                for i in range(PARTS):
                    step(dve.tensor_copy(gpart[:, i, :, :], rests[i][:, :, :]))
                    if i < PARTS - 1:
                        step(dve.tensor_tensor(rests[i + 1][:, :, :], rests[i][:, :, :], gpart[:, i, :, :], ALU.subtract))
                step(dve.tensor_tensor(lohot[:, :, :], iota_lo[:, :].unsqueeze(1).to_broadcast([P, TC, P]),
                                       lof[:, :].unsqueeze(2).to_broadcast([P, TC, P]), ALU.is_equal))
                filled = pay[:, :, 0, :]
                step(dve.tensor_tensor(filled, iota_hi[:, :].unsqueeze(1).to_broadcast([P, TC, ST]),
                                       hif[:, :].unsqueeze(2).to_broadcast([P, TC, ST]), ALU.is_equal))
                for s in range(TOP):
                    step(dve.tensor_tensor(pay[:, NT * s:NT * s + NT, 1, :], pay[:, NT * s:NT * s + NT, 0, :],
                                           iota_t[:, :].unsqueeze(2).to_broadcast([P, NT, ST]), ALU.mult))
                step(dve.tensor_scalar(pay[:, :, 2, :], filled, iota_p[:, 0:1], None, ALU.mult))
                for i in range(PARTS):
                    step(dve.tensor_tensor(pay[:, :, 3 + i, :], filled,
                                           gpart[:, i, :, :].rearrange("p s t -> p (s t)").unsqueeze(2).to_broadcast([P, TC, ST]),
                                           ALU.mult), RT_PAY if i == PARTS - 1 else None)
                dve.wait_ge(s_map, 1)
                step(dve.tensor_copy(slot[:, :, :], ps_t[:, 0:PAY * ST].rearrange("p (a h) -> p a h", a=PAY)), RT_SLOT)
                step(dve.scalar_tensor_tensor(stmp[0][:, :], slot[:, 1, :], float(P), slot[:, 2, :], ALU.mult, ALU.add))
                step(dve.tensor_scalar(stmp[1][:, 0:1], iota_p[:, :], float(TOKENS), None, ALU.add))
                step(dve.tensor_scalar(stmp[2][:, :], slot[:, 0, :], -1.0, 1.0, ALU.mult, ALU.add))
                step(dve.scalar_tensor_tensor(token[:, :], stmp[2][:, :], stmp[1][:, 0:1], stmp[0][:, :], ALU.mult, ALU.add))
                step(dve.tensor_tensor(sgate[:, :], slot[:, 3 + PARTS - 1, :], slot[:, 3 + PARTS - 2, :], ALU.add))
                step(dve.tensor_tensor(sgate[:, :], sgate[:, :], slot[:, 3, :], ALU.add), RT_STEPS)

            @block.vector
            def _(dve):
                def xb(b):
                    return x[:, bass.ds(QT * b, QT), :]

                def normed(c, r, before):
                    if not (isinstance(before, int) and before == 0):
                        dve.wait_ge(s_nT, c - 1)
                        dve.wait_ge(s_nout[r], before * 16)
                    layernorm(dve, nrm[r][:, :, :], xb(c), stats, mv, rs, lntmp, s_ln, c, s_passed)

                normed(0, 0, 0)
                normed(1, 1, 0)
                with dve.Fori(1, B // 2) as it:
                    normed(2 * it, 0, it)
                    normed(2 * it + 1, 1, it)

                route(dve)

                def product(u, f, w):
                    dve.wait_ge(s_gate, u + 1)
                    dve.wait_ge(s_down, u - FB + 1)
                    dve.tensor_tensor(hid[:, f, 0:w], gatea[f % 2][:, 0:w], ps_b[f % 2][:, 0:w], ALU.mult)\
                        .then_inc(s_hid, 1)

                def gated(e, r):
                    dve.wait_ge(s_yeT, e + 1)
                    if not (isinstance(e, int) and e < 2):
                        dve.wait_ge(s_scat, (e - 1) * (ET * 16))
                    for i in range(ET):
                        ins = dve.tensor_tensor(ye[r][:, i, :], ps_r[:, P * i:P * i + P],
                                                sgate[:, bass.ds(e * ET + i, 1)].to_broadcast([P, C]), ALU.mult)
                        if i == ET - 1:
                            ins.then_inc(s_ye, 1)

                def expert(e, r, first=False):
                    for f in range(FB):
                        product(U_EXP + e * FB + f, f, SLOTS)
                        if f == 1 and not first:
                            gated(e - 1, 1 - r)

                expert(0, 0, first=True)
                expert(1, 1)
                expert(2, 0)
                with dve.Fori(1, (E - 1) // 2) as it:
                    expert(2 * it + 1, 1)
                    expert(2 * it + 2, 0)
                gated(E - 1, 0)
                with dve.Fori(BEFORE, B) as c:
                    for f in range(FB):
                        product(E * FB + c * FB + f, f, T)
                for c in range(B):
                    dve.wait_ge(s_sT, c + 1)
                    dve.tensor_tensor(xb(c), xb(c), ps_t[:, :].rearrange("p (i c) -> p i c", i=QT), ALU.add)\
                        .then_inc(s_sum, 1)
                    dve.wait_ge(s_sum, 2 * c + 1)
                    dve.wait_ge(s_acc[c % 2], (c // 2 + 1) * 16)
                    dve.tensor_tensor(xb(c), xb(c), routed[c % 2][:, :, :], ALU.add).then_inc(s_sum, 1)
                    dve.wait_ge(s_sum, 2 * c + 2)
                    layernorm(dve, xb(c), xb(c), stats, mv, rs, lntmp, s_ln, B + c, s_passed)


RT_HOT = 12
RT_DIFF = 13
RT_PAY = 54
RT_SLOT = 55
RT_STEPS = 61


def dense_ffn(nc, x, ident, dram, out_rows, tag="f1"):
    with ExitStack() as ctx:
        def psum(name, shape, dt=F32):
            return ctx.enter_context(nc.psum_tensor(tag + name, shape, dt))

        def sbuf(name, shape, dt=F32):
            return ctx.enter_context(nc.sbuf_tensor(tag + name, shape, dt))

        def sem(name):
            return ctx.enter_context(nc.semaphore(tag + name))

        raw = {"w1": sbuf("w1r", [P, FB, C]), "w2": sbuf("w2r", [P, FB, C]), "h1": sbuf("h1r", [P, FB, FF]),
               "h2": sbuf("h2r", [P, FB, FF]), "w3": sbuf("w3r", [P, 1, FF])}
        wT = {"w1": sbuf("w1T", [P, 1, FF]), "w2": sbuf("w2T", [P, 1, FF]), "h1": sbuf("h1T", [P, FB, FF]),
              "h2": sbuf("h2T", [P, FB, FF]), "w3": sbuf("w3T", [P, FB, C])}
        sc = {"w1": sbuf("w1s", [P, FB]), "w2": sbuf("w2s", [P, FB]), "h1": sbuf("h1s", [P, FB]),
              "h2": sbuf("h2s", [P, FB]), "w3": sbuf("w3s", [P, 1])}
        half = sbuf("half", [P, FB])
        gated = sbuf("gated", [P, FB])
        xin = sbuf("xin", [P, QT, C])
        xT = sbuf("xT", [C, T])
        th = [sbuf(f"th{i}", [P, T]) for i in range(2)]
        u_sb = [sbuf(f"u{i}", [P, T]) for i in range(2)]
        hid = [sbuf(f"hid{i}", [P, FB, T]) for i in range(3)]
        yT = sbuf("yT", [C, T])
        res = sbuf("res", [P, QT, C])
        fin = [sbuf(f"fin{i}", [P, QT, C]) for i in range(2)]
        stats, mv = sbuf("stats", [P, QT, 6]), sbuf("mv", [P, QT, 2])
        lntmp, rs = sbuf("lntmp", [P, 4, QT]), sbuf("rs", [P, QT])
        ps_a = [psum(f"ps_a{i}", [P, T]) for i in range(2)]
        ps_b = [psum(f"ps_b{i}", [P, T]) for i in range(2)]
        ps_h = [psum(f"ps_h{i}", [P, T]) for i in range(2)]
        ps_y = psum("ps_y", [P, T])
        ps_t = psum("ps_t", [P, T])

        s_w = sem("w")
        s_wt = sem("wt")
        s_wc = sem("wc")
        s_sc = sem("sc")
        s_xin = sem("xin")
        s_xt = sem("xt")
        s_xc = sem("xc")
        s_up = sem("up")
        s_th = sem("th")
        s_g = sem("g")
        s_h = sem("h")
        s_ge = sem("ge")
        s_y = sem("y")
        s_yc = sem("yc")
        s_t = sem("t")
        s_res = sem("res")
        s_ln = sem("ln")
        s_out = [sem(f"out{i}") for i in range(2)]
        s_passed = sem("passed")

        TURNS = [("w1", [(0, o) for o in range(FB)]), ("w2", [(0, o) for o in range(FB)])] + \
                [(w, [(k, o) for o in range(FB)]) for w in ("h1", "h2") for k in range(FB)] + \
                [("w3", [(k, 0) for k in range(FB)])]

        with nc.Block() as block:
            @block.sync
            def _(sp):
                for w in ("w1", "w2", "h1", "h2", "w3"):
                    sp.dma_start(raw[w][:, :, :], dram[w + "_w"].rearrange("(o p) i -> p o i", p=P)).then_inc(s_w, 16)
                    with nc.allow_non_contiguous_dma(reason="a few hundred scales"):
                        sp.dma_start(sc[w][:, :], dram[w + "_s"].rearrange("(o p) -> p o", p=P)).then_inc(s_w, 16)

                def load(c):
                    if not (isinstance(c, int) and c == 0):
                        sp.wait_ge(s_xt, c)
                        by_itself(sp, s_passed)
                    sp.dma_start(xin[:, :, :], x[:, bass.ds(c * QT, QT), :]).then_inc(s_xin, 16)

                def store(c, r):
                    sp.wait_ge(s_ln, (c + 1) * LN_STEPS)
                    by_itself(sp, s_passed)
                    sp.dma_start(out_rows(c), fin[r][:, :, :]).then_inc(s_out[r], 16)

                load(0)
                load(1)
                with sp.Fori(0, B // 2 - 1) as it:
                    load(2 * it + 2)
                    store(2 * it, 0)
                    load(2 * it + 3)
                    store(2 * it + 1, 1)
                store(B - 2, 0)
                store(B - 1, 1)
                for r in range(2):
                    sp.wait_ge(s_out[r], B // 2 * 16)

            @block.scalar
            def _(act):
                for n, (w, blocks) in enumerate(TURNS):
                    act.wait_ge(s_wt, n + 1)
                    src = (ps_a + ps_b)[n % 4]
                    if w == "w3":
                        dst = wT[w][:, :, :].rearrange("p k c -> p (k c)")
                    else:
                        dst = wT[w][:, blocks[0][0], :]
                    act.activation(dst, src[:, :], ACT.Copy).then_inc(s_wc, 1)
                act.wait_ge(s_sc, 2)

                def turned(c):
                    act.wait_ge(s_xt, c + 1)
                    act.activation(xT[:, :], ps_t[:, :], ACT.Copy).then_inc(s_xc, 1)

                def gate(c, f):
                    u = c * FB + f
                    act.wait_ge(s_up, u + 1)
                    if not (isinstance(u, int) and u < 2):
                        act.wait_ge(s_g, 2 * (u - 1))
                    act.activation(th[f % 2][:, :], ps_a[f % 2][:, :], ACT.Tanh, scale=half[:, f:f + 1])\
                        .then_inc(s_th, 1)

                def layer(c, n):
                    w, first = ("h1", "h2")[n], not isinstance(c, int) or c > 0
                    for f in range(FB):
                        u = (2 * c + n) * FB + f
                        act.wait_ge(s_h, u + 1)
                        act.activation(hid[n + 1][:, f, :], ps_h[f % 2][:, :], ACT.Gelu, scale=sc[w][:, f:f + 1])\
                            .then_inc(s_ge, 1)

                def out(c):
                    act.wait_ge(s_y, c + 1)
                    act.activation(yT[:, :], ps_y[:, :], ACT.Copy, scale=sc["w3"][:, 0:1]).then_inc(s_yc, 1)

                def chunk(c, last=False):
                    layer(c, 0)
                    if not last:
                        turned(c + 1)
                        gate(c + 1, 0)
                        gate(c + 1, 1)
                    layer(c, 1)
                    if not last:
                        gate(c + 1, 2)
                        gate(c + 1, 3)
                    out(c)

                turned(0)
                for f in range(FB):
                    gate(0, f)
                with act.Fori(0, B - 1) as c:
                    chunk(c)
                chunk(B - 1, last=True)

            @block.tensor
            def _(pe):
                for n, (w, blocks) in enumerate(TURNS):
                    if n == 0:
                        pe.wait_ge(s_w, 10 * 16)
                    if n >= 4:
                        pe.wait_ge(s_wc, n - 3)
                    for i, (k, o) in enumerate(blocks):
                        last = pe.transpose((ps_a + ps_b)[n % 4][:, P * i:P * i + P], raw[w][:, o, P * k:P * k + P],
                                            ident[:, :])
                    last.then_inc(s_wt, 1)
                pe.wait_ge(s_wc, len(TURNS))

                def turn(c):
                    pe.wait_ge(s_xin, (c + 1) * 16)
                    if not (isinstance(c, int) and c <= 1):
                        pe.wait_ge(s_res, c - 1)
                    for i in range(QT):
                        last = pe.transpose(ps_t[:, P * i:P * i + P], xin[:, i, :], ident[:, :])
                    last.then_inc(s_xt, 1)

                def up(c, f):
                    u = c * FB + f
                    if f == 0:
                        pe.wait_ge(s_xc, c + 1)
                    if not (isinstance(u, int) and u < 2):
                        pe.wait_ge(s_g, 2 * (u - 1))
                    pe.matmul(ps_a[f % 2][:, :], wT["w1"][:, 0, P * f:P * f + P], xT[:, :], start=True, stop=True)
                    pe.matmul(ps_b[f % 2][:, :], wT["w2"][:, 0, P * f:P * f + P], xT[:, :], start=True, stop=True)\
                        .then_inc(s_up, 1)

                def layer(c, n):
                    w = ("h1", "h2")[n]
                    if n == 0:
                        pe.wait_ge(s_g, 2 * (c + 1) * FB)
                    else:
                        pe.wait_ge(s_ge, (2 * c + 1) * FB)
                    for f in range(FB):
                        u = (2 * c + n) * FB + f
                        if n or f >= 2:
                            pe.wait_ge(s_ge, u - 1)
                        for k in range(FB):
                            last = pe.matmul(ps_h[f % 2][:, :], wT[w][:, k, P * f:P * f + P], hid[n][:, k, :],
                                             start=(k == 0), stop=(k == FB - 1))
                        last.then_inc(s_h, 1)

                def out(c):
                    pe.wait_ge(s_ge, (2 * c + 2) * FB)
                    if not (isinstance(c, int) and c == 0):
                        pe.wait_ge(s_yc, c)
                    for k in range(FB):
                        last = pe.matmul(ps_y[:, :], wT["w3"][:, k, :], hid[2][:, k, :], start=(k == 0),
                                         stop=(k == FB - 1))
                    last.then_inc(s_y, 1)

                def back(c):
                    pe.wait_ge(s_yc, c + 1)
                    if not (isinstance(c, int) and c == 0):
                        pe.wait_ge(s_res, c)
                    for i in range(QT):
                        last = pe.transpose(ps_t[:, P * i:P * i + P], yT[:, P * i:P * i + P], ident[:, :])
                    last.then_inc(s_t, 1)

                def chunk(c, first=False, last=False):
                    if not last:
                        turn(c + 1)
                    layer(c, 0)
                    if not last:
                        up(c + 1, 0)
                        up(c + 1, 1)
                    layer(c, 1)
                    if not last:
                        up(c + 1, 2)
                        up(c + 1, 3)
                    out(c)
                    back(c)

                turn(0)
                for f in range(FB):
                    up(0, f)
                with pe.Fori(0, B - 1) as c:
                    chunk(c)
                chunk(B - 1, last=True)

            @block.vector
            def _(dve):
                dve.wait_ge(s_w, 10 * 16)
                dve.tensor_scalar(half[:, :], sc["w1"][:, :], 0.5, None, ALU.mult).then_inc(s_sc, 1)
                dve.wait_ge(s_sc, 1)
                dve.tensor_tensor(gated[:, :], half[:, :], sc["w2"][:, :], ALU.mult).then_inc(s_sc, 1)
                dve.wait_ge(s_sc, 2)

                def gate(c, f):
                    u = c * FB + f
                    dve.wait_ge(s_th, u + 1)
                    dve.scalar_tensor_tensor(u_sb[f % 2][:, :], th[f % 2][:, :], 1.0, ps_a[f % 2][:, :], ALU.add, ALU.mult)\
                        .then_inc(s_g, 1)
                    if not (isinstance(c, int) and c == 0):
                        dve.wait_ge(s_h, 2 * c * FB - FB)
                    dve.wait_ge(s_g, 2 * u + 1)
                    dve.scalar_tensor_tensor(hid[0][:, f, :], ps_b[f % 2][:, :], gated[:, f:f + 1], u_sb[f % 2][:, :],
                                             ALU.mult, ALU.mult).then_inc(s_g, 1)

                def finish(c, r, before):
                    dve.wait_ge(s_t, c + 1)
                    if not (isinstance(c, int) and c == 0):
                        by_itself(dve, s_passed)
                        dve.wait_ge(s_ln, c * LN_STEPS)
                    dve.tensor_tensor(res[:, :, :], x[:, bass.ds(c * QT, QT), :],
                                      ps_t[:, :].rearrange("p (i c) -> p i c", i=QT), ALU.add).then_inc(s_res, 1)
                    dve.wait_ge(s_res, c + 1)
                    if before is not None:
                        dve.wait_ge(s_out[r], before * 16)
                    layernorm(dve, fin[r][:, :, :], res[:, :, :], stats, mv, rs, lntmp, s_ln, c, s_passed)

                for f in range(FB):
                    gate(0, f)

                def chunk(c, r, before, last=False):
                    if not last:
                        for f in range(FB):
                            gate(c + 1, f)
                    finish(c, r, before)

                chunk(0, 0, None)
                chunk(1, 1, None)
                with dve.Fori(1, B // 2 - 1) as it:
                    chunk(2 * it, 0, it)
                    chunk(2 * it + 1, 1, it)
                chunk(B - 2, 0, B // 2 - 1)
                chunk(B - 1, 1, B // 2 - 1, last=True)


def prologue(nc, x, x_rows, ident, identb, mask, wqkv, heads0, wq1, heads1, wproj, wproj_dram, cos, sin, angles):
    with ExitStack() as ctx:
        def sbuf(name, shape, dt=F32):
            return ctx.enter_context(nc.sbuf_tensor("pre_" + name, shape, dt))

        def sem(name):
            return ctx.enter_context(nc.semaphore("pre_" + name))

        w0 = sbuf("w0", [C, 3 * C])
        w1 = [sbuf("w1" + n, [C, C]) for n in "qkv"]
        ps_w = [ctx.enter_context(nc.psum_tensor(f"pre_ps{i}", [P, C], F32)) for i in range(3)]
        s_w = sem("w")
        s_x = sem("x")
        s_const = sem("const")
        s_turn = sem("turn")
        s_done = sem("done")

        with nc.Block() as block:
            @block.sync
            def _(sp):
                sp.dma_start(w0[:, :], wqkv).then_inc(s_w, 16)
                for dst, src in zip(w1, wq1):
                    sp.dma_start(dst[:, :], src).then_inc(s_w, 16)
                sp.dma_start(wproj[:, :], wproj_dram).then_inc(s_w, 16)
                sp.wait_ge(s_w, 5 * 16)

            @block.scalar
            def _(act):
                for table, angle in ((cos, angles[0]), (sin, angles[1])):
                    for d in range(D):
                        act.dma_start(table[H * d:H * d + H, :], angle[d:d + 1, :].to_broadcast([H, T])).then_inc(s_x, 16)
                act.dma_start(x[:, :, :], x_rows).then_inc(s_x, 16)
                act.wait_ge(s_x, (2 * D + 1) * 16)

            @block.gpsimd
            def _(pool):
                for m in (ident, identb, mask):
                    pool.memset(m[:, :], 0.0).then_inc(s_const, 1)
                pool.wait_ge(s_const, 3)
                for m in (ident, identb):
                    pool.affine_select(out=m[:, :], in_=m[:, :], compare_op=ALU.not_equal, fill=1.0, base=0,
                                       pattern=[[-1, P]], channel_multiplier=1).then_inc(s_const, 1)
                pool.affine_select(out=mask[:, :], in_=mask[:, :], compare_op=ALU.is_ge, fill=-1e30, base=0,
                                   pattern=[[-1, P]], channel_multiplier=1).then_inc(s_const, 1)
                pool.wait_ge(s_const, 6)

            @block.tensor
            def _(pe):
                pe.wait_ge(s_w, 5 * 16)
                pe.wait_ge(s_const, 6)
                for i in range(3):
                    pe.transpose(ps_w[i][:, :], w1[i][:, :], ident[:, :]).then_inc(s_turn, 1)

            @block.vector
            def _(dve):
                def columns(out, name, src):
                    hd = src.rearrange("c (h d) -> c h d", h=H)
                    dve.tensor_copy(out[name][:, :].rearrange("c (d h) -> c h d", h=H), hd).then_inc(s_done, 1)
                    pairs = src.rearrange("c (h i two) -> c two h i", h=H, two=2)
                    dst = out[name + "r"][:, :].rearrange("c (i two h) -> c two h i", two=2, h=H)
                    dve.tensor_scalar(dst[:, 0], pairs[:, 1], -1.0, None, ALU.mult).then_inc(s_done, 1)
                    dve.tensor_copy(dst[:, 1], pairs[:, 0]).then_inc(s_done, 1)

                dve.wait_ge(s_w, 5 * 16)
                columns(heads0, "q", w0[:, 0:C])
                columns(heads0, "k", w0[:, C:2 * C])
                dve.tensor_copy(heads0["v"][:, :], w0[:, 2 * C:3 * C]).then_inc(s_done, 1)
                dve.wait_ge(s_turn, 3)
                columns(heads1, "q", ps_w[0][:, :])
                columns(heads1, "k", ps_w[1][:, :])
                dve.tensor_copy(heads1["v"][:, :], ps_w[2][:, :]).then_inc(s_done, 1)
                dve.wait_ge(s_done, 14)


class BatchRows:

    def __init__(self, array):
        self.array = array.rearrange("(b i p) c -> b p i c", p=P, i=QT)

    def __getitem__(self, b):
        if isinstance(b, int):
            return self.array[b]
        return self.array[bass.ds(b, 1)].rearrange("b p i c -> p (b i) c")


def transformer(nc, ins, angles, normed, acc, out):
    with ExitStack() as ctx:
        def sbuf(name, shape, dt=F32):
            return ctx.enter_context(nc.sbuf_tensor(name, shape, dt))

        x = sbuf("x_tiles", [P, NT, C])
        ident, identb = sbuf("ident", [P, P]), sbuf("identb", [P, P], BF16)
        mask = sbuf("mask", [P, P], BF16)
        wproj = sbuf("wproj", [C, C])
        cos, sin = sbuf("cos_table", [C, T]), sbuf("sin_table", [C, T])
        heads0, heads1 = [{n: sbuf(f"heads{i}_{n}", [C, C]) for n in ("k", "kr", "q", "qr", "v")} for i in range(2)]
        x_in = ins["L0_attn_x"].rearrange("b t c -> (b t) c")
        out_rows = out.rearrange("b t c -> (b t) c")

        prologue(nc, x, x_in.rearrange("(n p) c -> p n c", p=P), ident, identb, mask, ins["L0_attn_Wqkv"], heads0,
                 [ins["L1_attn_W" + n] for n in "qkv"], heads1, wproj, ins["L0_attn_Wproj"], cos, sin, angles)
        attention(nc, x, BatchRows(x_in), ident, identb, mask, heads0, wproj, cos, sin, True, "a0_")
        dram = {n: ins["L0_ffn_" + n] for n in ("ln_g", "ln_b", "Wr", "W1", "W3", "W2", "W1s", "W3s", "W2s")}
        moe_ffn(nc, x, ident, identb, dict(dram, acc=acc, normed=normed, normed_rows=BatchRows(normed[0:TOKENS, :]).__getitem__),
                "f0_")
        attention(nc, x, None, ident, identb, mask, heads1, None, cos, sin, False, "a1_")
        dense_ffn(nc, x, ident, {n + s: ins["L1_ffn_" + n + s] for n in ("w1", "w2", "h1", "h2", "w3") for s in ("_w", "_s")},
                  BatchRows(out_rows).__getitem__, "f1_")


_INS = ['L0_attn_x', 'L0_attn_Wqkv', 'L0_attn_Wproj', 'L0_ffn_ln_g', 'L0_ffn_ln_b', 'L0_ffn_Wr', 'L0_ffn_W1',
        'L0_ffn_W3', 'L0_ffn_W2', 'L0_ffn_W1s', 'L0_ffn_W3s', 'L0_ffn_W2s', 'L1_attn_Wq', 'L1_attn_Wk', 'L1_attn_Wv',
        'L1_ffn_w1_w', 'L1_ffn_w1_s', 'L1_ffn_w2_w', 'L1_ffn_w2_s', 'L1_ffn_h1_w', 'L1_ffn_h1_s', 'L1_ffn_h2_w',
        'L1_ffn_h2_s', 'L1_ffn_w3_w', 'L1_ffn_w3_s']


def kernel(**inputs):
    import numpy as _np
    import concourse.bacc as _bacc
    from concourse import mybir as _mybir
    from concourse.bass_utils import run_bass_kernel_spmd as _run

    nc = _bacc.Bacc("TRN2", target_bir_lowering=False, num_devices=1)
    arrays, ins = {}, {}

    def put(name, a):
        arrays[f"in_{name}_dram"] = a
        return nc.dram_tensor(f"in_{name}_dram", a.shape, _mybir.dt.from_np(a.dtype), kind="ExternalInput").ap()

    for name in _INS:
        ins[name] = put(name, _np.ascontiguousarray(inputs[name]))
    inv = (1.0 / 10000.0 ** (_np.arange(0, D, 2, dtype=_np.float32) / D)).astype(_np.float32)
    angle = (_np.arange(T, dtype=_np.float32)[:, None] * inv[None, :]).astype(_np.float32)
    angles = [put(name, _np.ascontiguousarray(_np.repeat(fn(angle), 2, axis=-1).T.astype(_np.float32)))
              for name, fn in (("cos", _np.cos), ("sin", _np.sin))]
    out = nc.dram_tensor("out_0_dram", (B, T, C), F32, kind="ExternalOutput").ap()
    normed = nc.dram_tensor("normed_rows_dram", (TOKENS + P, C), F32, kind="Internal").ap()
    acc = nc.dram_tensor("expert_sums_dram", (TOKENS + P, C), F32, kind="Internal").ap()
    transformer(nc, ins, angles, normed, acc, out)
    r = _run(nc, [arrays], core_ids=[0])
    return r.results[0]["out_0_dram"]
```

```python
import concourse.bass as bass
from concourse import mybir
from contextlib import ExitStack

F32 = mybir.dt.float32
BF16 = mybir.dt.bfloat16
ALU = mybir.AluOpType
ACT = mybir.ActivationFunctionType
AX = mybir.AxisListType

P = 128
C = 128
B, T = 8, 512
QT = T // P
NT = B * QT
H, D = 16, 8
HG = 4
NG = H // HG
PARTS = 3
PROD = PARTS * PARTS
ROWS = PROD * D
FULL = 96
VW = 32
EPS = 1e-5
NEWTON = 3


def causal_widths(causal):
    seen_by = [T - P * j if causal else T for j in range(QT)]
    sees = [P * (i + 1) if causal else T for i in range(QT)]
    return seen_by, sees


def by_itself(eng, sem):
    eng.sem_inc(sem, 1)


def layernorm_phase(dve, out, src, stats, mv, rs, tmp, sem, n, past, phase):
    var, y, half, t = (tmp[:, i, :] for i in range(4))
    I32 = mybir.dt.int32
    if phase > 0:
        dve.wait_ge(sem, n * LN_STEPS + LN_DONE[phase - 1])
    if phase < 2:
        by_itself(dve, past)
    if phase == 0:
        for i in range(QT):
            dve.bn_stats(stats[:, i, :], src[:, i, :]).then_inc(sem, 1)
    elif phase == 1:
        for i in range(QT):
            dve.bn_aggr(mv[:, i, :], stats[:, i, :]).then_inc(sem, 1)
    elif phase == 2:
        dve.tensor_scalar(var, mv[:, :, 1], EPS, None, ALU.add).then_inc(sem, 1)
    elif phase == 3:
        dve.tensor_scalar(half, var, -0.5, None, ALU.mult).then_inc(sem, 1)
        dve.tensor_scalar(t.bitcast(I32), var.bitcast(I32), 1, None, ALU.arith_shift_right).then_inc(sem, 1)
    elif phase == 4:
        dve.tensor_scalar(y.bitcast(I32), t.bitcast(I32), -1.0, float(0x5F3759DF), ALU.mult, ALU.add)\
            .then_inc(sem, 1)
    elif phase < 5 + 3 * NEWTON:
        k, part = divmod(phase - 5, 3)
        if part == 0:
            dve.tensor_tensor(t, y, y, ALU.mult).then_inc(sem, 1)
        elif part == 1:
            dve.tensor_tensor(t, t, half, ALU.mult).then_inc(sem, 1)
        else:
            dve.scalar_tensor_tensor(rs[:, :] if k == NEWTON - 1 else y, t, 1.5, y, ALU.add, ALU.mult)\
                .then_inc(sem, 1)
    else:
        for i in range(QT):
            dve.tensor_scalar(out[:, i, :], src[:, i, :], mv[:, i, 0:1], rs[:, i:i + 1],
                              ALU.subtract, ALU.mult).then_inc(sem, 1)


LN_PHASES = 6 + 3 * NEWTON
LN_DONE = [QT, 2 * QT, 2 * QT + 1, 2 * QT + 3, 2 * QT + 4] + [2 * QT + 5 + k for k in range(3 * NEWTON)] + \
          [3 * QT + 4 + 3 * NEWTON]
LN_STEPS = LN_DONE[-1]


def layernorm(dve, out, src, stats, mv, rs, tmp, sem, n, past):
    for phase in range(LN_PHASES):
        layernorm_phase(dve, out, src, stats, mv, rs, tmp, sem, n, past, phase)


def attention(nc, x, x_dram, ident, identb, mask, weights, wproj, cos, sin, causal, tag):
    seen_by, sees = causal_widths(causal)
    unit_heads = [T // w for w in seen_by]
    max_heads = [T // w for w in sees]
    SU = sum(HG // u for u in unit_heads)
    MU = sum(HG // u for u in max_heads)
    SBANKS, MBANKS = 2, 4
    assert NG * SU % SBANKS == 0 and NG * MU % MBANKS == 0
    RING = 4
    LAG = 2
    G = B * NG
    SLOTS = 4
    VALUES_AT = 3
    assert max(MU * (j + 1) // QT - MU * j // QT for j in range(QT)) <= SLOTS

    def jobs(b, g, j, first, last):
        out = []
        if j == 1 and not (last and g == NG - 1):
            out.append("maxT")
        if not last and g == 0:
            out += [["xT"], ["k", "kr"], ["q", "qr"], ["v"]][j]
        if j == 2 and not (first and g == 0):
            out.append("norm")
        if not first:
            out += {(0, 3): ["yT"], (1, 1): ["proj"]}.get((g, j), []) if wproj is not None else []
        assert len(out) < SLOTS
        return out

    START = ["xT", "k", "kr", "q", "qr", "v", "maxT"]
    END = ["norm"] + (["yT", "proj"] if wproj is not None else [])

    def batch_jobs(first, last):
        return [(g, j, name) for g in range(NG) for j in range(QT) for name in jobs(0, g, j, first, last)]

    N0, N1 = len(batch_jobs(True, False)), len(batch_jobs(False, False))

    def jobs_before(b, first):
        return len(START) if first else len(START) + N0 + (b - 1) * N1

    def number(b, first, last, g, name):
        at = [n for n, (gg, _, x) in enumerate(batch_jobs(first, last)) if (gg, x) == (g, name)]
        assert len(at) == 1
        return jobs_before(b, first) + at[0]

    FREED = 2
    ORDER = [("k", 0), ("k", 1), ("q", 0), ("k", 2), ("q", 1), ("q", 2)]
    POOL_AT = {(0, 1): [0], (0, 2): [1, 2], (0, 3): [3, 4], (1, 0): [5]}
    ACT_AT = {(0, 2): [0], (0, 3): [1, 2], (1, 0): [3, 4], (1, 1): [5]}

    with ExitStack() as ctx:
        def psum(name, shape, dt=F32):
            return ctx.enter_context(nc.psum_tensor(tag + name, shape, dt))

        def sbuf(name, shape, dt=F32):
            return ctx.enter_context(nc.sbuf_tensor(tag + name, shape, dt))

        def sem(name):
            return ctx.enter_context(nc.semaphore(tag + name))

        qst = [sbuf(f"qst{i}", [FULL, H, T], BF16) for i in range(2)]
        kst = [sbuf(f"kst{i}", [FULL, H, T], BF16) for i in range(2)]
        vst = [sbuf(f"vst{i}", [P, QT, H, VW]) for i in range(2)]
        prob = [sbuf(f"prob{i}", [P, HG, T]) for i in range(RING)]
        xin = sbuf("xin", [P, QT, C])
        xT = sbuf("xT", [C, T])
        rope = {n: sbuf("rope_" + n, [C, T]) for n in ("k", "kr", "q", "qr")}
        part = {n: sbuf("part_" + n, [C, PARTS, T], BF16) for n in ("k", "q")}
        mx = sbuf("mx", [P, 2, QT, HG])
        rest = sbuf("rest", [P, 2, QT, HG])
        mpart = sbuf("mpart", [P, QT, PARTS, HG], BF16)
        mrow = sbuf("mrow", [PARTS * HG, T], BF16)
        oT = sbuf("oT", [P, T])
        rden = sbuf("rden", [P, QT, HG])
        y = sbuf("y", [P, QT, C])
        yT = sbuf("yT", [C, T]) if wproj is not None else None
        ones = sbuf("ones", [PARTS, T], BF16)
        stats = sbuf("stats", [P, QT, 6])
        mv = sbuf("mv", [P, QT, 2])
        lntmp = sbuf("lntmp", [P, 4, QT])
        rs = sbuf("rs", [P, QT])
        ps_s = [psum(f"ps_s{i}", [P, T]) for i in range(SBANKS)]
        ps_m = [psum(f"ps_m{i}", [P, T]) for i in range(MBANKS)]
        ps_o = psum("ps_o", [P, T])
        ps_x = psum("ps_x", [P, T])

        s_score = sem("score")
        s_score_free = sem("score_free")
        s_max = sem("max")
        s_max_free = sem("max_free")
        s_masked = sem("masked")
        s_pv = sem("pv")
        s_oT = sem("oT")
        s_job = sem("job")
        s_job_free = sem("job_free")
        s_xin = sem("xin")
        s_split = sem("split")
        s_cast = sem("cast")
        s_st = {"k": sem("stack_k"), "q": sem("stack_q")}
        s_mp = sem("mp")
        s_mst = sem("mst")
        s_norm = sem("norm")
        s_ln = sem("ln")
        s_res = sem("res")
        s_init = sem("init")
        s_ones = sem("ones_dma")
        s_passed = sem("passed")
        s_vinit = sem("vinit")

        with nc.Block() as block:
            @block.sync
            def _(sp):
                def load(b, turned):
                    if turned is not None:
                        sp.wait_ge(s_job, turned + 1)
                        by_itself(sp, s_passed)
                    src = x_dram[b] if x_dram is not None else \
                        x[:, bass.ds(QT * b, QT), :] if not isinstance(b, int) else x[:, QT * b:QT * b + QT, :]
                    sp.dma_start(xin[:, :, :], src).then_inc(s_xin, 16)

                load(0, None)
                sp.wait_ge(s_init, 5)
                for i in range(2):
                    sp.dma_start(kst[i][ROWS:ROWS + PARTS, :, :],
                                 ones[:, :].unsqueeze(1).to_broadcast([PARTS, H, T])).then_inc(s_ones, 16)
                sp.wait_ge(s_ones, 32)

                def stacks(b, r, m, wait_scores):
                    name, part_no = ORDER[m]
                    dst = {"k": kst, "q": qst}[name][r]
                    sp.wait_ge(s_cast, b * len(ORDER) + m + 1)
                    by_itself(sp, s_passed)
                    if wait_scores is not None:
                        sp.wait_ge(s_score, wait_scores)
                        by_itself(sp, s_passed)
                    for other in range(PARTS):
                        row = (part_no * PARTS + other if name == "k" else other * PARTS + part_no) * D
                        sp.dma_start(dst[row:row + D, :, :], part[name][:, part_no, :]).then_inc(s_st[name], 16)

                def max_rows(turned, r, g):
                    sp.wait_ge(s_job_free, turned + FREED)
                    sp.dma_start(qst[r][ROWS:ROWS + PARTS, HG * g:HG * g + HG, :],
                                 mrow[:, :]).then_inc(s_mst, 16)

                def batch(b, r, first=False, last=False, before_last=False):
                    for g in range(NG):
                        if g == NG - 1 and not last and not before_last:
                            load(b + 2, number(b, first, last, 0, "xT"))
                        if g < NG - 1:
                            max_rows(number(b, first, last, g, "maxT"), r, g + 1)
                        elif not last:
                            max_rows(number(b, first, last, g, "maxT"), 1 - r, 0)
                        if g < 2 and not last:
                            for m in range(5) if g == 0 else [5]:
                                stacks(b + 1, 1 - r, m, None if first or m else b * (NG * SU))

                for m in range(len(ORDER)):
                    stacks(0, 0, m, None)
                load(1, 0)
                max_rows(len(START) - 1, 0, 0)
                batch(0, 0, first=True)
                with sp.Fori(0, B // 2 - 2) as it:
                    batch(2 * it + 1, 1)
                    batch(2 * it + 2, 0)
                batch(B - 3, 1)
                batch(B - 2, 0, before_last=True)
                batch(B - 1, 1, last=True)

            @block.gpsimd
            def _(pool):
                for st in (*qst, *kst):
                    pool.memset(st[64:FULL, :, :], 0.0).then_inc(s_init, 1)
                pool.wait_ge(s_init, 4)
                pool.memset(ones[:, :], 1.0).then_inc(s_init, 1)
                pool.wait_ge(s_init, 5)

                def left(b, m, turned):
                    name, part_no = ORDER[m]
                    s, t = rope[name], rope[name + "r"]
                    if part_no == 0:
                        pool.wait_ge(s_job_free, turned + FREED)
                        pool.tensor_tensor(s[:, :], s[:, :], t[:, :], ALU.add).then_inc(s_split, 1)
                    else:
                        pool.wait_ge(s_cast, b * len(ORDER) + ORDER.index((name, part_no - 1)) + 1)
                        pool.tensor_tensor(s[:, :], s[:, :], part[name][:, part_no - 1, :], ALU.subtract)\
                            .then_inc(s_split, 1)

                def batch(b, r, first=False, last=False):
                    for g in range(NG):
                        for j in range(QT):
                            if causal:
                                u0 = sum(HG // u for u in unit_heads[:j + 1])
                                pool.wait_ge(s_score_free, b * (NG * SU) + g * SU + u0 + SBANKS)
                                by_itself(pool, s_passed)
                                diag = prob[j % RING][:, :, 0:P]
                                pool.affine_select(out=diag, in_=diag, compare_op=ALU.is_ge, fill=0.0,
                                                   base=0, pattern=[[0, HG], [1, P]],
                                                   channel_multiplier=-1).then_inc(s_masked, 1)
                            for m in POOL_AT.get((g, j), []) if not last else []:
                                left(b + 1, m, number(b, first, last, 0, ORDER[m][0] + "r"))

                for m in range(len(ORDER)):
                    left(0, m, START.index(ORDER[m][0] + "r"))
                batch(0, 0, first=True)
                with pool.Fori(0, B // 2 - 1) as it:
                    batch(2 * it + 1, 1)
                    batch(2 * it + 2, 0)
                batch(B - 1, 1, last=True)

            @block.scalar
            def _(act):
                act.sem_inc(s_score_free, SBANKS)

                def job(name, b, r, n, count):
                    act.wait_ge(s_job, n + 1)
                    if name == "maxT" and count is not None:
                        act.wait_ge(s_mst, count * 16)
                    if name == "xT":
                        ins = act.activation(xT[:, :], ps_x[:, :], ACT.Copy)
                    elif name == "v":
                        ins = act.activation(vst[r][:, :, :, 0:D],
                                             ps_x[:, :].rearrange("p (t h d) -> p t h d", t=QT, h=H), ACT.Copy)
                    elif name == "maxT":
                        ins = act.activation(mrow[:, :], ps_x[0:PARTS * HG, 0:T // 2].bitcast(BF16), ACT.Copy)
                    elif name == "yT":
                        ins = act.activation(yT[:, :], ps_x[:, :], ACT.Copy)
                    ins.then_inc(s_job_free, 1)

                def batch(b, r, first=False, last=False):
                    k = 0
                    for g in range(NG):
                        for j in range(QT):
                            u0 = sum(HG // u for u in unit_heads[:j])
                            w = seen_by[j]
                            names = jobs(0, g, j, first, last)
                            for slot in range(SLOTS):
                                if slot < HG // unit_heads[j]:
                                    nu, h = unit_heads[j], slot * unit_heads[j]
                                    act.wait_ge(s_score, b * (NG * SU) + g * SU + u0 + slot + 1)
                                    if slot == 0 and not (first and g == 0):
                                        act.wait_ge(s_pv, b * (NG * QT) + g * QT + j - RING + 1)
                                    act.activation(prob[j % RING][:, h:h + nu, 0:w],
                                                   ps_s[(g * SU + u0 + slot) % SBANKS][:, 0:nu * w]
                                                   .rearrange("p (h t) -> p h t", h=nu), ACT.Exp,
                                                   scale=float(D) ** -0.5).then_inc(s_score_free, 1)
                                if slot == SLOTS - 1 and j == 1 and not (first and g == 0):
                                    out_evac(b * NG + g - 1, number(b, first, last, g - 1, "norm") if g > 0 and not (first and g == 1)
                                             else None if first else jobs_before(b, first) - 1)
                                if 0 < slot <= len(names):
                                    name, n = names[slot - 1], jobs_before(b, first) + k
                                    k += 1
                                    if name in ("xT", "v"):
                                        job(name, b + 1, 1 - r, n, None)
                                    elif name == "maxT":
                                        job(name, None, None, n, b * NG + g + 1)
                                    elif name == "yT":
                                        job(name, b - 1, None, n, None)
                            for m in ACT_AT.get((g, j), []) if not last else []:
                                cast(b + 1, m)

                def cast(b, m):
                    name, part_no = ORDER[m]
                    if not (isinstance(b, int) and b == 0):
                        act.wait_ge(s_st[name], b * (PROD * 16))
                    act.wait_ge(s_split, b * len(ORDER) + m + 1)
                    act.activation(part[name][:, part_no, :], rope[name][:, :], ACT.Copy).then_inc(s_cast, 1)

                def out_evac(n, turned):
                    act.wait_ge(s_pv, n * QT + QT)
                    if turned is not None:
                        act.wait_ge(s_job, turned + 1)
                    act.activation(oT[:, :], ps_o[:, :], ACT.Copy).then_inc(s_oT, 1)

                for n, name in enumerate(START):
                    if name in ("xT", "v"):
                        job(name, 0, 0, n, None)
                    elif name == "maxT":
                        for m in range(len(ORDER)):
                            cast(0, m)
                        job(name, None, None, n, None)
                batch(0, 0, first=True)
                with act.Fori(0, B // 2 - 1) as it:
                    batch(2 * it + 1, 1)
                    batch(2 * it + 2, 0)
                batch(B - 1, 1, last=True)
                out_evac(G - 1, number(B - 1, False, True, NG - 1, "norm"))
                if wproj is not None:
                    job("yT", B - 1, None, jobs_before(B - 1, False) + len(batch_jobs(False, True)) + 1, None)

            @block.tensor
            def _(pe):
                def job(name, b, r, n, count):
                    pe.wait_ge(s_job_free, n + 1)
                    if name == "xT":
                        pe.wait_ge(s_xin, (b + 1) * 16)
                        for i in range(QT):
                            last = pe.transpose(ps_x[:, P * i:P * i + P], xin[:, i, :], ident[:, :])
                    elif name in ("k", "kr", "q", "qr"):
                        last = pe.matmul(ps_x[:, :], weights[name][:, :], xT[:, :], start=True, stop=True)
                    elif name == "v":
                        for i in range(QT):
                            last = pe.matmul(ps_x[:, P * i:P * i + P], xT[:, P * i:P * i + P], weights["v"][:, :],
                                             start=True, stop=True)
                    elif name == "maxT":
                        pe.wait_ge(s_mp, (count + 1) * MP_STEPS)
                        for i in range(QT):
                            last = pe.transpose(ps_x[0:PARTS * HG, 0:T // 2].bitcast(BF16)[:, P * i:P * i + P],
                                                mpart[:, i, :, :].rearrange("p a h -> p (a h)"), identb[:, :])
                    elif name == "norm":
                        pe.wait_ge(s_oT, count + 1)
                        for i in range(QT):
                            last = pe.transpose(ps_x[:, P * i:P * i + P], oT[:, P * i:P * i + P], ident[:, :])
                    elif name == "yT":
                        for i in range(QT):
                            last = pe.transpose(ps_x[:, P * i:P * i + P], y[:, i, :], ident[:, :])
                    elif name == "proj":
                        for i in range(QT):
                            last = pe.matmul(ps_x[:, P * i:P * i + P], yT[:, P * i:P * i + P], wproj[:, :],
                                             start=True, stop=True)
                    last.then_inc(s_job, 1)

                def maxima(n, r, g, lo, hi):
                    unit = 0
                    for i in range(QT):
                        w = sees[i]
                        for u in range(HG // max_heads[i]):
                            if lo <= unit < hi:
                                pe.wait_ge(s_max_free, n * MU + unit + 1)
                                bank = ps_m[(unit + g * MU) % MBANKS]
                                mh = max_heads[i]
                                for v in range(mh):
                                    h = HG * g + u * mh + v
                                    last = pe.matmul(bank[:, v * w:v * w + w], qst[r][0:ROWS, h, P * i:P * i + P],
                                                     kst[r][0:ROWS, h, 0:w], start=True, stop=not causal)
                                    if causal:
                                        last = pe.matmul(bank[:, v * w + w - P:v * w + w], identb[:, :], mask[:, :],
                                                         start=False, stop=True)
                                last.then_inc(s_max, 1)
                            unit += 1

                def scores(b, r, g, j, u):
                    u0 = sum(HG // u for u in unit_heads[:j])
                    w, nu = seen_by[j], unit_heads[j]
                    pe.wait_ge(s_score_free, b * (NG * SU) + g * SU + u0 + u + 1)
                    pbank = ps_s[(g * SU + u0 + u) % SBANKS]
                    for v in range(nu):
                        h = HG * g + u * nu + v
                        last = pe.matmul(pbank[:, v * w:v * w + w], kst[r][:, h, P * j:P * j + P], qst[r][:, h, T - w:T],
                                         start=True, stop=True)
                    last.then_inc(s_score, 1)

                def values(b, r, g, j):
                    n = b * NG + g
                    if causal:
                        pe.wait_ge(s_masked, n * QT + j + 1)
                    else:
                        u0 = sum(HG // u for u in unit_heads[:j + 1])
                        pe.wait_ge(s_score_free, n * SU + u0 + SBANKS)
                    if j == 0:
                        pe.wait_ge(s_oT, n) if not (isinstance(n, int) and n == 0) else None
                    w = seen_by[j]
                    for h in range(HG):
                        last = pe.matmul(ps_o[VW * h:VW * h + VW, T - w:T], vst[r][:, j, HG * g + h, :],
                                         prob[j % RING][:, h, 0:w], start=(j == 0), stop=(j == QT - 1))
                    last.then_inc(s_pv, 1)

                def batch(b, r, first=False, last=False):
                    k = 0
                    for g in range(NG):
                        for j in range(QT):
                            if j == 0:
                                pe.wait_ge(s_mst, (b * NG + g + 1) * 16)
                            names = jobs(0, g, j, first, last)
                            lo, hi = MU * j // QT, MU * (j + 1) // QT
                            for slot in range(SLOTS):
                                if slot < HG // unit_heads[j]:
                                    scores(b, r, g, j, slot)
                                if (g < NG - 2 or not last) and lo + slot < hi:
                                    if (g, j, slot) == (NG - 2, 0, 0):
                                        for stack in s_st.values():
                                            pe.wait_ge(stack, (b + 2) * (PROD * 16))
                                    if g < NG - 2:
                                        maxima(b * NG + g + 2, r, g + 2, lo + slot, lo + slot + 1)
                                    else:
                                        maxima(b * NG + g + 2, 1 - r, g + 2 - NG, lo + slot, lo + slot + 1)
                                if slot == VALUES_AT:
                                    g2, j2 = (g, j - LAG) if j >= LAG else (g - 1, j - LAG + QT)
                                    if g2 >= 0:
                                        values(b, r, g2, j2)
                                    elif not first:
                                        values(b - 1, 1 - r, NG - 1, j2)
                                if 0 < slot <= len(names):
                                    name, n = names[slot - 1], jobs_before(b, first) + k
                                    k += 1
                                    if name in ("xT", "k", "kr", "q", "qr", "v"):
                                        job(name, b + 1, 1 - r, n, None)
                                    elif name == "maxT":
                                        job(name, None, None, n, b * NG + g + 1)
                                    elif name == "norm":
                                        job(name, None, None, n, b * NG + g - 1)
                                    else:
                                        job(name, b - 1, 1 - r, n, None)

                pe.wait_ge(s_vinit, 4)
                for n, name in enumerate(START[:-1]):
                    job(name, 0, 0, n, None)
                for stack in s_st.values():
                    pe.wait_ge(stack, PROD * 16)
                pe.wait_ge(s_ones, 32)
                maxima(0, 0, 0, 0, MU)
                maxima(1, 0, 1, 0, MU)
                job("maxT", None, None, len(START) - 1, 0)
                batch(0, 0, first=True)
                with pe.Fori(0, B // 2 - 1) as it:
                    batch(2 * it + 1, 1)
                    batch(2 * it + 2, 0)
                batch(B - 1, 1, last=True)
                for j in range(QT - LAG, QT):
                    values(B - 1, 1, NG - 1, j)
                n = jobs_before(B - 1, False) + len(batch_jobs(False, True))
                job("norm", None, None, n, G - 1)
                if wproj is not None:
                    job("yT", B - 1, 1, n + 1, None)
                    job("proj", B - 1, 1, n + 2, None)

            @block.vector
            def _(dve):
                dve.sem_inc(s_max_free, MBANKS)
                dve.sem_inc(s_job_free, 1)
                for i in range(2):
                    dve.memset(vst[i][:, :, :, D + 1:VW], 0.0).then_inc(s_vinit, 1)
                    dve.memset(vst[i][:, :, :, D:D + 1], 1.0).then_inc(s_vinit, 1)

                def job(name, b, r, n, count):
                    dve.wait_ge(s_job, n + 1)
                    if name in ("k", "kr", "q", "qr"):
                        if not (isinstance(b, int) and b == 0):
                            dve.wait_ge(s_cast, (b - 1) * len(ORDER) + ORDER.index((name[0], PARTS - 1)) + 1)
                        dve.tensor_tensor(rope[name][:, :], ps_x[:, :], (sin if name[-1] == "r" else cos)[:, :],
                                          ALU.mult).then_inc(s_job_free, 1)
                    elif name == "proj":
                        residual(b, ps_x[:, :].rearrange("p (i c) -> p i c", i=QT), n)

                def xb(b):
                    return x[:, QT * b:QT * b + QT, :] if isinstance(b, int) else x[:, bass.ds(QT * b, QT), :]

                def residual(b, add, shared):
                    done, count = (s_res, b + 1) if shared is None else (s_job_free, shared + FREED)
                    dve.tensor_tensor(xb(b), xb(b), add, ALU.add).then_inc(done, 1)
                    dve.wait_ge(done, count)

                def ln_phase(b, phase):
                    layernorm_phase(dve, xb(b), xb(b), stats, mv, rs, lntmp, s_ln, b, s_passed, phase)

                def reduce_units(n, g, lo, hi):
                    unit = 0
                    for i in range(QT):
                        w = sees[i]
                        for u in range(HG // max_heads[i]):
                            if lo <= unit < hi:
                                mh = max_heads[i]
                                dve.wait_ge(s_max, n * MU + unit + 1)
                                dve.reduce_max(mx[:, g % 2, i, u * mh:u * mh + mh],
                                               ps_m[(unit + g * MU) % MBANKS][:, 0:mh * w]
                                               .rearrange("p (h t) -> p h t", h=mh), AX.X)\
                                    .then_inc(s_max_free, 1)
                            unit += 1

                def split_max(n, g, step, turned=None):
                    left = [mx[:, g % 2, :, :], rest[:, 0, :, :], rest[:, 1, :, :]]
                    if step == 0:
                        dve.wait_ge(s_max_free, (n + 1) * MU + MBANKS)
                        if turned is not None:
                            dve.wait_ge(s_job, turned + 1)
                    else:
                        dve.wait_ge(s_mp, n * MP_STEPS + step)
                    i = step // 2
                    if step % 2 == 0:
                        dve.tensor_scalar(mpart[:, :, i, :], left[i], -1.0, None, ALU.mult).then_inc(s_mp, 1)
                    else:
                        dve.tensor_tensor(left[i + 1], left[i], mpart[:, :, i, :], ALU.add).then_inc(s_mp, 1)

                def batch(b, r, first=False, last=False):
                    k = 0
                    ln_slot = None
                    for g in range(NG):
                        for j in range(QT):
                            names = jobs(0, g, j, first, last)
                            lo, hi = MU * j // QT, MU * (j + 1) // QT
                            for slot in range(SLOTS):
                                taken = g < NG - 2 or not last
                                if taken and lo + slot < hi:
                                    reduce_units(b * NG + g + 2, (g + 2) % NG, lo + slot, lo + slot + 1)
                                    if lo + slot == MU - 1:
                                        dve.wait_ge(s_job, number(b, first, last, g, "maxT") + 1)
                                if j == 0 and not (first and g == 0) and not (last and g > NG - 2):
                                    for step in [slot] if slot < SLOTS - 1 else range(slot, MP_STEPS):
                                        split_max(b * NG + g + 1, (g + 1) % NG, step)
                                if ln_slot is not None and ln_slot < LN_PHASES:
                                    ln_phase(b - 1, ln_slot)
                                    ln_slot += 1
                                if 0 < slot <= len(names):
                                    name, n = names[slot - 1], jobs_before(b, first) + k
                                    k += 1
                                    if name in ("k", "kr", "q", "qr"):
                                        job(name, b + 1, None, n, None)
                                    elif name == "norm":
                                        norm_job(n, b, g - 1, first)
                                    elif name == "proj":
                                        job(name, b - 1, None, n, None)
                                    if name == "proj" or (name == "norm" and g == 0 and wproj is None):
                                        ln_slot = 0

                def norm_job(n, b, g, first):
                    count = b * NG + g
                    bb, gg = (b, g) if g >= 0 else (b - 1, NG - 1)
                    heads = ps_x[:, :].rearrange("p (i h v) -> p i h v", i=QT, h=HG)
                    dve.wait_ge(s_job, n + 1)
                    dve.reciprocal(rden[:, :, :], heads[:, :, :, D]).then_inc(s_norm, 1)
                    dve.wait_ge(s_norm, count + 1)
                    dve.tensor_tensor(y[:, :, gg * HG * D:(gg + 1) * HG * D].rearrange("p i (h d) -> p i h d", h=HG),
                                      heads[:, :, :, 0:D],
                                      rden[:, :, :].unsqueeze(3).to_broadcast([P, QT, HG, D]),
                                      ALU.mult).then_inc(s_job_free, 1)
                    if gg == NG - 1 and wproj is None:
                        dve.wait_ge(s_job_free, n + FREED)
                        residual(bb, y[:, :, :], None)

                for n, name in enumerate(START[:-1]):
                    if name in ("k", "kr", "q", "qr"):
                        job(name, 0, None, n, None)
                reduce_units(0, 0, 0, MU)
                for step in range(MP_STEPS):
                    split_max(0, 0, step)
                reduce_units(1, 1, 0, MU)
                for step in range(MP_STEPS):
                    split_max(1, 1, step, len(START) - 1)
                batch(0, 0, first=True)
                with dve.Fori(0, B // 2 - 1) as it:
                    batch(2 * it + 1, 1)
                    batch(2 * it + 2, 0)
                batch(B - 1, 1, last=True)
                n = jobs_before(B - 1, False) + len(batch_jobs(False, True))
                norm_job(n, B - 1, NG - 1, False)
                if wproj is not None:
                    job("proj", B - 1, None, n + 2, None)
                for phase in range(LN_PHASES):
                    ln_phase(B - 1, phase)


MP_STEPS = 5


I32 = mybir.dt.int32
FF = 512
FB = FF // P
E = 7
CAPACITY = 366
ET = 3
SLOTS = ET * P
ST = E * ET
TOP = 2
TC = TOP * NT
TOKENS = NT * P
PAY = 3 + PARTS
BEFORE = 6


def moe_ffn(nc, x, ident, identb, dram, tag="f0"):
    with ExitStack() as ctx:
        def psum(name, shape, dt=F32):
            return ctx.enter_context(nc.psum_tensor(tag + name, shape, dt))

        def sbuf(name, shape, dt=F32):
            return ctx.enter_context(nc.sbuf_tensor(tag + name, shape, dt))

        def sem(name):
            return ctx.enter_context(nc.semaphore(tag + name))

        nrm = [sbuf(f"nrm{i}", [P, QT, C]) for i in range(2)]
        hT = sbuf("hT", [C, TOKENS])
        ln_g = sbuf("ln_g", [C, 1])
        ln_b = sbuf("ln_b", [C, 1])
        wr = sbuf("wr", [C, E])
        w1 = [sbuf(f"w1_{i}", [C, FF]) for i in range(2)]
        w3 = [sbuf(f"w3_{i}", [C, FF]) for i in range(2)]
        w2 = [sbuf(f"w2_{i}", [P, FB, C]) for i in range(2)]
        w1s, w3s, w2s = sbuf("w1s", [C, FF]), sbuf("w3s", [C, FF]), sbuf("w2s", [P, FB, C])
        lgT = sbuf("lgT", [E, T])
        logit = sbuf("logit", [P, NT, E])
        stats, mv = sbuf("stats", [P, QT, 6]), sbuf("mv", [P, QT, 2])
        lntmp, rs = sbuf("lntmp", [P, 4, QT]), sbuf("rs", [P, QT])
        gatea = [sbuf(f"gatea{i}", [P, T]) for i in range(2)]
        copyb = [sbuf(f"copyb{i}", [P, T]) for i in range(2)]
        hid = sbuf("hid", [P, FB, T])
        sharedT = sbuf("sharedT", [C, TOKENS])
        routed = [sbuf(f"routed{i}", [P, QT, C]) for i in range(2)]
        iota_e = sbuf("iota_e", [P, E])
        iota_lo = sbuf("iota_lo", [P, P])
        iota_hi = sbuf("iota_hi", [P, ST])
        iota_t = sbuf("iota_t", [P, NT])
        iota_p = sbuf("iota_p", [P, 1])
        tri = sbuf("tri", [P, P], BF16)
        onesb = sbuf("onesb", [P, P], BF16)
        top = sbuf("top", [P, TOP, NT])
        hot = sbuf("hot", [P, TOP, NT, E])
        hotb = sbuf("hotb", [P, TOP, NT, E], BF16)
        wk = [sbuf(f"wk{i}", [P, TOP, NT, E]) for i in range(3)]
        expert = sbuf("expert", [P, TOP, NT])
        gate = sbuf("gate", [P, TOP, NT])
        grest = [sbuf(f"grest{i}", [P, TOP, NT]) for i in range(2)]
        gpart = sbuf("gpart", [P, PARTS, TOP, NT], BF16)
        small = [sbuf(f"small{i}", [P, TC]) for i in range(4)]
        smalli = [sbuf(f"smalli{i}", [P, TC], I32) for i in range(3)]
        lohot = sbuf("lohot", [P, TC, P], BF16)
        pay = sbuf("pay", [P, TC, PAY, ST], BF16)
        slot = sbuf("slot", [P, PAY, ST])
        sgate = sbuf("sgate", [P, ST])
        stmp = [sbuf(f"stmp{i}", [P, ST]) for i in range(3)]
        token = sbuf("token", [P, ST], I32)
        xg = [sbuf(f"xg{i}", [P, ET, C]) for i in range(2)]
        xeT = [sbuf(f"xeT{i}", [C, SLOTS]) for i in range(2)]
        yeT = sbuf("yeT", [C, SLOTS])
        ye = [sbuf(f"ye{i}", [P, ET, C]) for i in range(2)]
        zero = sbuf("zero", [P, C])
        ps_a = [psum(f"ps_a{i}", [P, T]) for i in range(2)]
        ps_b = [psum(f"ps_b{i}", [P, T]) for i in range(2)]
        ps_y = psum("ps_y", [P, T])
        ps_t = psum("ps_t", [P, T])
        ps_r = psum("ps_r", [P, T])
        ps_r2 = psum("ps_r2", [P, T])

        s_w = sem("w")
        s_we = [sem(f"we{i}") for i in range(2)]
        s_ln = sem("ln")
        s_nout = [sem(f"nout{i}") for i in range(2)]
        s_nT = sem("nT")
        s_hT = sem("hT")
        s_lgT = sem("lgT")
        s_lgc = sem("lgc")
        s_lg = sem("lg")
        s_lge = sem("lge")
        s_const = sem("const")
        s_zero = sem("zero")
        s_rt = sem("rt")
        s_exp = sem("exp")
        s_cnt = sem("cnt")
        s_map = sem("map")
        s_up = sem("up")
        s_gate = sem("gate")
        s_hid = sem("hid")
        s_down = sem("down")
        s_y = sem("y")
        s_gath = [sem(f"gath{i}") for i in range(2)]
        s_xgT = sem("xgT")
        s_xe = sem("xe")
        s_yeT = sem("yeT")
        s_ye = sem("ye")
        s_scat = sem("scat")
        s_sT = sem("sT")
        s_acc = [sem(f"acc{i}") for i in range(2)]
        s_sum = sem("sum")
        s_passed = sem("passed")

        CONSTS = 9
        U_EXP = BEFORE * FB
        U_END = U_EXP + E * FB
        UNITS = U_END + (B - BEFORE) * FB

        with nc.Block() as block:
            @block.sync
            def _(sp):
                for dst, src in ((ln_g[:, :], dram["ln_g"].rearrange("(c a) -> c a", a=1)),
                                 (ln_b[:, :], dram["ln_b"].rearrange("(c a) -> c a", a=1)),
                                 (wr[:, :], dram["Wr"]), (w1s[:, :], dram["W1s"]), (w3s[:, :], dram["W3s"]),
                                 (w2s[:, :, :], dram["W2s"].rearrange("(k p) d -> p k d", p=P))):
                    sp.dma_start(dst, src).then_inc(s_w, 16)

                def expert_weights(e, r):
                    sp.dma_start(w1[r][:, :], dram["W1"][e]).then_inc(s_we[r], 16)
                    sp.dma_start(w3[r][:, :], dram["W3"][e]).then_inc(s_we[r], 16)
                    sp.dma_start(w2[r][:, :, :], dram["W2"][e].rearrange("(k p) d -> p k d", p=P)).then_inc(s_we[r], 16)

                for e in range(2):
                    expert_weights(e, e)
                sp.wait_ge(s_const, 1)
                n_acc = TOKENS // P + 1
                sp.dma_start(dram["acc"].rearrange("(n p) c -> p n c", p=P),
                             zero[:, :].unsqueeze(1).to_broadcast([P, n_acc, C])).then_inc(s_zero, 16)
                sp.dma_start(dram["normed"][TOKENS:TOKENS + P, :], zero[:, :]).then_inc(s_zero, 16)

                def rows_out(c, r):
                    sp.wait_ge(s_ln, (c + 1) * LN_STEPS)
                    by_itself(sp, s_passed)
                    sp.dma_start(dram["normed_rows"](c), nrm[r][:, :, :]).then_inc(s_nout[r], 16)

                with sp.Fori(0, B // 2) as it:
                    rows_out(2 * it, 0)
                    rows_out(2 * it + 1, 1)
                for e in range(2, E):
                    sp.wait_ge(s_down, U_EXP + (e - 1) * FB)
                    expert_weights(e, e % 2)
                sp.wait_ge(s_scat, ST * 16)
                for c in range(B):
                    if c >= 2:
                        sp.wait_ge(s_sum, 2 * (c - 1))
                    sp.dma_start(routed[c % 2][:, :, :],
                                 dram["acc"][c * T:(c + 1) * T, :].rearrange("(i p) c -> p i c", p=P)).then_inc(s_acc[c % 2], 16)

            @block.gpsimd
            def _(pool):
                steps = [0]

                def const(ins):
                    steps[0] += 1
                    ins.then_inc(s_const, 1)

                const(pool.memset(zero[:, :], 0.0))
                const(pool.memset(tri[:, :], 1.0))
                const(pool.memset(onesb[:, :], 1.0))
                pool.wait_ge(s_const, steps[0])
                const(pool.affine_select(out=tri[:, :], in_=tri[:, :], compare_op=ALU.is_ge, fill=0.0, base=0,
                                         pattern=[[1, P]], channel_multiplier=-1))
                for dst, n in ((iota_e, E), (iota_lo, P), (iota_hi, ST), (iota_t, NT)):
                    const(pool.iota(dst[:, :], pattern=[[1, n]], base=0, channel_multiplier=0,
                                    allow_small_or_imprecise_dtypes=True))
                const(pool.iota(iota_p[:, :], pattern=[[1, 1]], base=0, channel_multiplier=1,
                                allow_small_or_imprecise_dtypes=True))
                assert steps[0] == CONSTS

                def product(u, f):
                    pool.wait_ge(s_gate, u + 1)
                    by_itself(pool, s_passed)
                    if not (isinstance(u, int) and u < FB):
                        pool.wait_ge(s_down, u - FB + 1)
                    pool.tensor_tensor(hid[:, f, :], gatea[f % 2][:, :], copyb[f % 2][:, :], ALU.mult)\
                        .then_inc(s_hid, 1)

                for f in range(FB):
                    product(f, f)
                with pool.Fori(1, BEFORE) as c:
                    for f in range(FB):
                        product(c * FB + f, f)
                pool.wait_ge(s_rt, RT_STEPS)
                for stored in s_nout:
                    pool.wait_ge(stored, B // 2 * 16)
                pool.wait_ge(s_zero, 32)

                def gather(e):
                    if e >= 2:
                        pool.wait_ge(s_xgT, e - 1)
                    for i in range(ET):
                        k = e * ET + i
                        pool.indirect_dma_start(xg[e % 2][:, i, :], None, dram["normed"],
                                                bass.IndirectOffsetOnAxis(ap=token[:, k:k + 1], axis=0))\
                            .then_inc(s_gath[e % 2], 16)

                def scatter(e):
                    pool.wait_ge(s_ye, e + 1)
                    for i in range(ET):
                        k = e * ET + i
                        if k:
                            pool.wait_ge(s_scat, k * 16)
                        pool.indirect_dma_start(dram["acc"],
                                                bass.IndirectOffsetOnAxis(ap=token[:, k:k + 1], axis=0),
                                                ye[e % 2][:, i, :], None, compute_op=ALU.add).then_inc(s_scat, 16)

                gather(0)
                gather(1)
                for e in range(E):
                    if e + 2 < E:
                        gather(e + 2)
                    scatter(e)

            @block.scalar
            def _(act):
                act.wait_ge(s_w, 6 * 16)

                def prepare(c):
                    act.wait_ge(s_nT, c + 1)
                    act.activation(hT[:, bass.ds(c * T, T)], ps_t[:, :], ACT.Identity, scale=ln_g[:, 0:1],
                                   bias=ln_b[:, 0:1]).then_inc(s_hT, 1)
                    act.wait_ge(s_lgT, c + 1)
                    act.activation(lgT[:, :], ps_r[0:E, :], ACT.Copy).then_inc(s_lgc, 1)
                    act.wait_ge(s_lg, c + 1)
                    act.activation(logit[:, bass.ds(c * QT, QT), :],
                                   ps_r2[:, 0:QT * E].rearrange("p (i e) -> p i e", i=QT), ACT.Copy)\
                        .then_inc(s_lge, 1)

                def unit(u, f, w, both):
                    act.wait_ge(s_up, u + 1)
                    if not (isinstance(u, int) and u < 2):
                        act.wait_ge(s_hid, u - 1)
                    if both:
                        act.activation(copyb[f % 2][:, 0:w], ps_b[f % 2][:, 0:w], ACT.Copy).then_inc(s_passed, 1)
                    act.activation(gatea[f % 2][:, 0:w], ps_a[f % 2][:, 0:w], ACT.Silu).then_inc(s_gate, 1)

                def shared_out(c, n):
                    act.wait_ge(s_down, n)
                    act.activation(sharedT[:, bass.ds(c * T, T)], ps_y[:, :], ACT.Copy).then_inc(s_y, 1)

                prepare(0)
                prepare(1)
                for f in range(FB):
                    unit(f, f, T, True)
                shared_out(0, FB)
                with act.Fori(1, B // 2) as c:
                    prepare(2 * c)
                    prepare(2 * c + 1)
                    for f in range(FB):
                        unit(c * FB + f, f, T, True)
                    shared_out(c, (c + 1) * FB)
                act.wait_ge(s_rt, RT_DIFF)
                act.activation(gate[:, 1, :], small[0][:, 0:NT], ACT.Exp).then_inc(s_exp, 1)
                with act.Fori(B // 2, BEFORE) as c:
                    for f in range(FB):
                        unit(c * FB + f, f, T, True)
                    shared_out(c, (c + 1) * FB)

                def rows(e, r):
                    act.wait_ge(s_xgT, e + 1)
                    act.activation(xeT[r][:, :], ps_t[:, 0:SLOTS], ACT.Identity, scale=ln_g[:, 0:1],
                                   bias=ln_b[:, 0:1]).then_inc(s_xe, 1)

                def expert_out(e):
                    act.wait_ge(s_down, U_EXP + (e + 1) * FB)
                    if not (isinstance(e, int) and e == 0):
                        act.wait_ge(s_yeT, e)
                    act.activation(yeT[:, :], ps_y[:, 0:SLOTS], ACT.Copy).then_inc(s_y, 1)

                def expert(e, r, last=False):
                    for f in range(FB):
                        unit(U_EXP + e * FB + f, f, SLOTS, False)
                        if f == 1 and not last:
                            rows(e + 1, 1 - r)
                    expert_out(e)

                rows(0, 0)
                expert(0, 0)
                with act.Fori(0, (E - 1) // 2 - 1) as it:
                    expert(2 * it + 1, 1)
                    expert(2 * it + 2, 0)
                expert(E - 2, 1)
                expert(E - 1, 0, last=True)
                with act.Fori(BEFORE, B) as c:
                    for f in range(FB):
                        unit(E * FB + c * FB + f, f, T, False)
                    shared_out(c, (c + 1) * FB + E * FB)

            @block.tensor
            def _(pe):
                pe.wait_ge(s_w, 6 * 16)

                def prepare(c, r):
                    pe.wait_ge(s_ln, (c + 1) * LN_STEPS)
                    if not (isinstance(c, int) and c == 0):
                        pe.wait_ge(s_hT, c)
                    for i in range(QT):
                        last = pe.transpose(ps_t[:, P * i:P * i + P], nrm[r][:, i, :], ident[:, :])
                    last.then_inc(s_nT, 1)
                    pe.wait_ge(s_hT, c + 1)
                    if not (isinstance(c, int) and c == 0):
                        pe.wait_ge(s_lgc, c)
                    pe.matmul(ps_r[0:E, :], wr[:, :], hT[:, bass.ds(c * T, T)], start=True, stop=True)\
                        .then_inc(s_lgT, 1)
                    pe.wait_ge(s_lgc, c + 1)
                    if not (isinstance(c, int) and c == 0):
                        pe.wait_ge(s_lge, c)
                    by_itself(pe, s_passed)
                    for i in range(QT):
                        last = pe.transpose(ps_r2[:, E * i:E * i + E], lgT[:, P * i:P * i + P], ident[0:E, 0:E])
                    last.then_inc(s_lg, 1)

                def up(u, f, wa, wb, rhs, w):
                    if not (isinstance(u, int) and u < 2):
                        pe.wait_ge(s_hid, u - 1)
                    pe.matmul(ps_a[f % 2][:, 0:w], wa[:, P * f:P * f + P], rhs, start=True, stop=True)
                    pe.matmul(ps_b[f % 2][:, 0:w], wb[:, P * f:P * f + P], rhs, start=True, stop=True)\
                        .then_inc(s_up, 1)

                def down(u, f, wd, w, outs):
                    pe.wait_ge(s_hid, u + 1)
                    if f == 0 and not (isinstance(outs, int) and outs == 0):
                        pe.wait_ge(s_y, outs)
                    pe.matmul(ps_y[:, 0:w], wd[:, f, :], hid[:, f, 0:w], start=(f == 0), stop=(f == FB - 1))\
                        .then_inc(s_down, 1)

                def shared(c, u, outs):
                    rhs = hT[:, bass.ds(c * T, T)]
                    for f in range(FB):
                        up(u + f, f, w1s, w3s, rhs, T)
                        if f:
                            down(u + f - 1, f - 1, w2s, T, outs)
                    down(u + FB - 1, FB - 1, w2s, T, outs)

                prepare(0, 0)
                prepare(1, 1)
                shared(0, 0, 0)
                with pe.Fori(1, B // 2) as c:
                    prepare(2 * c, 0)
                    prepare(2 * c + 1, 1)
                    shared(c, c * FB, c)
                pe.wait_ge(s_const, CONSTS)
                pe.wait_ge(s_rt, RT_HOT)
                pe.matmul(ps_r[:, 0:TC * E], tri[:, :], hotb[:, :, :, :].rearrange("p s t e -> p (s t e)"),
                          start=True, stop=True)
                pe.matmul(ps_r2[:, 0:TC * E], onesb[:, :], hotb[:, :, :, :].rearrange("p s t e -> p (s t e)"),
                          start=True, stop=True).then_inc(s_cnt, 1)
                with pe.Fori(B // 2, BEFORE) as c:
                    shared(c, c * FB, c)
                pe.wait_ge(s_rt, RT_PAY)
                for k in range(TC):
                    last = pe.matmul(ps_t[:, 0:PAY * ST], lohot[:, k, :], pay[:, k, :, :].rearrange("p a h -> p (a h)"),
                                     start=(k == 0), stop=(k == TC - 1))
                last.then_inc(s_map, 1)

                def rows(e, r, n):
                    pe.wait_ge(s_gath[r], n * ET * 16)
                    if isinstance(e, int) and e == 0:
                        pe.wait_ge(s_rt, RT_SLOT)
                    for i in range(ET):
                        last = pe.transpose(ps_t[:, P * i:P * i + P], xg[r][:, i, :], ident[:, :])
                    last.then_inc(s_xgT, 1)

                def back(e):
                    pe.wait_ge(s_y, BEFORE + e + 1)
                    if not (isinstance(e, int) and e == 0):
                        pe.wait_ge(s_ye, e)
                    for i in range(ET):
                        last = pe.transpose(ps_r[:, P * i:P * i + P], yeT[:, P * i:P * i + P], ident[:, :])
                    last.then_inc(s_yeT, 1)

                def expert(e, r, n, last=False, first=False):
                    u = U_EXP + e * FB
                    pe.wait_ge(s_we[r], n * 48)
                    for f in range(FB):
                        if f == 0:
                            pe.wait_ge(s_xe, e + 1)
                        up(u + f, f, w1[r], w3[r], xeT[r][:, :], SLOTS)
                        if f:
                            down(u + f - 1, f - 1, w2[r], SLOTS, BEFORE + e)
                        if f == 1:
                            if not last:
                                rows(e + 1, 1 - r, n + (1 if r else 0))
                            if not first:
                                back(e - 1)
                    down(u + FB - 1, FB - 1, w2[r], SLOTS, BEFORE + e)

                rows(0, 0, 1)
                expert(0, 0, 1, first=True)
                with pe.Fori(0, (E - 1) // 2 - 1) as it:
                    expert(2 * it + 1, 1, it + 1)
                    expert(2 * it + 2, 0, it + 2)
                expert(E - 2, 1, (E - 1) // 2)
                expert(E - 1, 0, (E + 1) // 2, last=True)
                back(E - 1)
                with pe.Fori(BEFORE, B) as c:
                    shared(c, c * FB + E * FB, c + E)

                def turn(c):
                    if not (isinstance(c, int) and c == 0):
                        pe.wait_ge(s_sum, 2 * c - 1)
                    for i in range(QT):
                        last = pe.transpose(ps_t[:, P * i:P * i + P], sharedT[:, (c * QT + i) * P:(c * QT + i + 1) * P],
                                            ident[:, :])
                    last.then_inc(s_sT, 1)

                pe.wait_ge(s_y, B + E)
                for c in range(B):
                    turn(c)

            def route(dve):
                steps = [0]

                def step(ins, at=None):
                    steps[0] += 1
                    ins.then_inc(s_rt, 1)
                    dve.wait_ge(s_rt, steps[0])
                    assert at is None or at == steps[0], (at, steps[0])

                def over_e(ap):
                    return ap.unsqueeze(2).to_broadcast([P, NT, E])

                def e_row():
                    return iota_e[:, :].unsqueeze(1).to_broadcast([P, NT, E])

                dve.wait_ge(s_const, CONSTS)
                dve.wait_ge(s_lge, B)
                left = logit[:, :, :]
                for s in range(TOP):
                    step(dve.reduce_max(top[:, s, :], left, AX.X))
                    a, b = wk[0][:, 0, :, :], wk[1][:, 0, :, :]
                    step(dve.tensor_tensor(a, left, over_e(top[:, s, :]), ALU.is_lt))
                    step(dve.scalar_tensor_tensor(b, a, 8.0, e_row(), ALU.mult, ALU.add))
                    step(dve.tensor_reduce(expert[:, s, :], b, AX.X, ALU.min))
                    step(dve.tensor_tensor(hot[:, s, :, :], e_row(), over_e(expert[:, s, :]), ALU.is_equal))
                    if s == 0:
                        left = wk[2][:, 0, :, :]
                        step(dve.scalar_tensor_tensor(left, hot[:, 0, :, :], -3.0e38, logit[:, :, :], ALU.mult, ALU.add))
                step(dve.tensor_copy(hotb[:, :, :, :], hot[:, :, :, :]), RT_HOT)
                step(dve.tensor_tensor(small[0][:, 0:NT], top[:, 1, :], top[:, 0, :], ALU.subtract), RT_DIFF)
                dve.wait_ge(s_cnt, 1)
                flat = [w[:, :, :, :].rearrange("p s t e -> p (s t) e") for w in wk]
                step(dve.tensor_copy(flat[0], ps_r2[:, 0:TC * E].rearrange("p (k e) -> p k e", e=E)))
                cur, nxt, d = 0, 1, 1
                while d < TC:
                    step(dve.tensor_copy(flat[nxt][:, 0:d, :], flat[cur][:, 0:d, :]))
                    step(dve.tensor_tensor(flat[nxt][:, d:TC, :], flat[cur][:, d:TC, :], flat[cur][:, 0:TC - d, :], ALU.add))
                    cur, nxt, d = nxt, cur, 2 * d
                step(dve.tensor_tensor(flat[cur], flat[cur], ps_r2[:, 0:TC * E].rearrange("p (k e) -> p k e", e=E), ALU.subtract))
                step(dve.tensor_tensor(flat[cur], flat[cur], ps_r[:, 0:TC * E].rearrange("p (k e) -> p k e", e=E), ALU.add))
                hotf = hot[:, :, :, :].rearrange("p s t e -> p (s t) e")
                step(dve.tensor_tensor(flat[2], flat[cur], hotf, ALU.mult))
                rank = small[1]
                step(dve.tensor_reduce(rank[:, :], flat[2], AX.X, ALU.add))
                pos, lo, hi = smalli
                step(dve.tensor_scalar(pos[:, :], rank[:, :], -1.0, None, ALU.add))
                step(dve.tensor_scalar(lo[:, :], pos[:, :], P - 1, None, ALU.bitwise_and))
                step(dve.tensor_scalar(hi[:, :], pos[:, :], P.bit_length() - 1, None, ALU.arith_shift_right))
                lof, hif = small[2], small[3]
                step(dve.tensor_copy(lof[:, :], lo[:, :]))
                step(dve.tensor_copy(hif[:, :], hi[:, :]))
                step(dve.scalar_tensor_tensor(hif[:, :], expert[:, :, :].rearrange("p s t -> p (s t)"), float(ET),
                                              hif[:, :], ALU.mult, ALU.add))
                step(dve.tensor_scalar(rank[:, :], rank[:, :], float(CAPACITY), 1000.0, ALU.is_gt, ALU.mult))
                step(dve.tensor_tensor(hif[:, :], hif[:, :], rank[:, :], ALU.add))
                dve.wait_ge(s_exp, 1)
                step(dve.tensor_scalar(gate[:, 0, :], gate[:, 1, :], 1.0, None, ALU.add))
                step(dve.reciprocal(gate[:, 0, :], gate[:, 0, :]))
                step(dve.tensor_tensor(gate[:, 1, :], gate[:, 1, :], gate[:, 0, :], ALU.mult))
                rests = [gate, grest[0], grest[1]]
                for i in range(PARTS):
                    step(dve.tensor_copy(gpart[:, i, :, :], rests[i][:, :, :]))
                    if i < PARTS - 1:
                        step(dve.tensor_tensor(rests[i + 1][:, :, :], rests[i][:, :, :], gpart[:, i, :, :], ALU.subtract))
                step(dve.tensor_tensor(lohot[:, :, :], iota_lo[:, :].unsqueeze(1).to_broadcast([P, TC, P]),
                                       lof[:, :].unsqueeze(2).to_broadcast([P, TC, P]), ALU.is_equal))
                filled = pay[:, :, 0, :]
                step(dve.tensor_tensor(filled, iota_hi[:, :].unsqueeze(1).to_broadcast([P, TC, ST]),
                                       hif[:, :].unsqueeze(2).to_broadcast([P, TC, ST]), ALU.is_equal))
                for s in range(TOP):
                    step(dve.tensor_tensor(pay[:, NT * s:NT * s + NT, 1, :], pay[:, NT * s:NT * s + NT, 0, :],
                                           iota_t[:, :].unsqueeze(2).to_broadcast([P, NT, ST]), ALU.mult))
                step(dve.tensor_scalar(pay[:, :, 2, :], filled, iota_p[:, 0:1], None, ALU.mult))
                for i in range(PARTS):
                    step(dve.tensor_tensor(pay[:, :, 3 + i, :], filled,
                                           gpart[:, i, :, :].rearrange("p s t -> p (s t)").unsqueeze(2).to_broadcast([P, TC, ST]),
                                           ALU.mult), RT_PAY if i == PARTS - 1 else None)
                dve.wait_ge(s_map, 1)
                step(dve.tensor_copy(slot[:, :, :], ps_t[:, 0:PAY * ST].rearrange("p (a h) -> p a h", a=PAY)), RT_SLOT)
                step(dve.scalar_tensor_tensor(stmp[0][:, :], slot[:, 1, :], float(P), slot[:, 2, :], ALU.mult, ALU.add))
                step(dve.tensor_scalar(stmp[1][:, 0:1], iota_p[:, :], float(TOKENS), None, ALU.add))
                step(dve.tensor_scalar(stmp[2][:, :], slot[:, 0, :], -1.0, 1.0, ALU.mult, ALU.add))
                step(dve.scalar_tensor_tensor(token[:, :], stmp[2][:, :], stmp[1][:, 0:1], stmp[0][:, :], ALU.mult, ALU.add))
                step(dve.tensor_tensor(sgate[:, :], slot[:, 3 + PARTS - 1, :], slot[:, 3 + PARTS - 2, :], ALU.add))
                step(dve.tensor_tensor(sgate[:, :], sgate[:, :], slot[:, 3, :], ALU.add), RT_STEPS)

            @block.vector
            def _(dve):
                def xb(b):
                    return x[:, bass.ds(QT * b, QT), :]

                def normed(c, r, before):
                    if not (isinstance(before, int) and before == 0):
                        dve.wait_ge(s_nT, c - 1)
                        dve.wait_ge(s_nout[r], before * 16)
                    layernorm(dve, nrm[r][:, :, :], xb(c), stats, mv, rs, lntmp, s_ln, c, s_passed)

                normed(0, 0, 0)
                normed(1, 1, 0)
                with dve.Fori(1, B // 2) as it:
                    normed(2 * it, 0, it)
                    normed(2 * it + 1, 1, it)

                route(dve)

                def product(u, f, w):
                    dve.wait_ge(s_gate, u + 1)
                    dve.wait_ge(s_down, u - FB + 1)
                    dve.tensor_tensor(hid[:, f, 0:w], gatea[f % 2][:, 0:w], ps_b[f % 2][:, 0:w], ALU.mult)\
                        .then_inc(s_hid, 1)

                def gated(e, r):
                    dve.wait_ge(s_yeT, e + 1)
                    if not (isinstance(e, int) and e < 2):
                        dve.wait_ge(s_scat, (e - 1) * (ET * 16))
                    for i in range(ET):
                        ins = dve.tensor_tensor(ye[r][:, i, :], ps_r[:, P * i:P * i + P],
                                                sgate[:, bass.ds(e * ET + i, 1)].to_broadcast([P, C]), ALU.mult)
                        if i == ET - 1:
                            ins.then_inc(s_ye, 1)

                def expert(e, r, first=False):
                    for f in range(FB):
                        product(U_EXP + e * FB + f, f, SLOTS)
                        if f == 1 and not first:
                            gated(e - 1, 1 - r)

                expert(0, 0, first=True)
                expert(1, 1)
                expert(2, 0)
                with dve.Fori(1, (E - 1) // 2) as it:
                    expert(2 * it + 1, 1)
                    expert(2 * it + 2, 0)
                gated(E - 1, 0)
                with dve.Fori(BEFORE, B) as c:
                    for f in range(FB):
                        product(E * FB + c * FB + f, f, T)
                for c in range(B):
                    dve.wait_ge(s_sT, c + 1)
                    dve.tensor_tensor(xb(c), xb(c), ps_t[:, :].rearrange("p (i c) -> p i c", i=QT), ALU.add)\
                        .then_inc(s_sum, 1)
                    dve.wait_ge(s_sum, 2 * c + 1)
                    dve.wait_ge(s_acc[c % 2], (c // 2 + 1) * 16)
                    dve.tensor_tensor(xb(c), xb(c), routed[c % 2][:, :, :], ALU.add).then_inc(s_sum, 1)
                    dve.wait_ge(s_sum, 2 * c + 2)
                    layernorm(dve, xb(c), xb(c), stats, mv, rs, lntmp, s_ln, B + c, s_passed)


RT_HOT = 12
RT_DIFF = 13
RT_PAY = 54
RT_SLOT = 55
RT_STEPS = 61


def dense_ffn(nc, x, ident, dram, out_rows, tag="f1"):
    with ExitStack() as ctx:
        def psum(name, shape, dt=F32):
            return ctx.enter_context(nc.psum_tensor(tag + name, shape, dt))

        def sbuf(name, shape, dt=F32):
            return ctx.enter_context(nc.sbuf_tensor(tag + name, shape, dt))

        def sem(name):
            return ctx.enter_context(nc.semaphore(tag + name))

        raw = {"w1": sbuf("w1r", [P, FB, C]), "w2": sbuf("w2r", [P, FB, C]), "h1": sbuf("h1r", [P, FB, FF]),
               "h2": sbuf("h2r", [P, FB, FF]), "w3": sbuf("w3r", [P, 1, FF])}
        wT = {"w1": sbuf("w1T", [P, 1, FF]), "w2": sbuf("w2T", [P, 1, FF]), "h1": sbuf("h1T", [P, FB, FF]),
              "h2": sbuf("h2T", [P, FB, FF]), "w3": sbuf("w3T", [P, FB, C])}
        sc = {"w1": sbuf("w1s", [P, FB]), "w2": sbuf("w2s", [P, FB]), "h1": sbuf("h1s", [P, FB]),
              "h2": sbuf("h2s", [P, FB]), "w3": sbuf("w3s", [P, 1])}
        half = sbuf("half", [P, FB])
        gated = sbuf("gated", [P, FB])
        xin = sbuf("xin", [P, QT, C])
        xT = sbuf("xT", [C, T])
        th = [sbuf(f"th{i}", [P, T]) for i in range(2)]
        u_sb = [sbuf(f"u{i}", [P, T]) for i in range(2)]
        hid = [sbuf(f"hid{i}", [P, FB, T]) for i in range(3)]
        yT = sbuf("yT", [C, T])
        res = sbuf("res", [P, QT, C])
        fin = [sbuf(f"fin{i}", [P, QT, C]) for i in range(2)]
        stats, mv = sbuf("stats", [P, QT, 6]), sbuf("mv", [P, QT, 2])
        lntmp, rs = sbuf("lntmp", [P, 4, QT]), sbuf("rs", [P, QT])
        ps_a = [psum(f"ps_a{i}", [P, T]) for i in range(2)]
        ps_b = [psum(f"ps_b{i}", [P, T]) for i in range(2)]
        ps_h = [psum(f"ps_h{i}", [P, T]) for i in range(2)]
        ps_y = psum("ps_y", [P, T])
        ps_t = psum("ps_t", [P, T])

        s_w = sem("w")
        s_wt = sem("wt")
        s_wc = sem("wc")
        s_sc = sem("sc")
        s_xin = sem("xin")
        s_xt = sem("xt")
        s_xc = sem("xc")
        s_up = sem("up")
        s_th = sem("th")
        s_g = sem("g")
        s_h = sem("h")
        s_ge = sem("ge")
        s_y = sem("y")
        s_yc = sem("yc")
        s_t = sem("t")
        s_res = sem("res")
        s_ln = sem("ln")
        s_out = [sem(f"out{i}") for i in range(2)]
        s_passed = sem("passed")

        TURNS = [("w1", [(0, o) for o in range(FB)]), ("w2", [(0, o) for o in range(FB)])] + \
                [(w, [(k, o) for o in range(FB)]) for w in ("h1", "h2") for k in range(FB)] + \
                [("w3", [(k, 0) for k in range(FB)])]

        with nc.Block() as block:
            @block.sync
            def _(sp):
                for w in ("w1", "w2", "h1", "h2", "w3"):
                    sp.dma_start(raw[w][:, :, :], dram[w + "_w"].rearrange("(o p) i -> p o i", p=P)).then_inc(s_w, 16)
                    with nc.allow_non_contiguous_dma(reason="a few hundred scales"):
                        sp.dma_start(sc[w][:, :], dram[w + "_s"].rearrange("(o p) -> p o", p=P)).then_inc(s_w, 16)

                def load(c):
                    if not (isinstance(c, int) and c == 0):
                        sp.wait_ge(s_xt, c)
                        by_itself(sp, s_passed)
                    sp.dma_start(xin[:, :, :], x[:, bass.ds(c * QT, QT), :]).then_inc(s_xin, 16)

                def store(c, r):
                    sp.wait_ge(s_ln, (c + 1) * LN_STEPS)
                    by_itself(sp, s_passed)
                    sp.dma_start(out_rows(c), fin[r][:, :, :]).then_inc(s_out[r], 16)

                load(0)
                load(1)
                with sp.Fori(0, B // 2 - 1) as it:
                    load(2 * it + 2)
                    store(2 * it, 0)
                    load(2 * it + 3)
                    store(2 * it + 1, 1)
                store(B - 2, 0)
                store(B - 1, 1)
                for r in range(2):
                    sp.wait_ge(s_out[r], B // 2 * 16)

            @block.scalar
            def _(act):
                for n, (w, blocks) in enumerate(TURNS):
                    act.wait_ge(s_wt, n + 1)
                    src = (ps_a + ps_b)[n % 4]
                    if w == "w3":
                        dst = wT[w][:, :, :].rearrange("p k c -> p (k c)")
                    else:
                        dst = wT[w][:, blocks[0][0], :]
                    act.activation(dst, src[:, :], ACT.Copy).then_inc(s_wc, 1)
                act.wait_ge(s_sc, 2)

                def turned(c):
                    act.wait_ge(s_xt, c + 1)
                    act.activation(xT[:, :], ps_t[:, :], ACT.Copy).then_inc(s_xc, 1)

                def gate(c, f):
                    u = c * FB + f
                    act.wait_ge(s_up, u + 1)
                    if not (isinstance(u, int) and u < 2):
                        act.wait_ge(s_g, 2 * (u - 1))
                    act.activation(th[f % 2][:, :], ps_a[f % 2][:, :], ACT.Tanh, scale=half[:, f:f + 1])\
                        .then_inc(s_th, 1)

                def layer(c, n):
                    w, first = ("h1", "h2")[n], not isinstance(c, int) or c > 0
                    for f in range(FB):
                        u = (2 * c + n) * FB + f
                        act.wait_ge(s_h, u + 1)
                        act.activation(hid[n + 1][:, f, :], ps_h[f % 2][:, :], ACT.Gelu, scale=sc[w][:, f:f + 1])\
                            .then_inc(s_ge, 1)

                def out(c):
                    act.wait_ge(s_y, c + 1)
                    act.activation(yT[:, :], ps_y[:, :], ACT.Copy, scale=sc["w3"][:, 0:1]).then_inc(s_yc, 1)

                def chunk(c, last=False):
                    layer(c, 0)
                    if not last:
                        turned(c + 1)
                        gate(c + 1, 0)
                        gate(c + 1, 1)
                    layer(c, 1)
                    if not last:
                        gate(c + 1, 2)
                        gate(c + 1, 3)
                    out(c)

                turned(0)
                for f in range(FB):
                    gate(0, f)
                with act.Fori(0, B - 1) as c:
                    chunk(c)
                chunk(B - 1, last=True)

            @block.tensor
            def _(pe):
                for n, (w, blocks) in enumerate(TURNS):
                    if n == 0:
                        pe.wait_ge(s_w, 10 * 16)
                    if n >= 4:
                        pe.wait_ge(s_wc, n - 3)
                    for i, (k, o) in enumerate(blocks):
                        last = pe.transpose((ps_a + ps_b)[n % 4][:, P * i:P * i + P], raw[w][:, o, P * k:P * k + P],
                                            ident[:, :])
                    last.then_inc(s_wt, 1)
                pe.wait_ge(s_wc, len(TURNS))

                def turn(c):
                    pe.wait_ge(s_xin, (c + 1) * 16)
                    if not (isinstance(c, int) and c <= 1):
                        pe.wait_ge(s_res, c - 1)
                    for i in range(QT):
                        last = pe.transpose(ps_t[:, P * i:P * i + P], xin[:, i, :], ident[:, :])
                    last.then_inc(s_xt, 1)

                def up(c, f):
                    u = c * FB + f
                    if f == 0:
                        pe.wait_ge(s_xc, c + 1)
                    if not (isinstance(u, int) and u < 2):
                        pe.wait_ge(s_g, 2 * (u - 1))
                    pe.matmul(ps_a[f % 2][:, :], wT["w1"][:, 0, P * f:P * f + P], xT[:, :], start=True, stop=True)
                    pe.matmul(ps_b[f % 2][:, :], wT["w2"][:, 0, P * f:P * f + P], xT[:, :], start=True, stop=True)\
                        .then_inc(s_up, 1)

                def layer(c, n):
                    w = ("h1", "h2")[n]
                    if n == 0:
                        pe.wait_ge(s_g, 2 * (c + 1) * FB)
                    else:
                        pe.wait_ge(s_ge, (2 * c + 1) * FB)
                    for f in range(FB):
                        u = (2 * c + n) * FB + f
                        if n or f >= 2:
                            pe.wait_ge(s_ge, u - 1)
                        for k in range(FB):
                            last = pe.matmul(ps_h[f % 2][:, :], wT[w][:, k, P * f:P * f + P], hid[n][:, k, :],
                                             start=(k == 0), stop=(k == FB - 1))
                        last.then_inc(s_h, 1)

                def out(c):
                    pe.wait_ge(s_ge, (2 * c + 2) * FB)
                    if not (isinstance(c, int) and c == 0):
                        pe.wait_ge(s_yc, c)
                    for k in range(FB):
                        last = pe.matmul(ps_y[:, :], wT["w3"][:, k, :], hid[2][:, k, :], start=(k == 0),
                                         stop=(k == FB - 1))
                    last.then_inc(s_y, 1)

                def back(c):
                    pe.wait_ge(s_yc, c + 1)
                    if not (isinstance(c, int) and c == 0):
                        pe.wait_ge(s_res, c)
                    for i in range(QT):
                        last = pe.transpose(ps_t[:, P * i:P * i + P], yT[:, P * i:P * i + P], ident[:, :])
                    last.then_inc(s_t, 1)

                def chunk(c, first=False, last=False):
                    if not last:
                        turn(c + 1)
                    layer(c, 0)
                    if not last:
                        up(c + 1, 0)
                        up(c + 1, 1)
                    layer(c, 1)
                    if not last:
                        up(c + 1, 2)
                        up(c + 1, 3)
                    out(c)
                    back(c)

                turn(0)
                for f in range(FB):
                    up(0, f)
                with pe.Fori(0, B - 1) as c:
                    chunk(c)
                chunk(B - 1, last=True)

            @block.vector
            def _(dve):
                dve.wait_ge(s_w, 10 * 16)
                dve.tensor_scalar(half[:, :], sc["w1"][:, :], 0.5, None, ALU.mult).then_inc(s_sc, 1)
                dve.wait_ge(s_sc, 1)
                dve.tensor_tensor(gated[:, :], half[:, :], sc["w2"][:, :], ALU.mult).then_inc(s_sc, 1)
                dve.wait_ge(s_sc, 2)

                def gate(c, f):
                    u = c * FB + f
                    dve.wait_ge(s_th, u + 1)
                    dve.scalar_tensor_tensor(u_sb[f % 2][:, :], th[f % 2][:, :], 1.0, ps_a[f % 2][:, :], ALU.add, ALU.mult)\
                        .then_inc(s_g, 1)
                    if not (isinstance(c, int) and c == 0):
                        dve.wait_ge(s_h, 2 * c * FB - FB)
                    dve.wait_ge(s_g, 2 * u + 1)
                    dve.scalar_tensor_tensor(hid[0][:, f, :], ps_b[f % 2][:, :], gated[:, f:f + 1], u_sb[f % 2][:, :],
                                             ALU.mult, ALU.mult).then_inc(s_g, 1)

                def finish(c, r, before):
                    dve.wait_ge(s_t, c + 1)
                    if not (isinstance(c, int) and c == 0):
                        by_itself(dve, s_passed)
                        dve.wait_ge(s_ln, c * LN_STEPS)
                    dve.tensor_tensor(res[:, :, :], x[:, bass.ds(c * QT, QT), :],
                                      ps_t[:, :].rearrange("p (i c) -> p i c", i=QT), ALU.add).then_inc(s_res, 1)
                    dve.wait_ge(s_res, c + 1)
                    if before is not None:
                        dve.wait_ge(s_out[r], before * 16)
                    layernorm(dve, fin[r][:, :, :], res[:, :, :], stats, mv, rs, lntmp, s_ln, c, s_passed)

                for f in range(FB):
                    gate(0, f)

                def chunk(c, r, before, last=False):
                    if not last:
                        for f in range(FB):
                            gate(c + 1, f)
                    finish(c, r, before)

                chunk(0, 0, None)
                chunk(1, 1, None)
                with dve.Fori(1, B // 2 - 1) as it:
                    chunk(2 * it, 0, it)
                    chunk(2 * it + 1, 1, it)
                chunk(B - 2, 0, B // 2 - 1)
                chunk(B - 1, 1, B // 2 - 1, last=True)


def prologue(nc, x, x_rows, ident, identb, mask, wqkv, heads0, wq1, heads1, wproj, wproj_dram, cos, sin, angles):
    with ExitStack() as ctx:
        def sbuf(name, shape, dt=F32):
            return ctx.enter_context(nc.sbuf_tensor("pre_" + name, shape, dt))

        def sem(name):
            return ctx.enter_context(nc.semaphore("pre_" + name))

        w0 = sbuf("w0", [C, 3 * C])
        w1 = [sbuf("w1" + n, [C, C]) for n in "qkv"]
        ps_w = [ctx.enter_context(nc.psum_tensor(f"pre_ps{i}", [P, C], F32)) for i in range(3)]
        s_w = sem("w")
        s_x = sem("x")
        s_const = sem("const")
        s_turn = sem("turn")
        s_done = sem("done")

        with nc.Block() as block:
            @block.sync
            def _(sp):
                sp.dma_start(w0[:, :], wqkv).then_inc(s_w, 16)
                for dst, src in zip(w1, wq1):
                    sp.dma_start(dst[:, :], src).then_inc(s_w, 16)
                sp.dma_start(wproj[:, :], wproj_dram).then_inc(s_w, 16)
                sp.wait_ge(s_w, 5 * 16)

            @block.scalar
            def _(act):
                for table, angle in ((cos, angles[0]), (sin, angles[1])):
                    for d in range(D):
                        act.dma_start(table[H * d:H * d + H, :], angle[d:d + 1, :].to_broadcast([H, T])).then_inc(s_x, 16)
                act.dma_start(x[:, :, :], x_rows).then_inc(s_x, 16)
                act.wait_ge(s_x, (2 * D + 1) * 16)

            @block.gpsimd
            def _(pool):
                for m in (ident, identb, mask):
                    pool.memset(m[:, :], 0.0).then_inc(s_const, 1)
                pool.wait_ge(s_const, 3)
                for m in (ident, identb):
                    pool.affine_select(out=m[:, :], in_=m[:, :], compare_op=ALU.not_equal, fill=1.0, base=0,
                                       pattern=[[-1, P]], channel_multiplier=1).then_inc(s_const, 1)
                pool.affine_select(out=mask[:, :], in_=mask[:, :], compare_op=ALU.is_ge, fill=-1e30, base=0,
                                   pattern=[[-1, P]], channel_multiplier=1).then_inc(s_const, 1)
                pool.wait_ge(s_const, 6)

            @block.tensor
            def _(pe):
                pe.wait_ge(s_w, 5 * 16)
                pe.wait_ge(s_const, 6)
                for i in range(3):
                    pe.transpose(ps_w[i][:, :], w1[i][:, :], ident[:, :]).then_inc(s_turn, 1)

            @block.vector
            def _(dve):
                def columns(out, name, src):
                    hd = src.rearrange("c (h d) -> c h d", h=H)
                    dve.tensor_copy(out[name][:, :].rearrange("c (d h) -> c h d", h=H), hd).then_inc(s_done, 1)
                    pairs = src.rearrange("c (h i two) -> c two h i", h=H, two=2)
                    dst = out[name + "r"][:, :].rearrange("c (i two h) -> c two h i", two=2, h=H)
                    dve.tensor_scalar(dst[:, 0], pairs[:, 1], -1.0, None, ALU.mult).then_inc(s_done, 1)
                    dve.tensor_copy(dst[:, 1], pairs[:, 0]).then_inc(s_done, 1)

                dve.wait_ge(s_w, 5 * 16)
                columns(heads0, "q", w0[:, 0:C])
                columns(heads0, "k", w0[:, C:2 * C])
                dve.tensor_copy(heads0["v"][:, :], w0[:, 2 * C:3 * C]).then_inc(s_done, 1)
                dve.wait_ge(s_turn, 3)
                columns(heads1, "q", ps_w[0][:, :])
                columns(heads1, "k", ps_w[1][:, :])
                dve.tensor_copy(heads1["v"][:, :], ps_w[2][:, :]).then_inc(s_done, 1)
                dve.wait_ge(s_done, 14)


class BatchRows:

    def __init__(self, array):
        self.array = array.rearrange("(b i p) c -> b p i c", p=P, i=QT)

    def __getitem__(self, b):
        if isinstance(b, int):
            return self.array[b]
        return self.array[bass.ds(b, 1)].rearrange("b p i c -> p (b i) c")


def transformer(nc, ins, angles, normed, acc, out):
    with ExitStack() as ctx:
        def sbuf(name, shape, dt=F32):
            return ctx.enter_context(nc.sbuf_tensor(name, shape, dt))

        x = sbuf("x_tiles", [P, NT, C])
        ident, identb = sbuf("ident", [P, P]), sbuf("identb", [P, P], BF16)
        mask = sbuf("mask", [P, P], BF16)
        wproj = sbuf("wproj", [C, C])
        cos, sin = sbuf("cos_table", [C, T]), sbuf("sin_table", [C, T])
        heads0, heads1 = [{n: sbuf(f"heads{i}_{n}", [C, C]) for n in ("k", "kr", "q", "qr", "v")} for i in range(2)]
        x_in = ins["L0_attn_x"].rearrange("b t c -> (b t) c")
        out_rows = out.rearrange("b t c -> (b t) c")

        prologue(nc, x, x_in.rearrange("(n p) c -> p n c", p=P), ident, identb, mask, ins["L0_attn_Wqkv"], heads0,
                 [ins["L1_attn_W" + n] for n in "qkv"], heads1, wproj, ins["L0_attn_Wproj"], cos, sin, angles)
        attention(nc, x, BatchRows(x_in), ident, identb, mask, heads0, wproj, cos, sin, True, "a0_")
        dram = {n: ins["L0_ffn_" + n] for n in ("ln_g", "ln_b", "Wr", "W1", "W3", "W2", "W1s", "W3s", "W2s")}
        moe_ffn(nc, x, ident, identb, dict(dram, acc=acc, normed=normed, normed_rows=BatchRows(normed[0:TOKENS, :]).__getitem__),
                "f0_")
        attention(nc, x, None, ident, identb, mask, heads1, None, cos, sin, False, "a1_")
        dense_ffn(nc, x, ident, {n + s: ins["L1_ffn_" + n + s] for n in ("w1", "w2", "h1", "h2", "w3") for s in ("_w", "_s")},
                  BatchRows(out_rows).__getitem__, "f1_")


_INS = ['L0_attn_x', 'L0_attn_Wqkv', 'L0_attn_Wproj', 'L0_ffn_ln_g', 'L0_ffn_ln_b', 'L0_ffn_Wr', 'L0_ffn_W1',
        'L0_ffn_W3', 'L0_ffn_W2', 'L0_ffn_W1s', 'L0_ffn_W3s', 'L0_ffn_W2s', 'L1_attn_Wq', 'L1_attn_Wk', 'L1_attn_Wv',
        'L1_ffn_w1_w', 'L1_ffn_w1_s', 'L1_ffn_w2_w', 'L1_ffn_w2_s', 'L1_ffn_h1_w', 'L1_ffn_h1_s', 'L1_ffn_h2_w',
        'L1_ffn_h2_s', 'L1_ffn_w3_w', 'L1_ffn_w3_s']


def kernel(**inputs):
    import numpy as _np
    import concourse.bacc as _bacc
    from concourse import mybir as _mybir
    from concourse.bass_utils import run_bass_kernel_spmd as _run

    nc = _bacc.Bacc("TRN2", target_bir_lowering=False, num_devices=1)
    arrays, ins = {}, {}

    def put(name, a):
        arrays[f"in_{name}_dram"] = a
        return nc.dram_tensor(f"in_{name}_dram", a.shape, _mybir.dt.from_np(a.dtype), kind="ExternalInput").ap()

    for name in _INS:
        ins[name] = put(name, _np.ascontiguousarray(inputs[name]))
    inv = (1.0 / 10000.0 ** (_np.arange(0, D, 2, dtype=_np.float32) / D)).astype(_np.float32)
    angle = (_np.arange(T, dtype=_np.float32)[:, None] * inv[None, :]).astype(_np.float32)
    angles = [put(name, _np.ascontiguousarray(_np.repeat(fn(angle), 2, axis=-1).T.astype(_np.float32)))
              for name, fn in (("cos", _np.cos), ("sin", _np.sin))]
    out = nc.dram_tensor("out_0_dram", (B, T, C), F32, kind="ExternalOutput").ap()
    normed = nc.dram_tensor("normed_rows_dram", (TOKENS + P, C), F32, kind="Internal").ap()
    acc = nc.dram_tensor("expert_sums_dram", (TOKENS + P, C), F32, kind="Internal").ap()
    transformer(nc, ins, angles, normed, acc, out)
    r = _run(nc, [arrays], core_ids=[0])
    return r.results[0]["out_0_dram"]
```

```python
import concourse.bass as bass
from concourse import mybir
from contextlib import ExitStack

F32 = mybir.dt.float32
BF16 = mybir.dt.bfloat16
F32R = mybir.dt.float32r
ALU = mybir.AluOpType
ACT = mybir.ActivationFunctionType
AX = mybir.AxisListType

P = 128
C = 128
B, T = 8, 512
QT = T // P
NT = B * QT
H, D = 16, 8
HG = 4
NG = H // HG
PARTS = 3
PROD = PARTS * PARTS
ROWS = PROD * D
SWAP = [(i + H) % (2 * H) for i in range(2 * H)]
FULL = 96
VW = 32
EPS = 1e-5
NEWTON = 3


def causal_widths(causal):
    seen_by = [T - P * j if causal else T for j in range(QT)]
    sees = [P * (i + 1) if causal else T for i in range(QT)]
    return seen_by, sees


def by_itself(eng, sem):
    eng.sem_inc(sem, 1)


def layernorm_phase(dve, out, src, stats, mv, rs, tmp, sem, n, past, phase):
    var, y, half, t = (tmp[:, i, :] for i in range(4))
    I32 = mybir.dt.int32
    if phase > 0:
        dve.wait_ge(sem, n * LN_STEPS + LN_DONE[phase - 1])
    if phase < 2:
        by_itself(dve, past)
    if phase == 0:
        for i in range(QT):
            dve.bn_stats(stats[:, i, :], src[:, i, :]).then_inc(sem, 1)
    elif phase == 1:
        for i in range(QT):
            dve.bn_aggr(mv[:, i, :], stats[:, i, :]).then_inc(sem, 1)
    elif phase == 2:
        dve.tensor_scalar(var, mv[:, :, 1], EPS, None, ALU.add).then_inc(sem, 1)
    elif phase == 3:
        dve.tensor_scalar(half, var, -0.5, None, ALU.mult).then_inc(sem, 1)
        dve.tensor_scalar(t.bitcast(I32), var.bitcast(I32), 1, None, ALU.arith_shift_right).then_inc(sem, 1)
    elif phase == 4:
        dve.tensor_scalar(y.bitcast(I32), t.bitcast(I32), -1.0, float(0x5F3759DF), ALU.mult, ALU.add)\
            .then_inc(sem, 1)
    elif phase < 5 + 3 * NEWTON:
        k, part = divmod(phase - 5, 3)
        if part == 0:
            dve.tensor_tensor(t, y, y, ALU.mult).then_inc(sem, 1)
        elif part == 1:
            dve.tensor_tensor(t, t, half, ALU.mult).then_inc(sem, 1)
        else:
            dve.scalar_tensor_tensor(rs[:, :] if k == NEWTON - 1 else y, t, 1.5, y, ALU.add, ALU.mult)\
                .then_inc(sem, 1)
    else:
        for i in range(QT):
            dve.tensor_scalar(out[:, i, :], src[:, i, :], mv[:, i, 0:1], rs[:, i:i + 1],
                              ALU.subtract, ALU.mult).then_inc(sem, 1)


LN_PHASES = 6 + 3 * NEWTON
LN_DONE = [QT, 2 * QT, 2 * QT + 1, 2 * QT + 3, 2 * QT + 4] + [2 * QT + 5 + k for k in range(3 * NEWTON)] + \
          [3 * QT + 4 + 3 * NEWTON]
LN_STEPS = LN_DONE[-1]


def layernorm(dve, out, src, stats, mv, rs, tmp, sem, n, past):
    for phase in range(LN_PHASES):
        layernorm_phase(dve, out, src, stats, mv, rs, tmp, sem, n, past, phase)


def layernorm_scales(dve, src, stats, mv, rs, shift, tmp, sem, n, past, tiles):
    var, y, half, t = (tmp[:, i, :] for i in range(4))
    I32 = mybir.dt.int32
    base = n * scale_steps(tiles)

    def wait(done):
        dve.wait_ge(sem, base + done)

    by_itself(dve, past)
    for i in range(tiles):
        dve.bn_stats(stats[:, i, :], src[:, i, :]).then_inc(sem, 1)
    wait(tiles)
    by_itself(dve, past)
    for i in range(tiles):
        dve.bn_aggr(mv[:, i, :], stats[:, i, :]).then_inc(sem, 1)
    wait(2 * tiles)
    dve.tensor_scalar(var, mv[:, :, 1], EPS, None, ALU.add).then_inc(sem, 1)
    dve.tensor_scalar(half, mv[:, :, 1], EPS, -0.5, ALU.add, ALU.mult).then_inc(sem, 1)
    wait(2 * tiles + 1)
    dve.tensor_scalar(t.bitcast(I32), var.bitcast(I32), 1, None, ALU.arith_shift_right).then_inc(sem, 1)
    wait(2 * tiles + 3)
    dve.tensor_scalar(y.bitcast(I32), t.bitcast(I32), -1.0, float(0x5F3759DF), ALU.mult, ALU.add).then_inc(sem, 1)
    for k in range(NEWTON):
        wait(2 * tiles + 4 + 3 * k)
        dve.tensor_tensor(t, y, y, ALU.mult).then_inc(sem, 1)
        wait(2 * tiles + 5 + 3 * k)
        dve.tensor_tensor(t, t, half, ALU.mult).then_inc(sem, 1)
        wait(2 * tiles + 6 + 3 * k)
        dve.scalar_tensor_tensor(rs if k == NEWTON - 1 else y, t, 1.5, y, ALU.add, ALU.mult).then_inc(sem, 1)
    wait(2 * tiles + 4 + 3 * NEWTON)
    dve.scalar_tensor_tensor(shift, mv[:, :, 0], -1.0, rs, ALU.mult, ALU.mult).then_inc(sem, 1)


def scale_steps(tiles):
    return 2 * tiles + 5 + 3 * NEWTON


def attention(nc, x, x_dram, ident, identb, mask, weights, wproj, cos, sin, causal, tag, ahead=None):
    seen_by, sees = causal_widths(causal)
    unit_heads = [T // w for w in seen_by]
    max_heads = [T // w for w in sees]
    SU = sum(HG // u for u in unit_heads)
    MU = sum(HG // u for u in max_heads)
    SBANKS, MBANKS = 2, 4
    assert NG * SU % SBANKS == 0 and NG * MU % MBANKS == 0
    RING = 4
    LAG = 2
    G = B * NG
    SLOTS = 4
    VALUES_AT = 3
    assert max(MU * (j + 1) // QT - MU * j // QT for j in range(QT)) <= SLOTS

    def jobs(b, g, j, first, last):
        out = []
        if not last and g == 0 and j == 0:
            out += ["xT", "k"]
        if j == 1 and not (last and g == NG - 1):
            out.append("maxT")
        if not last and g == 0 and j in (1, 3):
            out.append("q" if j == 1 else "v")
        if j == 2 and not (first and g == 0):
            out.append("norm")
        if not first:
            out += {(0, 3): ["yT"], (1, 1): ["proj"]}.get((g, j), []) if wproj is not None else []
        assert len(out) < SLOTS
        return out

    START = ["xT", "k", "q", "v", "maxT"]
    END = ["norm"] + (["yT", "proj"] if wproj is not None else [])

    def batch_jobs(first, last):
        return [(g, j, name) for g in range(NG) for j in range(QT) for name in jobs(0, g, j, first, last)]

    N0, N1 = len(batch_jobs(True, False)), len(batch_jobs(False, False))

    def jobs_before(b, first):
        return len(START) if first else len(START) + N0 + (b - 1) * N1

    def number(b, first, last, g, name):
        at = [n for n, (gg, _, x) in enumerate(batch_jobs(first, last)) if (gg, x) == (g, name)]
        assert len(at) == 1
        return jobs_before(b, first) + at[0]

    FREED = 2
    ORDER = [("k", 0), ("k", 1), ("q", 0), ("k", 2), ("q", 1), ("q", 2)]
    POOL_SENDS = [5]
    POOL_AT = {(0, 1): [0, 1], (0, 2): [2, 3], (0, 3): [4], (1, 0): [5]}
    ACT_AT = {(0, 1, 2): 0, (0, 2, 0): 1, (0, 2, 2): 2, (0, 3, 0): 3, (0, 3, 2): 4, (1, 0, 2): 5}

    with ExitStack() as ctx:
        def psum(name, shape, dt=F32):
            return ctx.enter_context(nc.psum_tensor(tag + name, shape, dt))

        def sbuf(name, shape, dt=F32):
            return ctx.enter_context(nc.sbuf_tensor(tag + name, shape, dt))

        def sem(name):
            return ctx.enter_context(nc.semaphore(tag + name))

        qst = [sbuf(f"qst{i}", [FULL, H, T], BF16) for i in range(2)]
        kst = [sbuf(f"kst{i}", [FULL, H, T], BF16) for i in range(2)]
        vst = [sbuf(f"vst{i}", [P, QT, H, VW]) for i in range(2)]
        prob = [sbuf(f"prob{i}", [P, HG, T]) for i in range(RING)]
        xin = sbuf("xin", [P, QT, C])
        xT = sbuf("xT", [C, T])
        rope = {n: sbuf("rope_" + n, [C, T]) for n in ("k", "q")}
        turned = {n: sbuf("turned_" + n, [C, T]) for n in ("k", "q")}
        part = {n: sbuf("part_" + n, [C, PARTS, T], BF16) for n in ("k", "q")}
        mx = sbuf("mx", [P, 2, QT, HG])
        rest = sbuf("rest", [P, 2, QT, HG])
        mpart = sbuf("mpart", [P, QT, PARTS, HG], BF16)
        mrow = sbuf("mrow", [PARTS * HG, T], BF16)
        oT = sbuf("oT", [P, T])
        rden = sbuf("rden", [P, QT, HG])
        y = sbuf("y", [P, QT, C])
        yT = sbuf("yT", [C, T]) if wproj is not None else None
        ones = sbuf("ones", [PARTS, T], BF16)
        stats = sbuf("stats", [P, QT, 6])
        mv = sbuf("mv", [P, QT, 2])
        lntmp = sbuf("lntmp", [P, 4, QT])
        rs = sbuf("rs", [P, QT])
        ps_s = [psum(f"ps_s{i}", [P, T]) for i in range(SBANKS)]
        ps_m = [psum(f"ps_m{i}", [P, T]) for i in range(MBANKS)]
        ps_o = psum("ps_o", [P, T])
        ps_x = psum("ps_x", [P, T])

        START_BANK = {"v": ps_o, "k": ps_m[0], "q": ps_m[1]}

        s_score = sem("score")
        s_score_free = sem("score_free")
        s_max = sem("max")
        s_max_free = sem("max_free")
        s_masked = sem("masked")
        s_pv = sem("pv")
        s_oT = sem("oT")
        s_job = sem("job")
        s_job_free = sem("job_free")
        s_xin = sem("xin")
        s_xres = sem("xres")
        s_rot = sem("rot")
        s_split = sem("split")
        s_cast = sem("cast")
        s_st = {"k": sem("stack_k"), "q": sem("stack_q")}
        s_pool_st = sem("pool_stack")
        s_mp = sem("mp")
        s_mst = sem("mst")
        s_norm = sem("norm")
        s_ln = sem("ln")
        s_res = sem("res")
        s_init = sem("init")
        s_ones = sem("ones_dma")
        s_passed = sem("passed")
        s_vinit = sem("vinit")

        def stack_rows(m):
            name, part_no = ORDER[m]
            return [(part_no * PARTS + other if name == "k" else other * PARTS + part_no) * D
                    for other in range(PARTS)]

        with nc.Block() as block:
            @block.sync
            def _(sp):
                def load(b, turned):
                    if turned is not None:
                        sp.wait_ge(s_job, turned + 1)
                        by_itself(sp, s_passed)
                    src = x_dram[b] if x_dram is not None else \
                        x[:, bass.ds(QT * b, QT), :] if not isinstance(b, int) else x[:, QT * b:QT * b + QT, :]
                    sp.dma_start(xin[:, :, :], src).then_inc(s_xin, 16)
                    if x_dram is not None:
                        sp.dma_start(x[:, QT * b:QT * b + QT, :] if isinstance(b, int) else
                                     x[:, bass.ds(QT * b, QT), :], src).then_inc(s_xres, 16)

                load(0, None)

                def ones_rows(i, inits):
                    sp.wait_ge(s_init, inits)
                    if i:
                        sp.wait_ge(s_ones, i * 16)
                    sp.dma_start(kst[i][ROWS:ROWS + PARTS, :, :],
                                 ones[:, :].unsqueeze(1).to_broadcast([PARTS, H, T])).then_inc(s_ones, 16)

                def stacks(b, r, m, wait_scores):
                    name, part_no = ORDER[m]
                    dst = {"k": kst, "q": qst}[name][r]
                    sp.wait_ge(s_cast, b * len(ORDER) + m + 1)
                    by_itself(sp, s_passed)
                    if wait_scores is not None:
                        sp.wait_ge(s_score, wait_scores)
                        by_itself(sp, s_passed)
                    for row in stack_rows(m):
                        sp.dma_start(dst[row:row + D, :, :], part[name][:, part_no, :]).then_inc(s_st[name], 16)

                def max_rows(turned, r, g):
                    sp.wait_ge(s_job_free, turned + FREED)
                    sp.dma_start(qst[r][ROWS:ROWS + PARTS, HG * g:HG * g + HG, :],
                                 mrow[:, :]).then_inc(s_mst, 16)

                def batch(b, r, first=False, last=False, before_last=False):
                    for g in range(NG):
                        if g == NG - 1 and not last and not before_last:
                            load(b + 2, number(b, first, last, 0, "xT"))
                        if g < NG - 1:
                            max_rows(number(b, first, last, g, "maxT"), r, g + 1)
                        elif not last:
                            max_rows(number(b, first, last, g, "maxT"), 1 - r, 0)
                        if g < 2 and not last:
                            for m in range(5) if g == 0 else [5]:
                                stacks(b + 1, 1 - r, m, None if first or m else b * (NG * SU))

                for m in range(len(ORDER)):
                    if ORDER[m] == ("k", PARTS - 1):
                        sp.wait_ge(s_init, 2)
                    if m not in POOL_SENDS:
                        stacks(0, 0, m, None)
                ones_rows(0, 3)
                load(1, 0)
                sp.wait_ge(s_pool_st, len(POOL_SENDS) * PARTS * 16)
                sp.sem_inc(s_st["q"], len(POOL_SENDS) * PARTS * 16)
                max_rows(len(START) - 1, 0, 0)
                ones_rows(1, 5)
                if ahead is not None:
                    ahead(sp)
                batch(0, 0, first=True)
                with sp.Fori(0, B // 2 - 2) as it:
                    batch(2 * it + 1, 1)
                    batch(2 * it + 2, 0)
                batch(B - 3, 1)
                batch(B - 2, 0, before_last=True)
                batch(B - 1, 1, last=True)

            def left(eng, b, m, n):
                name, part_no = ORDER[m]
                s, t = rope[name], turned[name]
                if part_no == 0:
                    eng.wait_ge(s_job_free, n + FREED)
                    eng.tensor_tensor(t[:, :], t[:, :], sin[:, :], ALU.mult).then_inc(s_rot, 1)
                    eng.wait_ge(s_rot, 2 * b + (1 if name == "k" else 2))
                    eng.tensor_tensor(s[:, :], s[:, :], t[:, :], ALU.add).then_inc(s_split, 1)
                else:
                    eng.wait_ge(s_cast, b * len(ORDER) + ORDER.index((name, part_no - 1)) + 1)
                    eng.tensor_tensor(s[:, :], s[:, :], part[name][:, part_no - 1, :], ALU.subtract)\
                        .then_inc(s_split, 1)

            @block.gpsimd
            def _(pool):
                for st in (kst[0], qst[0]):
                    pool.memset(st[64:FULL, :, :], 0.0).then_inc(s_init, 1)
                pool.wait_ge(s_init, 2)
                pool.memset(ones[:, :], 1.0).then_inc(s_init, 1)
                pool.wait_ge(s_init, 3)
                for m in POOL_SENDS:
                    pool.wait_ge(s_cast, m + 1)
                    for row in stack_rows(m):
                        pool.dma_start(qst[0][row:row + D, :, :], part["q"][:, ORDER[m][1], :])\
                            .then_inc(s_pool_st, 16)
                for st in (kst[1], qst[1]):
                    pool.memset(st[64:FULL, :, :], 0.0).then_inc(s_init, 1)
                pool.wait_ge(s_init, 5)

                def batch(b, r, first=False, last=False):
                    for g in range(NG):
                        for j in range(QT):
                            for m in POOL_AT.get((g, j), []) if not last else []:
                                left(pool, b + 1, m, number(b, first, last, 0, ORDER[m][0]))
                            if causal:
                                u0 = sum(HG // u for u in unit_heads[:j + 1])
                                pool.wait_ge(s_score_free, b * (NG * SU) + g * SU + u0 + SBANKS)
                                by_itself(pool, s_passed)
                                diag = prob[j % RING][:, :, 0:P]
                                pool.affine_select(out=diag, in_=diag, compare_op=ALU.is_ge, fill=0.0,
                                                   base=0, pattern=[[0, HG], [1, P]],
                                                   channel_multiplier=-1).then_inc(s_masked, 1)

                batch(0, 0, first=True)
                with pool.Fori(0, B // 2 - 1) as it:
                    batch(2 * it + 1, 1)
                    batch(2 * it + 2, 0)
                batch(B - 1, 1, last=True)

            @block.scalar
            def _(act):
                act.sem_inc(s_score_free, SBANKS)

                def job(name, b, r, n, count, bank=ps_x):
                    act.wait_ge(s_job, n + 1)
                    if name == "maxT" and count is not None:
                        act.wait_ge(s_mst, count * 16)
                    if name == "xT":
                        ins = act.activation(xT[:, :], ps_x[:, :], ACT.Copy)
                    elif name == "v":
                        ins = act.activation(vst[r][:, :, :, 0:D],
                                             bank[:, :].rearrange("p (t h d) -> p t h d", t=QT, h=H), ACT.Copy)
                    elif name == "maxT":
                        ins = act.activation(mrow[:, :], ps_x[0:PARTS * HG, 0:T // 2].bitcast(BF16), ACT.Copy)
                    elif name == "yT":
                        ins = act.activation(yT[:, :], ps_x[:, :], ACT.Copy)
                    ins.then_inc(s_job_free, 1)

                def batch(b, r, first=False, last=False):
                    k = 0
                    for g in range(NG):
                        for j in range(QT):
                            u0 = sum(HG // u for u in unit_heads[:j])
                            w = seen_by[j]
                            names = jobs(0, g, j, first, last)
                            for slot in range(SLOTS):
                                if slot < HG // unit_heads[j]:
                                    nu, h = unit_heads[j], slot * unit_heads[j]
                                    act.wait_ge(s_score, b * (NG * SU) + g * SU + u0 + slot + 1)
                                    if slot == 0 and not (first and g == 0):
                                        act.wait_ge(s_pv, b * (NG * QT) + g * QT + j - RING + 1)
                                    act.activation(prob[j % RING][:, h:h + nu, 0:w],
                                                   ps_s[(g * SU + u0 + slot) % SBANKS][:, 0:nu * w]
                                                   .rearrange("p (h t) -> p h t", h=nu), ACT.Exp,
                                                   scale=float(D) ** -0.5).then_inc(s_score_free, 1)
                                if (g, j, slot) in ACT_AT and not last:
                                    cast(b + 1, ACT_AT[g, j, slot])
                                if slot == SLOTS - 1 and j == 1 and not (first and g == 0):
                                    out_evac(b * NG + g - 1, number(b, first, last, g - 1, "norm") if g > 0 and not (first and g == 1)
                                             else None if first else jobs_before(b, first) - 1)
                                if 0 < slot <= len(names):
                                    name, n = names[slot - 1], jobs_before(b, first) + k
                                    k += 1
                                    if name in ("xT", "v"):
                                        job(name, b + 1, 1 - r, n, None)
                                    elif name == "maxT":
                                        job(name, None, None, n, b * NG + g + 1)
                                    elif name == "yT":
                                        job(name, b - 1, None, n, None)

                def cast(b, m):
                    name, part_no = ORDER[m]
                    if not (isinstance(b, int) and b == 0):
                        act.wait_ge(s_st[name], b * (PROD * 16))
                    act.wait_ge(s_split, b * len(ORDER) + m + 1)
                    act.activation(part[name][:, part_no, :], rope[name][:, :], ACT.Copy).then_inc(s_cast, 1)

                def out_evac(n, turned):
                    act.wait_ge(s_pv, n * QT + QT)
                    if turned is not None:
                        act.wait_ge(s_job, turned + 1)
                    act.activation(oT[:, :], ps_o[:, :], ACT.Copy).then_inc(s_oT, 1)

                job("xT", 0, 0, START.index("xT"), None)
                for m in range(len(ORDER)):
                    cast(0, m)
                act.wait_ge(s_job_free, START.index("v") + 1)
                job("v", 0, 0, START.index("v"), None, START_BANK["v"])
                job("maxT", None, None, START.index("maxT"), None)
                batch(0, 0, first=True)
                with act.Fori(0, B // 2 - 1) as it:
                    batch(2 * it + 1, 1)
                    batch(2 * it + 2, 0)
                batch(B - 1, 1, last=True)
                out_evac(G - 1, number(B - 1, False, True, NG - 1, "norm"))
                if wproj is not None:
                    job("yT", B - 1, None, jobs_before(B - 1, False) + len(batch_jobs(False, True)) + 1, None)

            @block.tensor
            def _(pe):
                def job(name, b, r, n, count, bank=ps_x):
                    pe.wait_ge(s_job_free, n + 1 if bank is ps_x else FREED)
                    if name == "xT":
                        pe.wait_ge(s_xin, (b + 1) * 16)
                        for i in range(QT):
                            last = pe.transpose(ps_x[:, P * i:P * i + P], xin[:, i, :], ident[:, :])
                    elif name in ("k", "q"):
                        last = pe.matmul(bank[:, :], weights[name][:, :], xT[:, :], start=True, stop=True)
                    elif name == "v":
                        for i in range(QT):
                            last = pe.matmul(bank[:, P * i:P * i + P], xT[:, P * i:P * i + P], weights["v"][:, :],
                                             start=True, stop=True)
                    elif name == "maxT":
                        pe.wait_ge(s_mp, (count + 1) * MP_STEPS)
                        for i in range(QT):
                            last = pe.transpose(ps_x[0:PARTS * HG, 0:T // 2].bitcast(BF16)[:, P * i:P * i + P],
                                                mpart[:, i, :, :].rearrange("p a h -> p (a h)"), identb[:, :])
                    elif name == "norm":
                        pe.wait_ge(s_oT, count + 1)
                        for i in range(QT):
                            last = pe.transpose(ps_x[:, P * i:P * i + P], oT[:, P * i:P * i + P], ident[:, :])
                    elif name == "yT":
                        for i in range(QT):
                            last = pe.transpose(ps_x[:, P * i:P * i + P], y[:, i, :], ident[:, :])
                    elif name == "proj":
                        for i in range(QT):
                            last = pe.matmul(ps_x[:, P * i:P * i + P], yT[:, P * i:P * i + P], wproj[:, :],
                                             start=True, stop=True)
                    last.then_inc(s_job, 1)

                def maxima(n, r, g, lo, hi):
                    unit = 0
                    for i in range(QT):
                        w = sees[i]
                        for u in range(HG // max_heads[i]):
                            if lo <= unit < hi:
                                pe.wait_ge(s_max_free, n * MU + unit + 1)
                                bank = ps_m[(unit + g * MU) % MBANKS]
                                mh = max_heads[i]
                                for v in range(mh):
                                    h = HG * g + u * mh + v
                                    last = pe.matmul(bank[:, v * w:v * w + w], qst[r][0:ROWS, h, P * i:P * i + P],
                                                     kst[r][0:ROWS, h, 0:w], start=True, stop=not causal)
                                    if causal:
                                        last = pe.matmul(bank[:, v * w + w - P:v * w + w], identb[:, :], mask[:, :],
                                                         start=False, stop=True)
                                last.then_inc(s_max, 1)
                            unit += 1

                def scores(b, r, g, j, u):
                    u0 = sum(HG // u for u in unit_heads[:j])
                    w, nu = seen_by[j], unit_heads[j]
                    pe.wait_ge(s_score_free, b * (NG * SU) + g * SU + u0 + u + 1)
                    pbank = ps_s[(g * SU + u0 + u) % SBANKS]
                    for v in range(nu):
                        h = HG * g + u * nu + v
                        last = pe.matmul(pbank[:, v * w:v * w + w], kst[r][:, h, P * j:P * j + P], qst[r][:, h, T - w:T],
                                         start=True, stop=True)
                    last.then_inc(s_score, 1)

                def values(b, r, g, j):
                    n = b * NG + g
                    if causal:
                        pe.wait_ge(s_masked, n * QT + j + 1)
                    else:
                        u0 = sum(HG // u for u in unit_heads[:j + 1])
                        pe.wait_ge(s_score_free, n * SU + u0 + SBANKS)
                    if j == 0:
                        pe.wait_ge(s_oT, n) if not (isinstance(n, int) and n == 0) else None
                    w = seen_by[j]
                    for h in range(HG):
                        last = pe.matmul(ps_o[VW * h:VW * h + VW, T - w:T], vst[r][:, j, HG * g + h, :],
                                         prob[j % RING][:, h, 0:w], start=(j == 0), stop=(j == QT - 1))
                    last.then_inc(s_pv, 1)

                def batch(b, r, first=False, last=False):
                    k = 0
                    for g in range(NG):
                        for j in range(QT):
                            if j == 0:
                                pe.wait_ge(s_mst, (b * NG + g + 1) * 16)
                            names = jobs(0, g, j, first, last)
                            lo, hi = MU * j // QT, MU * (j + 1) // QT
                            for slot in range(SLOTS):
                                if slot < HG // unit_heads[j]:
                                    scores(b, r, g, j, slot)
                                if (g < NG - 2 or not last) and lo + slot < hi:
                                    if (g, j, slot) == (NG - 2, 0, 0):
                                        for stack in s_st.values():
                                            pe.wait_ge(stack, (b + 2) * (PROD * 16))
                                    if g < NG - 2:
                                        maxima(b * NG + g + 2, r, g + 2, lo + slot, lo + slot + 1)
                                    else:
                                        maxima(b * NG + g + 2, 1 - r, g + 2 - NG, lo + slot, lo + slot + 1)
                                if slot == VALUES_AT:
                                    g2, j2 = (g, j - LAG) if j >= LAG else (g - 1, j - LAG + QT)
                                    if g2 >= 0:
                                        values(b, r, g2, j2)
                                    elif not first:
                                        values(b - 1, 1 - r, NG - 1, j2)
                                if 0 < slot <= len(names):
                                    name, n = names[slot - 1], jobs_before(b, first) + k
                                    k += 1
                                    if name in ("xT", "k", "q", "v"):
                                        job(name, b + 1, 1 - r, n, None)
                                    elif name == "maxT":
                                        job(name, None, None, n, b * NG + g + 1)
                                    elif name == "norm":
                                        job(name, None, None, n, b * NG + g - 1)
                                    else:
                                        job(name, b - 1, 1 - r, n, None)

                for n, name in enumerate(START[:-1]):
                    job(name, 0, 0, n, None, START_BANK.get(name, ps_x))
                pe.wait_ge(s_job_free, START.index("v") + FREED)
                for stack in s_st.values():
                    pe.wait_ge(stack, PROD * 16)
                maxima(0, 0, 0, 0, MU)
                maxima(1, 0, 1, 0, 4)
                job("maxT", None, None, len(START) - 1, 0)
                maxima(1, 0, 1, 4, MU)
                pe.wait_ge(s_ones, 16)
                pe.wait_ge(s_vinit, 4)
                batch(0, 0, first=True)
                pe.wait_ge(s_ones, 32)
                with pe.Fori(0, B // 2 - 1) as it:
                    batch(2 * it + 1, 1)
                    batch(2 * it + 2, 0)
                batch(B - 1, 1, last=True)
                for j in range(QT - LAG, QT):
                    values(B - 1, 1, NG - 1, j)
                n = jobs_before(B - 1, False) + len(batch_jobs(False, True))
                job("norm", None, None, n, G - 1)
                if wproj is not None:
                    job("yT", B - 1, 1, n + 1, None)
                    job("proj", B - 1, 1, n + 2, None)

            @block.vector
            def _(dve):
                dve.sem_inc(s_max_free, MBANKS)
                dve.sem_inc(s_job_free, 1)

                def job(name, b, r, n, count, bank=ps_x):
                    dve.wait_ge(s_job, n + 1)
                    if name in ("k", "q"):
                        if not (isinstance(b, int) and b == 0):
                            dve.wait_ge(s_cast, (b - 1) * len(ORDER) + ORDER.index((name[0], PARTS - 1)) + 1)
                        by_itself(dve, s_passed)
                        dve.stream_shuffle(turned[name][:, :], bank[:, :], SWAP)
                        dve.tensor_tensor(rope[name][:, :], bank[:, :], cos[:, :], ALU.mult).then_inc(s_job_free, 1)
                    elif name == "proj":
                        residual(b, ps_x[:, :].rearrange("p (i c) -> p i c", i=QT), n)

                def xb(b):
                    return x[:, QT * b:QT * b + QT, :] if isinstance(b, int) else x[:, bass.ds(QT * b, QT), :]

                def residual(b, add, shared):
                    done, count = (s_res, b + 1) if shared is None else (s_job_free, shared + FREED)
                    if x_dram is not None:
                        dve.wait_ge(s_xres, min(b + 3, B) * 16 if isinstance(b, int) else (b + 3) * 16)
                    dve.tensor_tensor(xb(b), xb(b), add, ALU.add).then_inc(done, 1)
                    dve.wait_ge(done, count)

                def ln_phase(b, phase):
                    layernorm_phase(dve, xb(b), xb(b), stats, mv, rs, lntmp, s_ln, b, s_passed, phase)

                def reduce_units(n, g, lo, hi):
                    unit = 0
                    for i in range(QT):
                        w = sees[i]
                        for u in range(HG // max_heads[i]):
                            if lo <= unit < hi:
                                mh = max_heads[i]
                                dve.wait_ge(s_max, n * MU + unit + 1)
                                dve.reduce_max(mx[:, g % 2, i, u * mh:u * mh + mh],
                                               ps_m[(unit + g * MU) % MBANKS][:, 0:mh * w]
                                               .rearrange("p (h t) -> p h t", h=mh), AX.X)\
                                    .then_inc(s_max_free, 1)
                            unit += 1

                def split_max(n, g, step, turned=None):
                    left = [mx[:, g % 2, :, :], rest[:, 0, :, :], rest[:, 1, :, :]]
                    if step == 0:
                        dve.wait_ge(s_max_free, (n + 1) * MU + MBANKS)
                        if turned is not None:
                            dve.wait_ge(s_job, turned + 1)
                    else:
                        dve.wait_ge(s_mp, n * MP_STEPS + step)
                    i = step // 2
                    if step % 2 == 0:
                        dve.tensor_scalar(mpart[:, :, i, :], left[i], -1.0, None, ALU.mult).then_inc(s_mp, 1)
                    else:
                        dve.tensor_tensor(left[i + 1], left[i], mpart[:, :, i, :], ALU.add).then_inc(s_mp, 1)

                def batch(b, r, first=False, last=False):
                    k = 0
                    ln_slot = None
                    for g in range(NG):
                        for j in range(QT):
                            names = jobs(0, g, j, first, last)
                            lo, hi = MU * j // QT, MU * (j + 1) // QT
                            for slot in range(SLOTS):
                                taken = g < NG - 2 or not last
                                if taken and lo + slot < hi:
                                    reduce_units(b * NG + g + 2, (g + 2) % NG, lo + slot, lo + slot + 1)
                                    if lo + slot == MU - 1:
                                        dve.wait_ge(s_job, number(b, first, last, g, "maxT") + 1)
                                if j == 0 and not (first and g == 0) and not (last and g > NG - 2):
                                    for step in [slot] if slot < SLOTS - 1 else range(slot, MP_STEPS):
                                        split_max(b * NG + g + 1, (g + 1) % NG, step)
                                if ln_slot is not None and ln_slot < LN_PHASES:
                                    ln_phase(b - 1, ln_slot)
                                    ln_slot += 1
                                if 0 < slot <= len(names):
                                    name, n = names[slot - 1], jobs_before(b, first) + k
                                    k += 1
                                    if name in ("k", "q"):
                                        job(name, b + 1, None, n, None)
                                    elif name == "norm":
                                        norm_job(n, b, g - 1, first)
                                    elif name == "proj":
                                        job(name, b - 1, None, n, None)
                                    if name == "proj" or (name == "norm" and g == 0 and wproj is None):
                                        ln_slot = 0

                def norm_job(n, b, g, first):
                    count = b * NG + g
                    bb, gg = (b, g) if g >= 0 else (b - 1, NG - 1)
                    heads = ps_x[:, :].rearrange("p (i h v) -> p i h v", i=QT, h=HG)
                    dve.wait_ge(s_job, n + 1)
                    dve.reciprocal(rden[:, :, :], heads[:, :, :, D]).then_inc(s_norm, 1)
                    dve.wait_ge(s_norm, count + 1)
                    dve.tensor_tensor(y[:, :, gg * HG * D:(gg + 1) * HG * D].rearrange("p i (h d) -> p i h d", h=HG),
                                      heads[:, :, :, 0:D],
                                      rden[:, :, :].unsqueeze(3).to_broadcast([P, QT, HG, D]),
                                      ALU.mult).then_inc(s_job_free, 1)
                    if gg == NG - 1 and wproj is None:
                        dve.wait_ge(s_job_free, n + FREED)
                        residual(bb, y[:, :, :], None)

                for name, parts in (("k", [0]), ("q", [1, 2, 3, 4, 5])):
                    job(name, 0, None, START.index(name), None, START_BANK[name])
                    for m in parts:
                        left(dve, 0, m, START.index(ORDER[m][0]))
                for i in range(2):
                    dve.memset(vst[i][:, :, :, D + 1:VW], 0.0).then_inc(s_vinit, 1)
                    dve.memset(vst[i][:, :, :, D:D + 1], 1.0).then_inc(s_vinit, 1)
                reduce_units(0, 0, 0, MU)
                for step in range(MP_STEPS):
                    split_max(0, 0, step)
                reduce_units(1, 1, 0, MU)
                for step in range(MP_STEPS):
                    split_max(1, 1, step, len(START) - 1)
                batch(0, 0, first=True)
                with dve.Fori(0, B // 2 - 1) as it:
                    batch(2 * it + 1, 1)
                    batch(2 * it + 2, 0)
                batch(B - 1, 1, last=True)
                n = jobs_before(B - 1, False) + len(batch_jobs(False, True))
                norm_job(n, B - 1, NG - 1, False)
                if wproj is not None:
                    job("proj", B - 1, None, n + 2, None)
                for phase in range(LN_PHASES):
                    ln_phase(B - 1, phase)


MP_STEPS = 5


I32 = mybir.dt.int32
FF = 512
FB = FF // P
E = 7
CAPACITY = 366
ET = 3
SLOTS = ET * P
ST = E * ET
TOP = 2
TC = TOP * NT
TOKENS = NT * P
ROWS_ALL = TOKENS + ET * P
PAY = 3 + PARTS
PAIR = 2 * QT
AHEAD = 3
BEFORE = 6


def moe_ffn(nc, x, ident, identb, dram, tag="f0"):
    with ExitStack() as ctx:
        def psum(name, shape, dt=F32):
            return ctx.enter_context(nc.psum_tensor(tag + name, shape, dt))

        def sbuf(name, shape, dt=F32):
            return ctx.enter_context(nc.sbuf_tensor(tag + name, shape, dt))

        def sem(name):
            return ctx.enter_context(nc.semaphore(tag + name))

        nrm = [sbuf(f"nrm{i}", [P, QT, C]) for i in range(2)]
        hT_hi, hT_lo = sbuf("hT_hi", [C, TOKENS], F32R), sbuf("hT_lo", [C, TOKENS], F32R)
        ws_hi = [sbuf(f"ws_hi{i}", [C, FF], F32R) for i in range(2)]
        ws_lo = [sbuf(f"ws_lo{i}", [C, FF], F32R) for i in range(2)]
        we_hi = [[sbuf(f"we_hi{r}{i}", [C, FF], F32R) for i in range(2)] for r in range(2)]
        we_lo = [[sbuf(f"we_lo{r}{i}", [C, FF], F32R) for i in range(2)] for r in range(2)]
        xe_hi = [sbuf(f"xe_hi{i}", [C, SLOTS], F32R) for i in range(2)]
        xe_lo = [sbuf(f"xe_lo{i}", [C, SLOTS], F32R) for i in range(2)]
        ln_g = sbuf("ln_g", [C, 1])
        ln_b = sbuf("ln_b", [C, 1])
        wr = sbuf("wr", [C, E])
        w1 = [sbuf(f"w1_{i}", [C, FF]) for i in range(2)]
        w3 = [sbuf(f"w3_{i}", [C, FF]) for i in range(2)]
        w2 = [sbuf(f"w2_{i}", [P, FB, C]) for i in range(2)]
        w1s, w3s, w2s = sbuf("w1s", [C, FF]), sbuf("w3s", [C, FF]), sbuf("w2s", [P, FB, C])
        logit = sbuf("logit", [P, NT, E])
        stats, mv = sbuf("stats", [P, PAIR, 6]), sbuf("mv", [P, PAIR, 2])
        lntmp = sbuf("lntmp", [P, 4, PAIR])
        rs, shift = sbuf("rs", [P, NT]), sbuf("shift", [P, NT])
        stats2, mv2, lntmp2 = sbuf("stats2", [P, NT // 2, 6]), sbuf("mv2", [P, NT // 2, 2]), sbuf("lntmp2", [P, 4, NT // 2])
        rs2, shift2 = sbuf("rs2", [P, NT]), sbuf("shift2", [P, NT])
        stage = [sbuf(f"stage{i}", [C, T]) for i in range(2)]
        gatea = [sbuf(f"gatea{i}", [P, T]) for i in range(2)]
        copyb = [sbuf(f"copyb{i}", [P, T]) for i in range(2)]
        hid = sbuf("hid", [P, FB, T])
        sharedT = sbuf("sharedT", [C, TOKENS])
        iota_e = sbuf("iota_e", [P, E])
        iota_lo = sbuf("iota_lo", [P, P])
        iota_hi = sbuf("iota_hi", [P, ST])
        iota_t = sbuf("iota_t", [P, NT])
        iota_p = sbuf("iota_p", [P, 1])
        spare = sbuf("spare", [P, ST])
        tri = sbuf("tri", [P, P], BF16)
        onesb = sbuf("onesb", [P, P], BF16)
        top = sbuf("top", [P, TOP, NT])
        hot = sbuf("hot", [P, TOP, NT, E])
        hotb = sbuf("hotb", [P, TOP, NT, E], BF16)
        wk = [sbuf(f"wk{i}", [P, TOP, NT, E]) for i in range(3)]
        expert = sbuf("expert", [P, TOP, NT])
        gate = sbuf("gate", [P, TOP, NT])
        grest = [sbuf(f"grest{i}", [P, TOP, NT]) for i in range(2)]
        gpart = sbuf("gpart", [P, PARTS, TOP, NT], BF16)
        small = [sbuf(f"small{i}", [P, TC]) for i in range(4)]
        smalli = [sbuf(f"smalli{i}", [P, TC], I32) for i in range(3)]
        lohot = sbuf("lohot", [P, TC, P], BF16)
        ye = lohot[:, :, :].rearrange("p k c -> p (k c)").bitcast(F32)
        pay = sbuf("pay", [P, TC, PAY, ST], BF16)
        slot = sbuf("slot", [P, PAY, ST])
        sgate = sbuf("sgate", [P, ST])
        stmp = [sbuf(f"stmp{i}", [P, ST]) for i in range(3)]
        token = sbuf("token", [P, ST], I32)
        xg = [sbuf(f"xg{i}", [P, ET, C]) for i in range(2)]
        xeT = [sbuf(f"xeT{i}", [C, SLOTS]) for i in range(2)]
        yeT = sbuf("yeT", [C, SLOTS])
        zero = sbuf("zero", [P, C])
        ps_a = [psum(f"ps_a{i}", [P, T]) for i in range(2)]
        ps_b = [psum(f"ps_b{i}", [P, T]) for i in range(2)]
        ps_y = psum("ps_y", [P, T])
        ps_t = psum("ps_t", [P, T])
        ps_r = psum("ps_r", [P, T])
        ps_r2 = psum("ps_r2", [P, T])

        s_w = sem("w")
        s_we = [sem(f"we{i}") for i in range(2)]
        s_w2 = [sem(f"w2{i}") for i in range(2)]
        s_ln = sem("ln")
        s_nrm = sem("nrm")
        s_nout = [sem(f"nout{i}") for i in range(2)]
        s_nT = sem("nT")
        s_hT = sem("hT")
        s_hlo = sem("hlo")
        s_whi = sem("whi")
        s_wlo0 = sem("wlo0")
        s_wlo = sem("wlo")
        s_xlo = sem("xlo")
        s_lg = sem("lg")
        s_lge = sem("lge")
        s_const = sem("const")
        s_zero = sem("zero")
        s_rt = sem("rt")
        s_exp = sem("exp")
        s_cnt = sem("cnt")
        s_map = sem("map")
        s_up = sem("up")
        s_gate = sem("gate")
        s_hid = sem("hid")
        s_down = sem("down")
        s_y = sem("y")
        s_gath = [sem(f"gath{i}") for i in range(2)]
        s_xgT = sem("xgT")
        s_xe = sem("xe")
        s_yeT = sem("yeT")
        s_ye = sem("ye")
        s_scat = sem("scat")
        s_row = sem("row")
        s_start = sem("start")
        s_sT = sem("sT")
        s_acc = [sem(f"acc{i}") for i in range(B // 2)]
        s_sum = sem("sum")
        s_psum = sem("psum")
        s_ln2 = sem("ln2")
        s_passed = sem("passed")

        def routed(p):
            return hT_hi[:, 2 * p * T:2 * (p + 1) * T].bitcast(F32).rearrange("q (i c) -> q i c", c=C)

        def shared_rows(c):
            return sharedT[:, c * T:(c + 1) * T].rearrange("q (i c) -> q i c", c=C)

        CONSTS = 10
        U_EXP = BEFORE * FB
        U_END = U_EXP + E * FB
        UNITS = U_END + (B - BEFORE) * FB

        with nc.Block() as block:
            @block.sync
            def _(sp):
                for dst, src in ((ln_g[:, :], dram["ln_g"].rearrange("(c a) -> c a", a=1)),
                                 (ln_b[:, :], dram["ln_b"].rearrange("(c a) -> c a", a=1)),
                                 (wr[:, :], dram["Wr"]), (w1s[:, :], dram["W1s"]), (w3s[:, :], dram["W3s"]),
                                 (w2s[:, :, :], dram["W2s"].rearrange("(k p) d -> p k d", p=P))):
                    sp.dma_start(dst, src).then_inc(s_w, 16)

                def expert_weights(e, r):
                    sp.dma_start(w1[r][:, :], dram["W1"][e]).then_inc(s_we[r], 16)
                    sp.dma_start(w3[r][:, :], dram["W3"][e]).then_inc(s_we[r], 16)

                def expert_down(e, r):
                    sp.dma_start(w2[r][:, :, :], dram["W2"][e].rearrange("(k p) d -> p k d", p=P)).then_inc(s_w2[r], 16)

                for e in range(2):
                    expert_weights(e, e)
                    expert_down(e, e)
                sp.wait_ge(s_const, 1)
                sp.dma_start(dram["acc"][BEFORE * T:, :].rearrange("(n p) c -> p n c", p=P),
                             zero[:, :].unsqueeze(1).to_broadcast([P, (ROWS_ALL - BEFORE * T) // P, C]))\
                    .then_inc(s_zero, 16)
                sp.dma_start(dram["normed"][TOKENS:, :].rearrange("(n p) c -> p n c", p=P),
                             zero[:, :].unsqueeze(1).to_broadcast([P, ET, C])).then_inc(s_zero, 16)

                def rows_out(c, r):
                    sp.wait_ge(s_nrm, c + 1)
                    by_itself(sp, s_passed)
                    sp.dma_start(dram["normed_rows"](c), nrm[r][:, :, :]).then_inc(s_nout[r], 16)

                with sp.Fori(0, B // 2) as it:
                    rows_out(2 * it, 0)
                    rows_out(2 * it + 1, 1)
                for c in range(BEFORE):
                    sp.wait_ge(s_row, c + 1)
                    sp.dma_start(dram["acc"][c * T:(c + 1) * T, :].rearrange("(i p) c -> p i c", p=P),
                                 shared_rows(c)).then_inc(s_start, 16)
                for e in range(2, E + 1):
                    if e < E:
                        sp.wait_ge(*(s_wlo0, 2) if e == 2 else (s_wlo, e - 2))
                        expert_weights(e, e % 2)
                    if e > 2:
                        sp.wait_ge(s_down, U_EXP + (e - 2) * FB)
                        expert_down(e - 1, (e - 1) % 2)
                sp.wait_ge(s_scat, ST * 16)
                for p in range(B // 2):
                    if 2 * p + 1 >= BEFORE:
                        sp.wait_ge(s_down, UNITS)
                    sp.dma_start(routed(p), dram["acc"][2 * p * T:2 * (p + 1) * T, :]
                                 .rearrange("(i p) c -> p i c", p=P)).then_inc(s_acc[p], 16)

            @block.gpsimd
            def _(pool):
                steps = [0]

                def const(ins):
                    steps[0] += 1
                    ins.then_inc(s_const, 1)

                const(pool.memset(zero[:, :], 0.0))
                const(pool.memset(tri[:, :], 1.0))
                const(pool.memset(onesb[:, :], 1.0))
                pool.wait_ge(s_const, steps[0])
                const(pool.affine_select(out=tri[:, :], in_=tri[:, :], compare_op=ALU.is_ge, fill=0.0, base=0,
                                         pattern=[[1, P]], channel_multiplier=-1))
                for dst, n in ((iota_e, E), (iota_lo, P), (iota_hi, ST), (iota_t, NT)):
                    const(pool.iota(dst[:, :], pattern=[[1, n]], base=0, channel_multiplier=0,
                                    allow_small_or_imprecise_dtypes=True))
                const(pool.iota(iota_p[:, :], pattern=[[1, 1]], base=0, channel_multiplier=1,
                                allow_small_or_imprecise_dtypes=True))
                const(pool.iota(spare[:, :], pattern=[[0, E], [P, ET]], base=TOKENS, channel_multiplier=1,
                                allow_small_or_imprecise_dtypes=True))
                assert steps[0] == CONSTS

                def product(u, f):
                    pool.wait_ge(s_gate, u + 1)
                    by_itself(pool, s_passed)
                    if not (isinstance(u, int) and u < FB):
                        pool.wait_ge(s_down, u - FB + 1)
                    pool.tensor_tensor(hid[:, f, :], gatea[f % 2][:, :], copyb[f % 2][:, :], ALU.mult)\
                        .then_inc(s_hid, 1)

                def low(c):
                    pool.wait_ge(s_hT, c + 1)
                    cols = slice(c * T, (c + 1) * T)
                    pool.tensor_tensor(hT_lo[:, cols], stage[c % 2][:, :], hT_hi[:, cols].bitcast(F32), ALU.subtract)\
                        .then_inc(s_hlo, 1)

                def weights_low(n, raw, hi, lo):
                    pool.wait_ge(s_whi, n)
                    for i in range(2):
                        ins = pool.tensor_tensor(lo[i][:, :], raw[i][:, :], hi[i][:, :].bitcast(F32), ALU.subtract)
                    ins.then_inc(s_wlo0, 1)

                weights_low(1, (w1s, w3s), ws_hi, ws_lo)
                low(0)
                low(1)
                weights_low(2, (w1[0], w3[0]), we_hi[0], we_lo[0])
                for u in range(2 * FB):
                    product(u, u % FB)
                    if u + 2 < B:
                        low(u + 2)
                with pool.Fori(2, BEFORE) as c:
                    for f in range(FB):
                        product(c * FB + f, f)
                pool.wait_ge(s_rt, RT_STEPS)
                for stored in s_nout:
                    pool.wait_ge(stored, B // 2 * 16)
                pool.wait_ge(s_zero, 32)

                def gather(e, i):
                    if e >= 2 and i == 0:
                        pool.wait_ge(s_xgT, e - 1)
                    k = e * ET + i
                    pool.indirect_dma_start(xg[e % 2][:, i, :], None, dram["normed"],
                                            bass.IndirectOffsetOnAxis(ap=token[:, k:k + 1], axis=0))\
                        .then_inc(s_gath[e % 2], 16)

                def scatter(e, i):
                    if i == 0:
                        pool.wait_ge(s_ye, e + 1)
                        if e:
                            pool.wait_ge(s_scat, e * (ET * 16))
                    k = e * ET + i
                    pool.indirect_dma_start(dram["acc"],
                                            bass.IndirectOffsetOnAxis(ap=token[:, k:k + 1], axis=0),
                                            ye[:, k * C:(k + 1) * C], None, compute_op=ALU.add).then_inc(s_scat, 16)

                for e in range(AHEAD):
                    for i in range(ET):
                        gather(e, i)
                pool.wait_ge(s_start, BEFORE * 16)
                for e in range(E):
                    for i in range(ET):
                        if e + AHEAD < E:
                            gather(e + AHEAD, i)
                    for i in range(ET):
                        scatter(e, i)
                for p in range(1, B // 2, 2):
                    pair = x[:, p * PAIR:(p + 1) * PAIR, :]
                    pool.wait_ge(s_acc[p], 16)
                    pool.wait_ge(s_sum, B - BEFORE)
                    pool.tensor_tensor(pair, pair, routed(p), ALU.add).then_inc(s_psum, 1)

            @block.scalar
            def _(act):
                act.wait_ge(s_w, 6 * 16)

                def norm(c):
                    r = c % 2
                    act.wait_ge(s_ln, (c // 2 + 1) * scale_steps(PAIR))
                    if c >= 2:
                        act.wait_ge(s_nT, c - 1)
                        act.wait_ge(s_nout[r], c // 2 * 16)
                    for i in range(QT):
                        k = c * QT + i
                        last = act.activation(nrm[r][:, i, :], x[:, k, :], ACT.Identity, scale=rs[:, k:k + 1],
                                              bias=shift[:, k:k + 1])
                    last.then_inc(s_nrm, 1)

                def turned(c):
                    act.wait_ge(s_nT, c + 1)
                    if c >= 2:
                        act.wait_ge(s_lg, c - 1)
                        act.wait_ge(s_hlo, c - 1)
                    act.activation(stage[c % 2][:, :], ps_t[:, :], ACT.Identity, scale=ln_g[:, 0:1], bias=ln_b[:, 0:1])\
                        .then_inc(s_passed, 1)
                    act.activation(hT_hi[:, c * T:(c + 1) * T], ps_t[:, :], ACT.Identity, scale=ln_g[:, 0:1],
                                   bias=ln_b[:, 0:1]).then_inc(s_hT, 1)

                def logits(c):
                    act.wait_ge(s_lg, c + 1)
                    act.activation(logit[:, c * QT:(c + 1) * QT, :],
                                   (ps_r, ps_r2)[c % 2][:, 0:QT * E].rearrange("p (i e) -> p i e", i=QT), ACT.Copy)\
                        .then_inc(s_lge, 1)

                def unit(u, f, w, both):
                    act.wait_ge(s_up, u + 1)
                    if not (isinstance(u, int) and u < 2):
                        act.wait_ge(s_hid, u - 1)
                    if both:
                        act.activation(copyb[f % 2][:, 0:w], ps_b[f % 2][:, 0:w], ACT.Copy).then_inc(s_passed, 1)
                    act.activation(gatea[f % 2][:, 0:w], ps_a[f % 2][:, 0:w], ACT.Silu).then_inc(s_gate, 1)

                def shared_out(c, n):
                    act.wait_ge(s_down, n)
                    act.activation(sharedT[:, bass.ds(c * T, T)], ps_y[:, :], ACT.Copy).then_inc(s_y, 1)

                def weights_high(raw, hi):
                    for i in range(2):
                        ins = act.activation(hi[i][:, :], raw[i][:, :], ACT.Copy)
                    ins.then_inc(s_whi, 1)

                norm(0)
                weights_high((w1s, w3s), ws_hi)
                norm(1)
                turned(0)
                turned(1)
                norm(2)
                logits(0)
                logits(1)
                norm(3)
                act.wait_ge(s_we[0], 32)
                weights_high((w1[0], w3[0]), we_hi[0])
                for c in range(2):
                    for f in range(FB):
                        unit(c * FB + f, f, T, True)
                        k = c * FB + f + 2
                        if k < B:
                            turned(k)
                        if 2 < k <= B:
                            logits(k - 1)
                        if k + 2 < B:
                            norm(k + 2)
                        if f == 1 and c:
                            shared_out(c - 1, c * FB)
                for f in range(FB):
                    unit(2 * FB + f, f, T, True)
                    if f == 1:
                        shared_out(1, 2 * FB)
                        act.wait_ge(s_rt, RT_DIFF)
                        act.activation(gate[:, 1, :], small[0][:, 0:NT], ACT.Exp).then_inc(s_exp, 1)
                with act.Fori(3, BEFORE) as c:
                    for f in range(FB):
                        unit(c * FB + f, f, T, True)
                        if f == 1:
                            shared_out(c - 1, c * FB)
                shared_out(BEFORE - 1, BEFORE * FB)
                for c in range(BEFORE):
                    act.wait_ge(s_sT, c + 1)
                    act.activation(sharedT[:, c * T:(c + 1) * T], (ps_a + ps_b)[c % 4][:, :], ACT.Copy).then_inc(s_row, 1)

                def rows(e, r):
                    act.wait_ge(s_xgT, e + 1)
                    if not (isinstance(e, int) and e < 2):
                        act.wait_ge(s_xlo, e - 1)
                    act.activation(xeT[r][:, :], ps_t[:, 0:SLOTS], ACT.Identity, scale=ln_g[:, 0:1],
                                   bias=ln_b[:, 0:1]).then_inc(s_passed, 1)
                    act.activation(xe_hi[r][:, :], ps_t[:, 0:SLOTS], ACT.Identity, scale=ln_g[:, 0:1],
                                   bias=ln_b[:, 0:1]).then_inc(s_xe, 1)

                def expert_out(e):
                    act.wait_ge(s_down, U_EXP + (e + 1) * FB)
                    if not (isinstance(e, int) and e == 0):
                        act.wait_ge(s_yeT, e)
                    act.activation(yeT[:, :], ps_y[:, 0:SLOTS], ACT.Copy).then_inc(s_y, 1)

                def expert(e, r, n, first=False, last=False):
                    loads = n + (1 if r else 0)
                    for f in range(FB):
                        unit(U_EXP + e * FB + f, f, SLOTS, False)
                        if f == 0 and not last:
                            act.wait_ge(s_we[1 - r], loads * 32)
                            weights_high((w1[1 - r], w3[1 - r]), we_hi[1 - r])
                        if f == 1:
                            if not first:
                                expert_out(e - 1)
                            if not last:
                                rows(e + 1, 1 - r)

                rows(0, 0)
                expert(0, 0, 1, first=True)
                with act.Fori(0, (E - 1) // 2 - 1) as it:
                    expert(2 * it + 1, 1, it + 1)
                    expert(2 * it + 2, 0, it + 2)
                expert(E - 2, 1, (E - 1) // 2)
                expert(E - 1, 0, (E + 1) // 2, last=True)
                for c in range(BEFORE, B):
                    for f in range(FB):
                        unit(E * FB + c * FB + f, f, T, False)
                        if f == 1:
                            if c == BEFORE:
                                expert_out(E - 1)
                            else:
                                shared_out(c - 1, c * FB + E * FB)
                shared_out(B - 1, UNITS)
                for half in range(2):
                    act.wait_ge(s_ln2, (half + 1) * scale_steps(NT // 2))
                    for k in range(half * NT // 2, NT // 2 if half == 0 else NT - PAIR):
                        act.activation(x[:, k, :], x[:, k, :], ACT.Identity, scale=rs2[:, k:k + 1],
                                       bias=shift2[:, k:k + 1]).then_inc(s_passed, 1)

            @block.tensor
            def _(pe):
                pe.wait_ge(s_w, 6 * 16)

                def turn_rows(c):
                    pe.wait_ge(s_nrm, c + 1)
                    if c:
                        pe.wait_ge(s_hT, c)
                    for i in range(QT):
                        last = pe.transpose(ps_t[:, P * i:P * i + P], nrm[c % 2][:, i, :], ident[:, :])
                    last.then_inc(s_nT, 1)

                def logits(c):
                    pe.wait_ge(s_hT, c + 1)
                    if c >= 2:
                        pe.wait_ge(s_lge, c - 1)
                    for i in range(QT):
                        last = pe.matmul((ps_r, ps_r2)[c % 2][:, E * i:E * i + E], stage[c % 2][:, P * i:P * i + P],
                                         wr[:, :], start=True, stop=True)
                    last.then_inc(s_lg, 1)

                def up(u, f, w_hi, w_lo, hi, lo, w):
                    if not (isinstance(u, int) and u < 2):
                        pe.wait_ge(s_hid, u - 1)
                    for i, bank in enumerate((ps_a[f % 2], ps_b[f % 2])):
                        wh, wl = (part[i][:, P * f:P * f + P] for part in (w_hi, w_lo))
                        pe.matmul(bank[:, 0:w], wh, hi, start=True, stop=False)
                        pe.matmul(bank[:, 0:w], wl, hi, start=False, stop=False)
                        last = pe.matmul(bank[:, 0:w], wh, lo, start=False, stop=True)
                    last.then_inc(s_up, 1)

                def down(u, f, wd, w, outs):
                    pe.wait_ge(s_hid, u + 1)
                    if f == 0 and not (isinstance(outs, int) and outs == 0):
                        pe.wait_ge(s_y, outs)
                    pe.matmul(ps_y[:, 0:w], wd[:, f, :], hid[:, f, 0:w], start=(f == 0), stop=(f == FB - 1))\
                        .then_inc(s_down, 1)

                def shared(c, u, outs, before, between=None):
                    cols = bass.ds(c * T, T)
                    pe.wait_ge(s_hlo, min(c + 1, B) if isinstance(c, int) else c + 1)
                    for f in range(FB):
                        up(u + f, f, ws_hi, ws_lo, hT_hi[:, cols], hT_lo[:, cols], T)
                        if f >= 2:
                            down(u + f - 2, f - 2, w2s, T, outs)
                        elif before is not None:
                            down(u + f - 2, f + 2, *before, None)
                        if between is not None:
                            between(f)

                def rest(u, wd, w):
                    for f in (2, 3):
                        down(u + f - FB, f, wd, w, None)

                def turn(c, bank):
                    for i in range(QT):
                        last = pe.transpose(bank[:, P * i:P * i + P], sharedT[:, c * T + P * i:c * T + P * i + P],
                                            ident[:, :])
                    last.then_inc(s_sT, 1)

                def ready(c):
                    def between(f):
                        k = c * FB + f + 2
                        if k < B:
                            turn_rows(k)
                        if 2 < k <= B:
                            logits(k - 1)
                    return between

                def counts(f):
                    if f == 1:
                        pe.wait_ge(s_const, CONSTS)
                        pe.wait_ge(s_rt, RT_HOT)
                        pe.matmul(ps_r[:, 0:TC * E], tri[:, :], hotb[:, :, :, :].rearrange("p s t e -> p (s t e)"),
                                  start=True, stop=True)
                        pe.matmul(ps_r2[:, 0:TC * E], onesb[:, :], hotb[:, :, :, :].rearrange("p s t e -> p (s t e)"),
                                  start=True, stop=True).then_inc(s_cnt, 1)

                turn_rows(0)
                turn_rows(1)
                logits(0)
                logits(1)
                pe.wait_ge(s_wlo0, 1)
                for c in range(2):
                    shared(c, c * FB, c, (w2s, T) if c else None, ready(c))
                shared(2, 2 * FB, 2, (w2s, T), counts)
                with pe.Fori(3, BEFORE) as c:
                    shared(c, c * FB, c, (w2s, T))
                rest(U_EXP, w2s, T)
                pe.wait_ge(s_y, BEFORE)
                for c in range(BEFORE):
                    if c >= 4:
                        pe.wait_ge(s_row, c - 3)
                    turn(c, (ps_a + ps_b)[c % 4])
                pe.wait_ge(s_rt, RT_PAY)
                for k in range(TC):
                    last = pe.matmul(ps_t[:, 0:PAY * ST], lohot[:, k, :], pay[:, k, :, :].rearrange("p a h -> p (a h)"),
                                     start=(k == 0), stop=(k == TC - 1))
                last.then_inc(s_map, 1)

                def rows(e, r, n):
                    pe.wait_ge(s_gath[r], n * ET * 16)
                    if isinstance(e, int) and e == 0:
                        pe.wait_ge(s_rt, RT_SLOT)
                    for i in range(ET):
                        last = pe.transpose(ps_t[:, P * i:P * i + P], xg[r][:, i, :], ident[:, :])
                    last.then_inc(s_xgT, 1)

                def back(e):
                    pe.wait_ge(s_y, BEFORE + e + 1)
                    if not (isinstance(e, int) and e == 0):
                        pe.wait_ge(s_ye, e)
                    for i in range(ET):
                        last = pe.transpose(ps_r[:, P * i:P * i + P], yeT[:, P * i:P * i + P], ident[:, :])
                    last.then_inc(s_yeT, 1)

                def expert(e, r, n, last=False, first=False):
                    u = U_EXP + e * FB
                    for f in range(FB):
                        if f == 0:
                            pe.wait_ge(s_xlo, e + 1)
                            if isinstance(e, int) and e == 0:
                                pe.wait_ge(s_wlo0, 2)
                            else:
                                pe.wait_ge(s_wlo, e)
                        up(u + f, f, we_hi[r], we_lo[r], xe_hi[r][:, :], xe_lo[r][:, :], SLOTS)
                        if f == 2:
                            pe.wait_ge(s_w2[r], n * 16)
                        if f >= 2:
                            down(u + f - 2, f - 2, w2[r], SLOTS, BEFORE + e)
                        elif not first:
                            down(u + f - 2, f + 2, w2[1 - r], SLOTS, None)
                        if f == 1 and not last:
                            rows(e + 1, 1 - r, n + (1 if r else 0))
                        if f == 3 and not first:
                            back(e - 1)

                rows(0, 0, 1)
                pe.wait_ge(s_row, BEFORE)
                expert(0, 0, 1, first=True)
                with pe.Fori(0, (E - 1) // 2 - 1) as it:
                    expert(2 * it + 1, 1, it + 1)
                    expert(2 * it + 2, 0, it + 2)
                expert(E - 2, 1, (E - 1) // 2)
                expert(E - 1, 0, (E + 1) // 2, last=True)

                def behind(f):
                    if f == 3:
                        back(E - 1)

                def turn_first(f):
                    if f == 3:
                        pe.wait_ge(s_y, BEFORE + E + 1)
                        turn(BEFORE, ps_r2)

                assert B == BEFORE + 2
                shared(BEFORE, U_END, BEFORE + E, (w2[0], SLOTS), behind)
                shared(B - 1, U_END + FB, B - 1 + E, (w2s, T), turn_first)
                rest(UNITS, w2s, T)
                pe.wait_ge(s_y, B + E)
                pe.wait_ge(s_sum, 1)
                turn(B - 1, ps_r2)

            def route(dve):
                steps = [0]

                def step(ins, at=None):
                    steps[0] += 1
                    ins.then_inc(s_rt, 1)
                    dve.wait_ge(s_rt, steps[0])
                    assert at is None or at == steps[0], (at, steps[0])

                def over_e(ap):
                    return ap.unsqueeze(2).to_broadcast([P, NT, E])

                def e_row():
                    return iota_e[:, :].unsqueeze(1).to_broadcast([P, NT, E])

                dve.wait_ge(s_const, CONSTS)
                dve.wait_ge(s_lge, B)
                left = logit[:, :, :]
                for s in range(TOP):
                    step(dve.reduce_max(top[:, s, :], left, AX.X))
                    a, b = wk[0][:, 0, :, :], wk[1][:, 0, :, :]
                    step(dve.tensor_tensor(a, left, over_e(top[:, s, :]), ALU.is_lt))
                    step(dve.scalar_tensor_tensor(b, a, 8.0, e_row(), ALU.mult, ALU.add))
                    step(dve.tensor_reduce(expert[:, s, :], b, AX.X, ALU.min))
                    step(dve.tensor_tensor(hot[:, s, :, :], e_row(), over_e(expert[:, s, :]), ALU.is_equal))
                    if s == 0:
                        left = wk[2][:, 0, :, :]
                        step(dve.scalar_tensor_tensor(left, hot[:, 0, :, :], -3.0e38, logit[:, :, :], ALU.mult, ALU.add))
                step(dve.tensor_copy(hotb[:, :, :, :], hot[:, :, :, :]), RT_HOT)
                step(dve.tensor_tensor(small[0][:, 0:NT], top[:, 1, :], top[:, 0, :], ALU.subtract), RT_DIFF)
                dve.wait_ge(s_cnt, 1)
                flat = [w[:, :, :, :].rearrange("p s t e -> p (s t) e") for w in wk]
                step(dve.tensor_copy(flat[0], ps_r2[:, 0:TC * E].rearrange("p (k e) -> p k e", e=E)))
                cur, nxt, d = 0, 1, 1
                while d < TC:
                    step(dve.tensor_copy(flat[nxt][:, 0:d, :], flat[cur][:, 0:d, :]))
                    step(dve.tensor_tensor(flat[nxt][:, d:TC, :], flat[cur][:, d:TC, :], flat[cur][:, 0:TC - d, :], ALU.add))
                    cur, nxt, d = nxt, cur, 2 * d
                step(dve.tensor_tensor(flat[cur], flat[cur], ps_r2[:, 0:TC * E].rearrange("p (k e) -> p k e", e=E), ALU.subtract))
                step(dve.tensor_tensor(flat[cur], flat[cur], ps_r[:, 0:TC * E].rearrange("p (k e) -> p k e", e=E), ALU.add))
                hotf = hot[:, :, :, :].rearrange("p s t e -> p (s t) e")
                step(dve.tensor_tensor(flat[2], flat[cur], hotf, ALU.mult))
                rank = small[1]
                step(dve.tensor_reduce(rank[:, :], flat[2], AX.X, ALU.add))
                pos, lo, hi = smalli
                step(dve.tensor_scalar(pos[:, :], rank[:, :], -1.0, None, ALU.add))
                step(dve.tensor_scalar(lo[:, :], pos[:, :], P - 1, None, ALU.bitwise_and))
                step(dve.tensor_scalar(hi[:, :], pos[:, :], P.bit_length() - 1, None, ALU.arith_shift_right))
                lof, hif = small[2], small[3]
                step(dve.tensor_copy(lof[:, :], lo[:, :]))
                step(dve.tensor_copy(hif[:, :], hi[:, :]))
                step(dve.scalar_tensor_tensor(hif[:, :], expert[:, :, :].rearrange("p s t -> p (s t)"), float(ET),
                                              hif[:, :], ALU.mult, ALU.add))
                step(dve.tensor_scalar(rank[:, :], rank[:, :], float(CAPACITY), 1000.0, ALU.is_gt, ALU.mult))
                step(dve.tensor_tensor(hif[:, :], hif[:, :], rank[:, :], ALU.add))
                dve.wait_ge(s_exp, 1)
                step(dve.tensor_scalar(gate[:, 0, :], gate[:, 1, :], 1.0, None, ALU.add))
                step(dve.reciprocal(gate[:, 0, :], gate[:, 0, :]))
                step(dve.tensor_tensor(gate[:, 1, :], gate[:, 1, :], gate[:, 0, :], ALU.mult))
                rests = [gate, grest[0], grest[1]]
                for i in range(PARTS):
                    step(dve.tensor_copy(gpart[:, i, :, :], rests[i][:, :, :]))
                    if i < PARTS - 1:
                        step(dve.tensor_tensor(rests[i + 1][:, :, :], rests[i][:, :, :], gpart[:, i, :, :], ALU.subtract))
                step(dve.tensor_tensor(lohot[:, :, :], iota_lo[:, :].unsqueeze(1).to_broadcast([P, TC, P]),
                                       lof[:, :].unsqueeze(2).to_broadcast([P, TC, P]), ALU.is_equal))
                filled = pay[:, :, 0, :]
                step(dve.tensor_tensor(filled, iota_hi[:, :].unsqueeze(1).to_broadcast([P, TC, ST]),
                                       hif[:, :].unsqueeze(2).to_broadcast([P, TC, ST]), ALU.is_equal))
                for s in range(TOP):
                    step(dve.tensor_tensor(pay[:, NT * s:NT * s + NT, 1, :], pay[:, NT * s:NT * s + NT, 0, :],
                                           iota_t[:, :].unsqueeze(2).to_broadcast([P, NT, ST]), ALU.mult))
                step(dve.tensor_scalar(pay[:, :, 2, :], filled, iota_p[:, 0:1], None, ALU.mult))
                for i in range(PARTS):
                    step(dve.tensor_tensor(pay[:, :, 3 + i, :], filled,
                                           gpart[:, i, :, :].rearrange("p s t -> p (s t)").unsqueeze(2).to_broadcast([P, TC, ST]),
                                           ALU.mult), RT_PAY if i == PARTS - 1 else None)
                dve.wait_ge(s_map, 1)
                step(dve.tensor_copy(slot[:, :, :], ps_t[:, 0:PAY * ST].rearrange("p (a h) -> p a h", a=PAY)), RT_SLOT)
                step(dve.scalar_tensor_tensor(stmp[0][:, :], slot[:, 1, :], float(P), slot[:, 2, :], ALU.mult, ALU.add))
                step(dve.tensor_scalar(stmp[2][:, :], slot[:, 0, :], -1.0, 1.0, ALU.mult, ALU.add))
                step(dve.tensor_tensor(stmp[1][:, :], stmp[2][:, :], spare[:, :], ALU.mult))
                step(dve.tensor_tensor(token[:, :], stmp[1][:, :], stmp[0][:, :], ALU.add))
                step(dve.tensor_tensor(sgate[:, :], slot[:, 3 + PARTS - 1, :], slot[:, 3 + PARTS - 2, :], ALU.add))
                step(dve.tensor_tensor(sgate[:, :], sgate[:, :], slot[:, 3, :], ALU.add), RT_STEPS)

            @block.vector
            def _(dve):
                def xb(b):
                    return x[:, bass.ds(QT * b, QT), :]

                def scales(p, n):
                    tiles = bass.ds(p * PAIR, PAIR)
                    layernorm_scales(dve, x[:, tiles, :], stats, mv, rs[:, tiles], shift[:, tiles], lntmp, s_ln, n,
                                     s_passed, PAIR)

                with dve.Fori(0, B // 2) as p:
                    scales(p, p)

                route(dve)

                def product(u, f, w):
                    dve.wait_ge(s_gate, u + 1)
                    dve.wait_ge(s_down, u - FB + 1)
                    dve.tensor_tensor(hid[:, f, 0:w], gatea[f % 2][:, 0:w], ps_b[f % 2][:, 0:w], ALU.mult)\
                        .then_inc(s_hid, 1)

                def gated(e):
                    dve.wait_ge(s_yeT, e + 1)
                    by_itself(dve, s_passed)
                    for i in range(ET):
                        ins = dve.tensor_tensor(ye[:, bass.ds((e * ET + i) * C, C)],
                                                ps_r[:, P * i:P * i + P],
                                                sgate[:, bass.ds(e * ET + i, 1)].to_broadcast([P, C]), ALU.mult)
                        if i == ET - 1:
                            ins.then_inc(s_ye, 1)

                def add_shared(c):
                    dve.wait_ge(s_sT, c + 1)
                    dve.tensor_tensor(xb(c), xb(c), ps_r2[:, :].rearrange("p (i c) -> p i c", i=QT), ALU.add)\
                        .then_inc(s_sum, 1)

                def rows_low(e, r):
                    dve.wait_ge(s_xe, e + 1)
                    by_itself(dve, s_passed)
                    dve.tensor_tensor(xe_lo[r][:, :], xeT[r][:, :], xe_hi[r][:, :].bitcast(F32), ALU.subtract)\
                        .then_inc(s_xlo, 1)

                def expert(e, r, first=False, last=False):
                    for f in range(FB):
                        product(U_EXP + e * FB + f, f, SLOTS)
                        if f == 0 and not last:
                            dve.wait_ge(s_whi, e + 3)
                            by_itself(dve, s_passed)
                            for i, raw in enumerate((w1[1 - r], w3[1 - r])):
                                ins = dve.tensor_tensor(we_lo[1 - r][i][:, :], raw[:, :], we_hi[1 - r][i][:, :].bitcast(F32),
                                                        ALU.subtract)
                            ins.then_inc(s_wlo, 1)
                        if f == 1 and not last:
                            rows_low(e + 1, 1 - r)
                        if f == 3 and not first:
                            gated(e - 1)

                rows_low(0, 0)
                expert(0, 0, first=True)
                with dve.Fori(0, (E - 1) // 2 - 1) as it:
                    expert(2 * it + 1, 1)
                    expert(2 * it + 2, 0)
                expert(E - 2, 1)
                expert(E - 1, 0, last=True)
                for f in range(FB):
                    product(U_END + f, f, T)
                gated(E - 1)
                for f in range(FB):
                    product(U_END + FB + f, f, T)
                add_shared(BEFORE)
                add_shared(B - 1)
                for half in range(2):
                    p = 2 * half
                    pair = x[:, p * PAIR:(p + 1) * PAIR, :]
                    dve.wait_ge(s_sum, B - BEFORE + half)
                    dve.wait_ge(s_acc[p], 16)
                    dve.tensor_tensor(pair, pair, routed(p), ALU.add).then_inc(s_sum, 1)
                    dve.wait_ge(s_sum, B - BEFORE + half + 1)
                    dve.wait_ge(s_psum, half + 1)
                    tiles = slice(half * NT // 2, (half + 1) * NT // 2)
                    layernorm_scales(dve, x[:, tiles, :], stats2, mv2, rs2[:, tiles], shift2[:, tiles], lntmp2, s_ln2,
                                     half, s_passed, NT // 2)
                dve.wait_ge(s_ln2, 2 * scale_steps(NT // 2))
                for k in range(NT - PAIR, NT):
                    dve.tensor_scalar(x[:, k, :], x[:, k, :], rs2[:, k:k + 1], shift2[:, k:k + 1], ALU.mult, ALU.add)\
                        .then_inc(s_passed, 1)


RT_HOT = 12
RT_DIFF = 13
RT_PAY = 54
RT_SLOT = 55
RT_STEPS = 61


FF = 512
FB = FF // P


class DenseWeights:

    SHAPES = {"w1": [P, FB, C], "w2": [P, FB, C], "h1": [P, FB, FF], "h2": [P, FB, FF], "w3": [P, 1, FF]}

    def __init__(self, nc, ctx, dram, tag="f1w_"):
        self.nc, self.dram = nc, dram
        self.raw = {w: ctx.enter_context(nc.sbuf_tensor(tag + w, shape, F32)) for w, shape in self.SHAPES.items()}
        self.scale = {w: ctx.enter_context(nc.sbuf_tensor(tag + w + "s", shape[:2], F32))
                      for w, shape in self.SHAPES.items()}
        self.sem = ctx.enter_context(nc.semaphore(tag + "loaded"))
        self.loads = 2 * len(self.SHAPES)

    def load(self, sp):
        for w in self.SHAPES:
            sp.dma_start(self.raw[w][:, :, :], self.dram[w + "_w"].rearrange("(o p) i -> p o i", p=P)).then_inc(self.sem, 16)
            with self.nc.allow_non_contiguous_dma(reason="a few hundred scales"):
                sp.dma_start(self.scale[w][:, :], self.dram[w + "_s"].rearrange("(o p) -> p o", p=P)).then_inc(self.sem, 16)


def dense_ffn(nc, x, ident, weights, out_rows, tag="f1"):
    with ExitStack() as ctx:
        def psum(name, shape, dt=F32):
            return ctx.enter_context(nc.psum_tensor(tag + name, shape, dt))

        def sbuf(name, shape, dt=F32):
            return ctx.enter_context(nc.sbuf_tensor(tag + name, shape, dt))

        def sem(name):
            return ctx.enter_context(nc.semaphore(tag + name))

        raw, sc, s_w = weights.raw, weights.scale, weights.sem
        shapes = {"w1": [P, 1, FF], "w2": [P, 1, FF], "h1": [P, FB, FF], "h2": [P, FB, FF], "w3": [P, FB, C]}
        w_hi = {w: sbuf(w + "_hi", shape, F32R) for w, shape in shapes.items()}
        w_lo = {w: sbuf(w + "_lo", shape, F32R) for w, shape in shapes.items()}
        half = sbuf("half", [P, FB])
        gated = sbuf("gated", [P, FB])
        xin = sbuf("xin", [P, QT, C])
        x_hi, x_lo = sbuf("x_hi", [C, T], F32R), sbuf("x_lo", [C, T], F32R)
        th = [sbuf(f"th{i}", [P, T]) for i in range(2)]
        u_sb = [sbuf(f"u{i}", [P, T]) for i in range(2)]
        gated_h = [sbuf(f"gated_h{i}", [P, T]) for i in range(2)]
        gelu_h = [sbuf(f"gelu_h{i}", [P, T]) for i in range(2)]
        hid_hi = [sbuf(f"hid_hi{i}", [P, FB, T], F32R) for i in range(3)]
        hid_lo = [sbuf(f"hid_lo{i}", [P, FB, T], F32R) for i in range(3)]
        yT = sbuf("yT", [C, T])
        res = sbuf("res", [P, QT, C])
        fin = [sbuf(f"fin{i}", [P, QT, C]) for i in range(2)]
        stats, mv = sbuf("stats", [P, QT, 6]), sbuf("mv", [P, QT, 2])
        lntmp, rs = sbuf("lntmp", [P, 4, QT]), sbuf("rs", [P, QT])
        ps_a = [psum(f"ps_a{i}", [P, T]) for i in range(2)]
        ps_b = [psum(f"ps_b{i}", [P, T]) for i in range(2)]
        ps_h = [psum(f"ps_h{i}", [P, T]) for i in range(2)]
        ps_y = psum("ps_y", [P, T])
        ps_t = psum("ps_t", [P, T])

        s_wt = sem("wt")
        s_wc = sem("wc")
        s_wl = sem("wl")
        s_xl = sem("xl")
        s_hi = sem("hi")
        s_lo = sem("lo")
        s_sc = sem("sc")
        s_xin = sem("xin")
        s_xt = sem("xt")
        s_xc = sem("xc")
        s_up = sem("up")
        s_th = sem("th")
        s_g = sem("g")
        s_h = sem("h")
        s_ge = sem("ge")
        s_y = sem("y")
        s_yc = sem("yc")
        s_t = sem("t")
        s_res = sem("res")
        s_ln = sem("ln")
        s_out = [sem(f"out{i}") for i in range(2)]
        s_passed = sem("passed")

        def gate_no(c, f):
            return f if isinstance(c, int) and c == 0 else FB + (c - 1) * 3 * FB + (FB + f if f < 2 else 2 * FB + f)

        def layer_no(c, n, f, last=False):
            return c * (3 * FB) + FB + f + (0 if n == 0 else FB if last else FB + 2)

        TURNS = [("w1", [(0, o) for o in range(FB)]), ("w2", [(0, o) for o in range(FB)])] + \
                [(w, [(k, o) for o in range(FB)]) for w in ("h1", "h2") for k in range(FB)] + \
                [("w3", [(k, 0) for k in range(FB)])]

        with nc.Block() as block:
            @block.sync
            def _(sp):
                def load(c):
                    if not (isinstance(c, int) and c == 0):
                        sp.wait_ge(s_xt, c)
                        by_itself(sp, s_passed)
                    sp.dma_start(xin[:, :, :], x[:, bass.ds(c * QT, QT), :]).then_inc(s_xin, 16)

                def store(c, r):
                    sp.wait_ge(s_ln, (c + 1) * LN_STEPS)
                    by_itself(sp, s_passed)
                    sp.dma_start(out_rows(c), fin[r][:, :, :]).then_inc(s_out[r], 16)

                load(0)
                load(1)
                with sp.Fori(0, B // 2 - 1) as it:
                    load(2 * it + 2)
                    store(2 * it, 0)
                    load(2 * it + 3)
                    store(2 * it + 1, 1)
                store(B - 2, 0)
                store(B - 1, 1)
                for r in range(2):
                    sp.wait_ge(s_out[r], B // 2 * 16)

            @block.scalar
            def _(act):
                for n, (w, blocks) in enumerate(TURNS):
                    act.wait_ge(s_wt, n + 1)
                    src = (ps_a + ps_b)[n % 4]
                    if w == "w3":
                        dst = w_hi[w][:, :, :].rearrange("p k c -> p (k c)")
                    else:
                        dst = w_hi[w][:, blocks[0][0], :]
                    act.activation(dst, src[:, :], ACT.Copy).then_inc(s_wc, 1)
                act.wait_ge(s_sc, 2)

                def turned(c):
                    act.wait_ge(s_xt, c + 1)
                    act.activation(x_hi[:, :], ps_t[:, :], ACT.Copy).then_inc(s_xc, 1)

                def gate(c, f):
                    u = c * FB + f
                    act.wait_ge(s_up, u + 1)
                    if not (isinstance(u, int) and u < 2):
                        act.wait_ge(s_g, 2 * (u - 1))
                    act.activation(th[f % 2][:, :], ps_a[f % 2][:, :], ACT.Tanh, scale=half[:, f:f + 1])\
                        .then_inc(s_th, 1)

                def gate_hi(c, f):
                    act.wait_ge(s_g, 2 * (c * FB + f + 1))
                    act.activation(hid_hi[0][:, f, :], gated_h[f % 2][:, :], ACT.Copy).then_inc(s_hi, 1)

                def layer(c, n, last):
                    w = ("h1", "h2")[n]
                    for f in range(FB):
                        act.wait_ge(s_h, (2 * c + n) * FB + f + 1)
                        if f >= 2:
                            act.wait_ge(s_lo, layer_no(c, n, f - 2, last) + 1)
                        act.activation(gelu_h[f % 2][:, :], ps_h[f % 2][:, :], ACT.Gelu, scale=sc[w][:, f:f + 1])\
                            .then_inc(s_ge, 1)
                        act.wait_ge(s_ge, (2 * c + n) * FB + f + 1)
                        act.activation(hid_hi[n + 1][:, f, :], gelu_h[f % 2][:, :], ACT.Copy).then_inc(s_hi, 1)
                        if n == 0 and f == 2 and not last:
                            turned(c + 1)

                def out(c):
                    act.wait_ge(s_y, c + 1)
                    act.activation(yT[:, :], ps_y[:, :], ACT.Copy, scale=sc["w3"][:, 0:1]).then_inc(s_yc, 1)

                def chunk(c, last=False):
                    layer(c, 0, last)
                    if not last:
                        for f in (0, 1):
                            gate(c + 1, f)
                        for f in (0, 1):
                            gate_hi(c + 1, f)
                    layer(c, 1, last)
                    if not last:
                        for f in (2, 3):
                            gate(c + 1, f)
                        for f in (2, 3):
                            gate_hi(c + 1, f)
                    out(c)

                turned(0)
                for f in range(FB):
                    gate(0, f)
                    gate_hi(0, f)
                with act.Fori(0, B - 1) as c:
                    chunk(c)
                chunk(B - 1, last=True)

            @block.gpsimd
            def _(pool):
                def low(no, dst, src, hi):
                    pool.wait_ge(s_hi, no + 1)
                    by_itself(pool, s_passed)
                    pool.tensor_tensor(dst, src[:, :], hi.bitcast(F32), ALU.subtract).then_inc(s_lo, 1)

                def gate_low(c, f):
                    low(gate_no(c, f), hid_lo[0][:, f, :], gated_h[f % 2], hid_hi[0][:, f, :])

                def chunk(c, last=False):
                    for n in range(2):
                        for f in range(FB):
                            low(layer_no(c, n, f, last), hid_lo[n + 1][:, f, :], gelu_h[f % 2], hid_hi[n + 1][:, f, :])
                        if not last:
                            gate_low(c + 1, 2 * n)
                            gate_low(c + 1, 2 * n + 1)

                for f in range(FB):
                    gate_low(0, f)
                with pool.Fori(0, B - 1) as c:
                    chunk(c)
                chunk(B - 1, last=True)

            @block.tensor
            def _(pe):
                for n, (w, blocks) in enumerate(TURNS):
                    if n == 0:
                        pe.wait_ge(s_w, weights.loads * 16)
                    if n >= 4:
                        pe.wait_ge(s_wc, n - 3)
                        pe.wait_ge(s_wl, n - 3)
                    for i, (k, o) in enumerate(blocks):
                        last = pe.transpose((ps_a + ps_b)[n % 4][:, P * i:P * i + P], raw[w][:, o, P * k:P * k + P],
                                            ident[:, :])
                    last.then_inc(s_wt, 1)
                pe.wait_ge(s_wc, len(TURNS))
                pe.wait_ge(s_wl, len(TURNS))

                def products(out, w, k, f, hi, lo, start, stop):
                    cols = slice(P * f, P * f + P)
                    pe.matmul(out, w_hi[w][:, k, cols], hi, start=start, stop=False)
                    pe.matmul(out, w_lo[w][:, k, cols], hi, start=False, stop=False)
                    return pe.matmul(out, w_hi[w][:, k, cols], lo, start=False, stop=stop)

                def turn(c):
                    pe.wait_ge(s_xin, (c + 1) * 16)
                    if not (isinstance(c, int) and c <= 1):
                        pe.wait_ge(s_res, c - 1)
                    for i in range(QT):
                        last = pe.transpose(ps_t[:, P * i:P * i + P], xin[:, i, :], ident[:, :])
                    last.then_inc(s_xt, 1)

                def up(c, f):
                    u = c * FB + f
                    if f == 0:
                        pe.wait_ge(s_xc, c + 1)
                        pe.wait_ge(s_xl, c + 1)
                    if not (isinstance(u, int) and u < 2):
                        pe.wait_ge(s_g, 2 * (u - 1))
                    products(ps_a[f % 2][:, :], "w1", 0, f, x_hi[:, :], x_lo[:, :], True, True)
                    products(ps_b[f % 2][:, :], "w2", 0, f, x_hi[:, :], x_lo[:, :], True, True).then_inc(s_up, 1)

                def layer(c, n, last):
                    for f in range(FB):
                        if n or f >= 2:
                            pe.wait_ge(s_ge, (2 * c + n) * FB + f - 1)
                        for k in range(FB):
                            if f == 0:
                                pe.wait_ge(s_lo, (gate_no(c, k) if n == 0 else layer_no(c, 0, k)) + 1)
                            ins = products(ps_h[f % 2][:, :], ("h1", "h2")[n], k, f, hid_hi[n][:, k, :],
                                           hid_lo[n][:, k, :], k == 0, k == FB - 1)
                        ins.then_inc(s_h, 1)
                        if n == 0 and f == 0 and not (isinstance(c, int) and c == 0):
                            back(c - 1)
                        if n == 0 and f == 2 and not last:
                            turn(c + 1)

                def out(c, last):
                    if not (isinstance(c, int) and c == 0):
                        pe.wait_ge(s_yc, c)
                    for k in range(FB):
                        pe.wait_ge(s_lo, layer_no(c, 1, k, last) + 1)
                        ins = products(ps_y[:, :], "w3", k, 0, hid_hi[2][:, k, :], hid_lo[2][:, k, :], k == 0,
                                       k == FB - 1)
                    ins.then_inc(s_y, 1)

                def back(c):
                    pe.wait_ge(s_yc, c + 1)
                    if not (isinstance(c, int) and c == 0):
                        pe.wait_ge(s_res, c)
                    for i in range(QT):
                        last = pe.transpose(ps_t[:, P * i:P * i + P], yT[:, P * i:P * i + P], ident[:, :])
                    last.then_inc(s_t, 1)

                def chunk(c, first=False, last=False):
                    layer(c, 0, last)
                    if not last:
                        up(c + 1, 0)
                        up(c + 1, 1)
                    layer(c, 1, last)
                    if not last:
                        up(c + 1, 2)
                        up(c + 1, 3)
                    out(c, last)

                turn(0)
                for f in range(FB):
                    up(0, f)
                chunk(0)
                with pe.Fori(1, B - 1) as c:
                    chunk(c)
                chunk(B - 1, last=True)
                back(B - 1)

            @block.vector
            def _(dve):
                dve.wait_ge(s_w, weights.loads * 16)
                dve.tensor_scalar(half[:, :], sc["w1"][:, :], 0.5, None, ALU.mult).then_inc(s_sc, 1)
                dve.wait_ge(s_sc, 1)
                dve.tensor_tensor(gated[:, :], half[:, :], sc["w2"][:, :], ALU.mult).then_inc(s_sc, 1)
                dve.wait_ge(s_sc, 2)
                for n, (w, blocks) in enumerate(TURNS):
                    dve.wait_ge(s_wc, n + 1)
                    if w == "w3":
                        hi, lo = (part[w][:, :, :].rearrange("p k c -> p (k c)") for part in (w_hi, w_lo))
                    else:
                        hi, lo = (part[w][:, blocks[0][0], :] for part in (w_hi, w_lo))
                    dve.tensor_tensor(lo, (ps_a + ps_b)[n % 4][:, :], hi.bitcast(F32), ALU.subtract).then_inc(s_wl, 1)

                def x_low(c):
                    dve.wait_ge(s_xc, c + 1)
                    dve.tensor_tensor(x_lo[:, :], ps_t[:, :], x_hi[:, :].bitcast(F32), ALU.subtract).then_inc(s_xl, 1)

                def gate(c, f):
                    u = c * FB + f
                    dve.wait_ge(s_th, u + 1)
                    dve.scalar_tensor_tensor(u_sb[f % 2][:, :], th[f % 2][:, :], 1.0, ps_a[f % 2][:, :], ALU.add, ALU.mult)\
                        .then_inc(s_g, 1)
                    if f >= 2 or not (isinstance(c, int) and c == 0):
                        dve.wait_ge(s_lo, (gate_no(c, f - 2) if f >= 2 else gate_no(c - 1, f + 2)) + 1)
                    dve.wait_ge(s_g, 2 * u + 1)
                    dve.scalar_tensor_tensor(gated_h[f % 2][:, :], ps_b[f % 2][:, :], gated[:, f:f + 1],
                                             u_sb[f % 2][:, :], ALU.mult, ALU.mult).then_inc(s_g, 1)

                def residual(c):
                    dve.wait_ge(s_t, c + 1)
                    if not (isinstance(c, int) and c == 0):
                        by_itself(dve, s_passed)
                        dve.wait_ge(s_ln, c * LN_STEPS)
                    dve.tensor_tensor(res[:, :, :], x[:, bass.ds(c * QT, QT), :],
                                      ps_t[:, :].rearrange("p (i c) -> p i c", i=QT), ALU.add).then_inc(s_res, 1)

                def normed(c, r, before):
                    dve.wait_ge(s_res, c + 1)
                    if not (isinstance(before, int) and before == 0):
                        dve.wait_ge(s_out[r], before * 16)
                    layernorm(dve, fin[r][:, :, :], res[:, :, :], stats, mv, rs, lntmp, s_ln, c, s_passed)

                def chunk(c, r, before, last=False):
                    if not (isinstance(c, int) and c == 0):
                        residual(c - 1)
                    if not last:
                        x_low(c + 1)
                        gate(c + 1, 0)
                        gate(c + 1, 1)
                    if not (isinstance(c, int) and c == 0):
                        normed(c - 1, r, before)
                    if not last:
                        gate(c + 1, 2)
                        gate(c + 1, 3)

                x_low(0)
                for f in range(FB):
                    gate(0, f)
                chunk(0, None, None)
                chunk(1, 0, 0)
                chunk(2, 1, 0)
                with dve.Fori(1, B // 2 - 1) as it:
                    chunk(2 * it + 1, 0, it)
                    chunk(2 * it + 2, 1, it)
                chunk(B - 1, 0, B // 2 - 1, last=True)
                residual(B - 1)
                normed(B - 1, 1, B // 2 - 1)


def prologue(nc, ident, identb, mask, wqkv, heads0, wq1, heads1, wproj, wproj_dram, cos, sin, angles):
    with ExitStack() as ctx:
        def sbuf(name, shape, dt=F32):
            return ctx.enter_context(nc.sbuf_tensor("pre_" + name, shape, dt))

        def sem(name):
            return ctx.enter_context(nc.semaphore("pre_" + name))

        w0 = sbuf("w0", [C, 3 * C])
        w1 = [sbuf("w1" + n, [C, C]) for n in "qkv"]
        ps_w = [ctx.enter_context(nc.psum_tensor(f"pre_ps{i}", [P, C], F32)) for i in range(3)]
        s_w = sem("w")
        s_x = sem("x")
        s_const = sem("const")
        s_turn = sem("turn")
        s_done = sem("done")

        with nc.Block() as block:
            @block.sync
            def _(sp):
                sp.dma_start(w0[:, :], wqkv).then_inc(s_w, 16)
                for dst, src in zip(w1, wq1):
                    sp.dma_start(dst[:, :], src).then_inc(s_w, 16)
                sp.dma_start(wproj[:, :], wproj_dram).then_inc(s_w, 16)
                sp.wait_ge(s_w, 5 * 16)

            @block.scalar
            def _(act):
                for table, angle in ((cos, angles[0]), (sin, angles[1])):
                    act.dma_start(table[:, :], angle.unsqueeze(1).to_broadcast([D, H, T])).then_inc(s_x, 16)
                act.wait_ge(s_x, 2 * 16)

            @block.gpsimd
            def _(pool):
                for m in (ident, identb, mask):
                    pool.memset(m[:, :], 0.0).then_inc(s_const, 1)
                pool.wait_ge(s_const, 3)
                for m in (ident, identb):
                    pool.affine_select(out=m[:, :], in_=m[:, :], compare_op=ALU.not_equal, fill=1.0, base=0,
                                       pattern=[[-1, P]], channel_multiplier=1).then_inc(s_const, 1)
                pool.affine_select(out=mask[:, :], in_=mask[:, :], compare_op=ALU.is_ge, fill=-1e30, base=0,
                                   pattern=[[-1, P]], channel_multiplier=1).then_inc(s_const, 1)
                pool.wait_ge(s_const, 6)

            @block.tensor
            def _(pe):
                pe.wait_ge(s_w, 5 * 16)
                pe.wait_ge(s_const, 6)
                for i in range(3):
                    pe.transpose(ps_w[i][:, :], w1[i][:, :], ident[:, :]).then_inc(s_turn, 1)

            @block.vector
            def _(dve):
                def columns(out, name, src):
                    hd = src.rearrange("c (h d) -> c h d", h=H)
                    dve.tensor_copy(out[name][:, :].rearrange("c (d h) -> c h d", h=H), hd).then_inc(s_done, 1)

                dve.wait_ge(s_w, 5 * 16)
                columns(heads0, "q", w0[:, 0:C])
                columns(heads0, "k", w0[:, C:2 * C])
                dve.tensor_copy(heads0["v"][:, :], w0[:, 2 * C:3 * C]).then_inc(s_done, 1)
                dve.wait_ge(s_turn, 3)
                columns(heads1, "q", ps_w[0][:, :])
                columns(heads1, "k", ps_w[1][:, :])
                dve.tensor_copy(heads1["v"][:, :], ps_w[2][:, :]).then_inc(s_done, 1)
                dve.wait_ge(s_done, 6)


class BatchRows:

    def __init__(self, array):
        self.array = array.rearrange("(b i p) c -> b p i c", p=P, i=QT)

    def __getitem__(self, b):
        if isinstance(b, int):
            return self.array[b]
        return self.array[bass.ds(b, 1)].rearrange("b p i c -> p (b i) c")


def transformer(nc, ins, angles, normed, acc, out):
    with ExitStack() as ctx:
        def sbuf(name, shape, dt=F32):
            return ctx.enter_context(nc.sbuf_tensor(name, shape, dt))

        x = sbuf("x_tiles", [P, NT, C])
        ident, identb = sbuf("ident", [P, P]), sbuf("identb", [P, P], BF16)
        mask = sbuf("mask", [P, P], BF16)
        wproj = sbuf("wproj", [C, C])
        cos, sin = sbuf("cos_table", [C, T]), sbuf("sin_table", [C, T])
        heads0, heads1 = [{n: sbuf(f"heads{i}_{n}", [C, C]) for n in ("k", "q", "v")} for i in range(2)]
        x_in = ins["L0_attn_x"].rearrange("b t c -> (b t) c")
        out_rows = out.rearrange("b t c -> (b t) c")

        prologue(nc, ident, identb, mask, ins["L0_attn_Wqkv"], heads0,
                 [ins["L1_attn_W" + n] for n in "qkv"], heads1, wproj, ins["L0_attn_Wproj"], cos, sin, angles)
        attention(nc, x, BatchRows(x_in), ident, identb, mask, heads0, wproj, cos, sin, True, "a0_")
        dram = {n: ins["L0_ffn_" + n] for n in ("ln_g", "ln_b", "Wr", "W1", "W3", "W2", "W1s", "W3s", "W2s")}
        moe_ffn(nc, x, ident, identb, dict(dram, acc=acc, normed=normed, normed_rows=BatchRows(normed[0:TOKENS, :]).__getitem__),
                "f0_")
        weights = DenseWeights(nc, ctx, {n + s: ins["L1_ffn_" + n + s] for n in DenseWeights.SHAPES for s in ("_w", "_s")})
        attention(nc, x, None, ident, identb, mask, heads1, None, cos, sin, False, "a1_", ahead=weights.load)
        dense_ffn(nc, x, ident, weights,
                  BatchRows(out_rows).__getitem__, "f1_")


_INS = ['L0_attn_x', 'L0_attn_Wqkv', 'L0_attn_Wproj', 'L0_ffn_ln_g', 'L0_ffn_ln_b', 'L0_ffn_Wr', 'L0_ffn_W1',
        'L0_ffn_W3', 'L0_ffn_W2', 'L0_ffn_W1s', 'L0_ffn_W3s', 'L0_ffn_W2s', 'L1_attn_Wq', 'L1_attn_Wk', 'L1_attn_Wv',
        'L1_ffn_w1_w', 'L1_ffn_w1_s', 'L1_ffn_w2_w', 'L1_ffn_w2_s', 'L1_ffn_h1_w', 'L1_ffn_h1_s', 'L1_ffn_h2_w',
        'L1_ffn_h2_s', 'L1_ffn_w3_w', 'L1_ffn_w3_s']


def kernel(**inputs):
    import numpy as _np
    import concourse.bacc as _bacc
    from concourse import mybir as _mybir
    from concourse.bass_utils import run_bass_kernel_spmd as _run

    nc = _bacc.Bacc("TRN2", target_bir_lowering=False, num_devices=1)
    arrays, ins = {}, {}

    def put(name, a):
        arrays[f"in_{name}_dram"] = a
        return nc.dram_tensor(f"in_{name}_dram", a.shape, _mybir.dt.from_np(a.dtype), kind="ExternalInput").ap()

    for name in _INS:
        ins[name] = put(name, _np.ascontiguousarray(inputs[name]))
    inv = (1.0 / 10000.0 ** (_np.arange(0, D, 2, dtype=_np.float32) / D)).astype(_np.float32)
    angle = (_np.arange(T, dtype=_np.float32)[:, None] * inv[None, :]).astype(_np.float32)
    angles = [put(name, _np.ascontiguousarray(_np.stack(pair, axis=-1).reshape(T, D).T.astype(_np.float32)))
              for name, pair in (("cos", (_np.cos(angle),) * 2), ("sin", (-_np.sin(angle), _np.sin(angle))))]
    out = nc.dram_tensor("out_0_dram", (B, T, C), F32, kind="ExternalOutput").ap()
    normed = nc.dram_tensor("normed_rows_dram", (ROWS_ALL, C), F32, kind="Internal").ap()
    acc = nc.dram_tensor("expert_sums_dram", (ROWS_ALL, C), F32, kind="Internal").ap()
    transformer(nc, ins, angles, normed, acc, out)
    r = _run(nc, [arrays], core_ids=[0])
    return r.results[0]["out_0_dram"]
```
